# Optimizing a Trainium2 kernel written in Bass

```python
import numpy as np
import jax
import jax.numpy as jnp

def _softmax(x, axis=-1):
    return jax.nn.softmax(x, axis=axis)

def _gelu(x):
    return jax.nn.gelu(x, approximate=True)

def _silu(x):
    return jax.nn.silu(x)

def _sigmoid(x):
    return jax.nn.sigmoid(x)

def _layernorm(x, axis=-1, eps=1e-05):
    m = jnp.mean(x, axis=axis, keepdims=True)
    v = jnp.var(x, axis=axis, keepdims=True)
    return (x - m) / jnp.sqrt(v + eps)

def _scatter_add(tgt, idx, src, axis=0):
    return tgt.at[idx].add(src)

def _segment_sum(src, seg, n):
    return jax.ops.segment_sum(src, seg, n)
kernel_name = 'mk_decoder_postln_d1_seqx_r8_44c269'

def setup_inputs(seed: int=0):
    np.random.seed(seed)
    _w = jnp.asarray

    def _rec_inputs():
        import jax
        import jax.numpy as jnp
        _rk = jax.random.key(seed)
        x = 7.22e-05 + 1 * jax.random.normal(jax.random.fold_in(_rk, 1), (32, 64, 256), jnp.float32)
        _lenS = 64 - jax.random.randint(jax.random.fold_in(_rk, 7), (32,), 0, max(1, 64 // 4) + 1, jnp.int32)
        _lenS2 = 64 - jax.random.randint(jax.random.fold_in(_rk, 8), (32,), 0, max(1, 64 // 4) + 1, jnp.int32)
        _ctx_512P = jax.random.normal(jax.random.fold_in(_rk, 11), (32, 16, 64), jnp.float32)
        _ctx_512c = jax.random.dirichlet(jax.random.fold_in(_rk, 511), 0.3 * jnp.ones((16,), jnp.float32), (32, 64))
        _ctx_512t = jnp.einsum('bsk,bkd->bsd', _ctx_512c, _ctx_512P)
        _ctx_512t = _ctx_512t * jax.lax.rsqrt(jnp.mean(jnp.square(_ctx_512t)) + 1e-12) * 0.953939
        ctx_512 = -0.000514642 + 1.00011 * (_ctx_512t + 0.3 * jax.random.normal(jax.random.fold_in(_rk, 611), (32, 64, 64), jnp.float32))
        return (x, ctx_512)
    x, ctx_512 = _rec_inputs()

    def _L0_attn_setup():
        import jax, jax.numpy as jnp
        import numpy as np
        H, DK, DV, HID, KSZ, CHUNK = (6, 32, 64, 256, 4, 64)
        EPS = 1e-05

        def _short_conv(x, w):
            C, K = (w.shape[0], w.shape[2])
            y = jax.lax.conv_general_dilated(x.transpose(0, 2, 1), w, window_strides=(1,), padding=[(K - 1, 0)], feature_group_count=C, dimension_numbers=('NCH', 'OIH', 'NCH'))
            return jax.nn.silu(y.transpose(0, 2, 1))

        def _l2norm(x, eps=1e-06):
            return x * jax.lax.rsqrt(jnp.sum(x * x, axis=-1, keepdims=True) + eps)
        key = jax.random.key(seed)
        ks = jax.random.split(key, 16)
        B, T = (2, 256)

        def w(k, shape):
            s = 1.0 / np.sqrt(shape[-1] if len(shape) == 2 else shape[-1] * shape[-2] + 1e-09)
            if len(shape) == 3:
                s = 1.0 / np.sqrt(shape[2])
            return jax.random.uniform(k, shape, jnp.float32, -s, s)
        dt = jnp.exp(jax.random.uniform(ks[7], (H,), jnp.float32) * (np.log(0.1) - np.log(0.001)) + np.log(0.001))
        dt = jnp.clip(dt, 0.0001)
        return {'x': jax.random.normal(ks[0], (B, T, HID), jnp.float32), 'Wq': w(ks[1], (H * DK, HID)), 'Wk': w(ks[2], (H * DK, HID)), 'Wv': w(ks[3], (H * DV, HID)), 'Wa': w(ks[4], (H, HID)), 'Wb': w(ks[5], (H, HID)), 'A_log': jnp.log(jax.random.uniform(ks[6], (H,), jnp.float32, 1.0, 16.0)), 'dt_bias': dt + jnp.log(-jnp.expm1(-dt)), 'conv_q_w': w(ks[8], (H * DK, 1, KSZ)), 'conv_k_w': w(ks[9], (H * DK, 1, KSZ)), 'conv_v_w': w(ks[10], (H * DV, 1, KSZ)), 'Wg': w(ks[11], (H * DV, HID)), 'norm_w': jnp.ones((DV,), jnp.float32), 'Wo': w(ks[12], (HID, H * DV))}
    _L0_attn_all = _L0_attn_setup()
    _L0_attn_in = {k: v for k, v in _L0_attn_all.items() if k in ('Wq', 'Wk', 'Wv', 'Wa', 'Wb', 'A_log', 'dt_bias', 'conv_q_w', 'conv_k_w', 'conv_v_w', 'Wg', 'norm_w', 'Wo')}
    del _L0_attn_all

    def _L0_xattn_setup():
        import jax, jax.numpy as jnp
        import numpy as np
        N_HEADS = 16
        N_KV_HEADS = 4
        ROPE_THETA = 10000.0
        EPS = 1e-05

        def _rms_norm(x, w):
            var = jnp.mean(x * x, axis=-1, keepdims=True)
            return x * jax.lax.rsqrt(var + EPS) * w

        def _rope_sin_cos(T, head_dim, dtype):
            inv_freq = 1.0 / ROPE_THETA ** (jnp.arange(0, head_dim, 2, dtype=jnp.float32) / head_dim)
            t = jnp.arange(T, dtype=jnp.float32)
            freqs = jnp.outer(t, inv_freq)
            emb = jnp.concatenate([freqs, freqs], -1)
            return (jnp.sin(emb).astype(dtype)[None, None], jnp.cos(emb).astype(dtype)[None, None])

        def _rotate_half(x):
            h = x.shape[-1] // 2
            x1, x2 = (x[..., :h], x[..., h:])
            return jnp.concatenate([-x2, x1], axis=-1)
        key = jax.random.key(seed)
        ks = jax.random.split(key, 6)
        B, T, C = (2, 256, 256)
        Ckv = C // N_HEADS * N_KV_HEADS
        return {'q': jax.random.normal(ks[0], (B, T, C), jnp.float32), 'k': jax.random.normal(ks[1], (B, T, Ckv), jnp.float32), 'v': jax.random.normal(ks[2], (B, T, Ckv), jnp.float32), 'q_norm_w': jnp.ones((C,), jnp.float32), 'k_norm_w': jnp.ones((Ckv,), jnp.float32), 'w_out': jax.random.normal(ks[3], (C, C), jnp.float32) * C ** (-0.5)}
    _L0_xattn_all = _L0_xattn_setup()
    _L0_xattn_in = {k: v for k, v in _L0_xattn_all.items() if k in ('q_norm_w', 'k_norm_w', 'w_out')}
    del _L0_xattn_all

    def _L0_ffn_setup():
        import jax, jax.numpy as jnp
        import numpy as np
        B, S, D, F, E, SH, K = (2, 256, 256, 128, 16, 2, 2)

        def _experts_all(x, g, gb, w1, b1, w2, b2):
            y = jax.nn.gelu(jnp.einsum('bsd,edf->bsef', x, g) + gb, approximate=False)
            y = y * (jnp.einsum('bsd,edf->bsef', x, w1) + b1)
            return jnp.einsum('bsef,efd->bsed', y, w2) + b2
        key = jax.random.key(seed)
        ks = jax.random.split(key, 8)
        std = 0.02
        mk = lambda k, sh: jax.random.normal(k, sh, jnp.float32) * std
        return {'x': jax.random.normal(ks[0], (B, S, D), jnp.float32), 'wa': mk(ks[1], (D, E)), 'rg': mk(ks[2], (E, D, F)), 'rgb': jnp.zeros((E, F), jnp.float32), 'rw1': mk(ks[3], (E, D, F)), 'rb1': jnp.zeros((E, F), jnp.float32), 'rw2': mk(ks[4], (E, F, D)), 'rb2': jnp.zeros((E, D), jnp.float32), 'sg': mk(ks[5], (SH, D, F)), 'sgb': jnp.zeros((SH, F), jnp.float32), 'sw1': mk(ks[6], (SH, D, F)), 'sb1': jnp.zeros((SH, F), jnp.float32), 'sw2': mk(ks[7], (SH, F, D)), 'sb2': jnp.zeros((SH, D), jnp.float32)}
    _L0_ffn_all = _L0_ffn_setup()
    _L0_ffn_in = {k: v for k, v in _L0_ffn_all.items() if k in ('wa', 'rg', 'rgb', 'rw1', 'rb1', 'rw2', 'rb2', 'sg', 'sgb', 'sw1', 'sb1', 'sw2', 'sb2')}
    del _L0_ffn_all
    return {'x': x, 'ctx_512': ctx_512, 'L0_attn_Wq': _L0_attn_in['Wq'], 'L0_attn_Wk': _L0_attn_in['Wk'], 'L0_attn_Wv': _L0_attn_in['Wv'], 'L0_attn_Wa': _L0_attn_in['Wa'], 'L0_attn_Wb': _L0_attn_in['Wb'], 'L0_attn_A_log': _L0_attn_in['A_log'], 'L0_attn_dt_bias': _L0_attn_in['dt_bias'], 'L0_attn_conv_q_w': _L0_attn_in['conv_q_w'], 'L0_attn_conv_k_w': _L0_attn_in['conv_k_w'], 'L0_attn_conv_v_w': _L0_attn_in['conv_v_w'], 'L0_attn_Wg': _L0_attn_in['Wg'], 'L0_attn_norm_w': _L0_attn_in['norm_w'], 'L0_attn_Wo': _L0_attn_in['Wo'], 'L0_xattn_q_norm_w': _L0_xattn_in['q_norm_w'], 'L0_xattn_k_norm_w': _L0_xattn_in['k_norm_w'], 'L0_xattn_w_out': _L0_xattn_in['w_out'], 'L0_ffn_wa': _L0_ffn_in['wa'], 'L0_ffn_rg': _L0_ffn_in['rg'], 'L0_ffn_rgb': _L0_ffn_in['rgb'], 'L0_ffn_rw1': _L0_ffn_in['rw1'], 'L0_ffn_rb1': _L0_ffn_in['rb1'], 'L0_ffn_rw2': _L0_ffn_in['rw2'], 'L0_ffn_rb2': _L0_ffn_in['rb2'], 'L0_ffn_sg': _L0_ffn_in['sg'], 'L0_ffn_sgb': _L0_ffn_in['sgb'], 'L0_ffn_sw1': _L0_ffn_in['sw1'], 'L0_ffn_sb1': _L0_ffn_in['sb1'], 'L0_ffn_sw2': _L0_ffn_in['sw2'], 'L0_ffn_sb2': _L0_ffn_in['sb2']}

def reference(x, ctx_512, L0_attn_Wq, L0_attn_Wk, L0_attn_Wv, L0_attn_Wa, L0_attn_Wb, L0_attn_A_log, L0_attn_dt_bias, L0_attn_conv_q_w, L0_attn_conv_k_w, L0_attn_conv_v_w, L0_attn_Wg, L0_attn_norm_w, L0_attn_Wo, L0_xattn_q_norm_w, L0_xattn_k_norm_w, L0_xattn_w_out, L0_ffn_wa, L0_ffn_rg, L0_ffn_rgb, L0_ffn_rw1, L0_ffn_rb1, L0_ffn_rw2, L0_ffn_rb2, L0_ffn_sg, L0_ffn_sgb, L0_ffn_sw1, L0_ffn_sb1, L0_ffn_sw2, L0_ffn_sb2):
    import jax
    import jax.numpy as jnp

    def _L0_attn_ref(x, Wq, Wk, Wv, Wa, Wb, A_log, dt_bias, conv_q_w, conv_k_w, conv_v_w, Wg, norm_w, Wo):
        import jax, jax.numpy as jnp
        import numpy as np
        H, DK, DV, HID, KSZ, CHUNK = (6, 32, 64, 256, 4, 64)
        EPS = 1e-05

        def _short_conv(x, w):
            C, K = (w.shape[0], w.shape[2])
            y = jax.lax.conv_general_dilated(x.transpose(0, 2, 1), w, window_strides=(1,), padding=[(K - 1, 0)], feature_group_count=C, dimension_numbers=('NCH', 'OIH', 'NCH'))
            return jax.nn.silu(y.transpose(0, 2, 1))

        def _l2norm(x, eps=1e-06):
            return x * jax.lax.rsqrt(jnp.sum(x * x, axis=-1, keepdims=True) + eps)
        B, T, _ = x.shape
        q = _short_conv(x @ Wq.T, conv_q_w).reshape(B, T, H, DK)
        k = _short_conv(x @ Wk.T, conv_k_w).reshape(B, T, H, DK)
        v = _short_conv(x @ Wv.T, conv_v_w).reshape(B, T, H, DV)
        q = _l2norm(q) * DK ** (-0.5)
        k = _l2norm(k)
        g = -jnp.exp(A_log) * jax.nn.softplus(x @ Wa.T + dt_bias)
        beta = jax.nn.sigmoid(x @ Wb.T)

        def tm(a):
            a = jnp.moveaxis(a, 1, 0)
            return a.reshape((T // CHUNK, CHUNK) + a.shape[1:])
        qc, kc, vc, gc, bc = map(tm, (q, k, v, g, beta))

        def step(S, inp):
            q_t, k_t, v_t, g_t, b_t = inp
            S = S * jnp.exp(g_t)[..., None, None]
            delta = (v_t - jnp.einsum('bhk,bhkv->bhv', k_t, S)) * b_t[..., None]
            S = S + k_t[..., None] * delta[:, :, None, :]
            return (S, jnp.einsum('bhk,bhkv->bhv', q_t, S))

        @jax.checkpoint
        def chunk(S, inp):
            return jax.lax.scan(step, S, inp)
        S0 = jnp.zeros((B, H, DK, DV), x.dtype)
        _, o = jax.lax.scan(chunk, S0, (qc, kc, vc, gc, bc))
        o = jnp.moveaxis(o.reshape(T, B, H, DV), 0, 1)
        gate = (x @ Wg.T).reshape(B, T, H, DV)
        og = o * jax.nn.silu(gate)
        og = og * jax.lax.rsqrt(jnp.mean(og * og, axis=-1, keepdims=True) + EPS) * norm_w
        return og.reshape(B, T, H * DV) @ Wo.T

    def _L0_xattn_ref(q, k, v, q_norm_w, k_norm_w, w_out):
        import jax, jax.numpy as jnp
        import numpy as np
        N_HEADS = 16
        N_KV_HEADS = 4
        ROPE_THETA = 10000.0
        EPS = 1e-05

        def _rms_norm(x, w):
            var = jnp.mean(x * x, axis=-1, keepdims=True)
            return x * jax.lax.rsqrt(var + EPS) * w

        def _rope_sin_cos(T, head_dim, dtype):
            inv_freq = 1.0 / ROPE_THETA ** (jnp.arange(0, head_dim, 2, dtype=jnp.float32) / head_dim)
            t = jnp.arange(T, dtype=jnp.float32)
            freqs = jnp.outer(t, inv_freq)
            emb = jnp.concatenate([freqs, freqs], -1)
            return (jnp.sin(emb).astype(dtype)[None, None], jnp.cos(emb).astype(dtype)[None, None])

        def _rotate_half(x):
            h = x.shape[-1] // 2
            x1, x2 = (x[..., :h], x[..., h:])
            return jnp.concatenate([-x2, x1], axis=-1)
        B, T, C = q.shape
        hd = C // N_HEADS
        g = N_HEADS // N_KV_HEADS
        q = _rms_norm(q, q_norm_w)
        k = _rms_norm(k, k_norm_w)
        q = q.reshape(B, T, N_HEADS, hd).transpose(0, 2, 1, 3)
        k = k.reshape(B, T, N_KV_HEADS, hd).transpose(0, 2, 1, 3)
        v = v.reshape(B, T, N_KV_HEADS, hd).transpose(0, 2, 1, 3)
        sin, cos = _rope_sin_cos(T, hd, q.dtype)
        q = q * cos + _rotate_half(q) * sin
        k = k * cos + _rotate_half(k) * sin
        qg = q.reshape(B, N_KV_HEADS, g, T, hd)
        scale = 1.0 / jnp.sqrt(jnp.asarray(hd, q.dtype))
        scores = jnp.einsum('bgnqd,bgkd->bgnqk', qg, k) * scale
        causal = jnp.tril(jnp.ones((T, T), bool))
        scores = jnp.where(causal, scores, jnp.asarray(-1e+30, scores.dtype))
        attn = jax.nn.softmax(scores, axis=-1)
        out = jnp.einsum('bgnqk,bgkd->bgnqd', attn, v)
        out = out.reshape(B, N_HEADS, T, hd).transpose(0, 2, 1, 3).reshape(B, T, C)
        return out @ w_out.T

    def _L0_ffn_ref(x, wa, rg, rgb, rw1, rb1, rw2, rb2, sg, sgb, sw1, sb1, sw2, sb2):
        import jax, jax.numpy as jnp
        import numpy as np
        B, S, D, F, E, SH, K = (2, 256, 256, 128, 16, 2, 2)

        def _experts_all(x, g, gb, w1, b1, w2, b2):
            y = jax.nn.gelu(jnp.einsum('bsd,edf->bsef', x, g) + gb, approximate=False)
            y = y * (jnp.einsum('bsd,edf->bsef', x, w1) + b1)
            return jnp.einsum('bsef,efd->bsed', y, w2) + b2
        aff = jax.nn.sigmoid(jnp.einsum('bsd,de->bse', x, wa))
        topk_p, topk_i = jax.lax.top_k(aff, K)
        topk_p = topk_p / jnp.sum(topk_p, axis=-1, keepdims=True)
        combine = jnp.sum(jax.nn.one_hot(topk_i, E, dtype=x.dtype) * topk_p[..., None], axis=2)
        routed = jnp.einsum('bsed,bse->bsd', _experts_all(x, rg, rgb, rw1, rb1, rw2, rb2), combine)
        shared = jnp.sum(_experts_all(x, sg, sgb, sw1, sb1, sw2, sb2), axis=2)
        return x + shared + routed
    x = _layernorm(x + _L0_attn_ref(x, L0_attn_Wq, L0_attn_Wk, L0_attn_Wv, L0_attn_Wa, L0_attn_Wb, L0_attn_A_log, L0_attn_dt_bias, L0_attn_conv_q_w, L0_attn_conv_k_w, L0_attn_conv_v_w, L0_attn_Wg, L0_attn_norm_w, L0_attn_Wo), axis=-1)
    x = _layernorm(x + _L0_xattn_ref(x, ctx_512, ctx_512, L0_xattn_q_norm_w, L0_xattn_k_norm_w, L0_xattn_w_out), axis=-1)
    x = _layernorm(x + _L0_ffn_ref(x, L0_ffn_wa, L0_ffn_rg, L0_ffn_rgb, L0_ffn_rw1, L0_ffn_rb1, L0_ffn_rw2, L0_ffn_rb2, L0_ffn_sg, L0_ffn_sgb, L0_ffn_sw1, L0_ffn_sb1, L0_ffn_sw2, L0_ffn_sb2), axis=-1)
    return x

_drawn_inputs = setup_inputs


def setup_inputs(seed=0):
    import zlib

    import numpy as np

    out = dict(_drawn_inputs(seed))
    spreads = {'L0_attn_norm_w': (1.0, 0.2),
     'L0_xattn_q_norm_w': (1.0, 0.2),
     'L0_xattn_k_norm_w': (1.0, 0.2),
     'L0_ffn_rgb': (0.0, 0.8),
     'L0_ffn_rb1': (0.0, 0.8),
     'L0_ffn_rb2': (0.0, 0.8),
     'L0_ffn_sgb': (0.0, 0.8),
     'L0_ffn_sb1': (0.0, 0.8),
     'L0_ffn_sb2': (0.0, 0.488)}
    factors = {'L0_ffn_rg': 8.0,
     'L0_ffn_rw1': 8.0,
     'L0_ffn_rw2': 8.0,
     'L0_ffn_sg': 6.234,
     'L0_ffn_sw1': 6.048,
     'L0_ffn_sw2': 5.777}
    for name, (base, spread) in spreads.items():
        noise = np.random.default_rng([zlib.crc32(name.encode()), seed]).standard_normal(out[name].shape)
        drawn = base * np.exp(spread * noise) if base else spread * noise
        out[name] = jnp.asarray(drawn.astype(out[name].dtype))
    for name, factor in factors.items():
        out[name] = (out[name] * factor).astype(out[name].dtype)
    return out
```

```python
from contextlib import ExitStack

import numpy as np

import concourse.bass as bass
from concourse import mybir

F32 = mybir.dt.float32
BF16 = mybir.dt.bfloat16
U32 = mybir.dt.uint32
ALU = mybir.AluOpType
ACT = mybir.ActivationFunctionType
AXX = mybir.AxisListType.X

B, T, D = 32, 64, 256
NTOK = B * T
P = 128
NT = NTOK // P
KD = D // P
H, DK, DV = 6, 32, 64
HH = H // 2
KR = HH * DK
HV = H * DV
KSZ = 4
GT = 512
NG = NTOK // GT
SPG = GT // P
SEQG = GT // T
NCH = 7
ROWS = [KR] * 4 + [P] * 3
CH0 = [0, KR, 2 * KR, 3 * KR, 4 * KR, 4 * KR + P, 4 * KR + 2 * P]
NCHAN = 4 * KR + 3 * P
NGATE = HV + 2 * H
NH, NKV, HD = 16, 4, 16
CKV = NKV * HD
E, SH, F = 16, 2, 128
NE = E + SH
BL = 32
HEAD = 16
NEG = -1e30

C_ID = 0
C_LTRI = C_ID + P
C_TM = C_LTRI + P
C_NEG = C_TM + T
C_CAUS = C_NEG + T
C_HSEL = C_CAUS + T
C_HM = C_HSEL + 32
C_KM = C_HM + HH
C_VM = C_KM + 8
C_COS = C_VM + 32
C_SIN = C_COS + HD
C_IOTA = C_SIN + HD
NCONST = C_IOTA + NE


def constants():
    c = np.zeros((P, NCONST), np.float32)
    p = np.arange(P)[:, None]
    f = np.arange(P)[None, :]
    t = np.arange(T)[None, :]
    c[:, C_ID:C_ID + P] = p == f
    c[:, C_LTRI:C_LTRI + P] = (p > f) & (p // T == f // T)
    c[:, C_TM:C_TM + T] = p % T <= t
    c[:, C_NEG:C_NEG + T] = np.where(t < p % T, NEG, 0.0)
    c[:, C_CAUS:C_CAUS + T] = np.where(t > p % T, NEG, 0.0)
    a = np.arange(32)[None, :]
    c[:, C_HSEL:C_HSEL + 32] = (p // DK == a) & (a < HH) & (p < KR)
    c[:, C_HM:C_HM + HH] = p // DK == np.arange(HH)[None, :]
    c[:, C_KM:C_KM + 8] = p // HD == np.arange(8)[None, :]
    c[:, C_VM:C_VM + 32] = p // T == a // HD
    inv = (1.0 / np.float32(10000.0) ** (np.arange(0, HD, 2, dtype=np.float32) / np.float32(HD))).astype(np.float32)
    fr = np.outer(np.arange(T, dtype=np.float32), inv)
    emb = np.concatenate([fr, fr], -1)
    sign = np.where(np.arange(HD) < HD // 2, -1.0, 1.0)
    c[:, C_COS:C_COS + HD] = np.tile(np.cos(emb), (2, 1))
    c[:, C_SIN:C_SIN + HD] = np.tile(np.sin(emb) * sign, (2, 1))
    c[:, C_IOTA:C_IOTA + NE] = np.arange(NE)[None, :]
    return c


R_ALOG = 0
R_DT = R_ALOG + H
R_QN = R_DT + H
R_KN = R_QN + D
NROW = R_KN + CKV

W_TAP = 0
W_NORM = W_TAP + NCH * KSZ
W_GB = W_NORM + 1
W_B1 = W_GB + NE
NCOL = W_B1 + NE


def at(count):
    return count + HEAD


def alone(eng):
    eng.nop(nofuse=True)


def over(ap, axis, n):
    ap = ap.unsqueeze(axis)
    shape = list(ap.shape)
    shape[axis] = n
    return ap.to_broadcast(shape)


def build(nc, xt_d, x_d, ctx_d, consts_d, row_d, col_d, wc_d, wg_d, wo_d, wout_d, wa_d, wexp_d, b2_d, out_d):
    with ExitStack() as ctx:
        def sb(name, cols, dt=F32):
            return ctx.enter_context(nc.sbuf_tensor(name, [P, cols], dt))

        engine_sems = {"pe": [], "act": [], "dve": [], "pool": []}

        def counted(engine, name):
            s = ctx.enter_context(nc.semaphore(name))
            engine_sems[engine].append(s)
            return s

        def dma_sem(name):
            return ctx.enter_context(nc.semaphore(name))

        def start_counts(eng, name):
            for s in engine_sems[name]:
                eng.sem_inc(s, HEAD)

        scores_dr = nc.dram_tensor("scores_dr", [NT, P, H * T], F32, kind="Internal").ap()
        attend_dr = nc.dram_tensor("attend_dr", [NT, P, H * T], F32, kind="Internal").ap()
        inverse_dr = nc.dram_tensor("inverse_dr", [2, 2, B, HH * BL * BL], F32, kind="Internal").ap()

        consts = sb("consts", NCONST)
        rowp = sb("rowp", NROW)
        colp = sb("colp", NCOL)
        idb = sb("idb", P, BF16)
        negb = sb("negb", 2 * T, BF16)
        xT = sb("xT", KD * NTOK)
        xn = sb("xn", NT * D)
        arena = sb("arena", 4 * NTOK)
        vt = sb("vt", NT * HV)
        sg = sb("sg", NT * HV)
        ab = sb("ab", NT * 2 * H)
        wc = sb("wc", KD * NCHAN)
        wg = sb("wg", KD * NGATE)
        wo = sb("wo", 3 * D)
        wout = sb("wout", KD * D)
        ctxn = sb("ctxn", NT * CKV)
        krope = sb("krope", NT * CKV)
        ropes = sb("ropes", 2 * D + 2 * CKV)
        n2 = sb("n2", NT * 2 * H)
        small = sb("small", 8 * NT * H)
        work = sb("work", 12 * 1024)

        ident = consts[:, C_ID:C_ID + P]
        tmask = consts[:, C_TM:C_TM + T]

        ps = ctx.enter_context(nc.psum_tensor("ps", [P, 8, 512], F32))

        x3 = xn[:].rearrange("p (n d) -> p n d", d=D)
        xT3 = xT[:].rearrange("p (k n) -> p k n", k=KD)
        wc3 = wc[:].rearrange("p (k c) -> p k c", k=KD)
        wg3 = wg[:].rearrange("p (k c) -> p k c", k=KD)
        wo3 = wo[:].rearrange("p (k c) -> p k c", k=3)
        wout3 = wout[:].rearrange("p (k c) -> p k c", k=KD)
        ab3 = ab[:].rearrange("p (n c) -> p n c", c=2 * H)
        n23 = n2[:].rearrange("p (n c) -> p n c", c=2 * H)

        def tab(k):
            return small[:, k * NT * H:(k + 1) * NT * H]
        T_G, T_C, T_NK, T_RQ, T_A, T_B = range(6)
        stats = small[:, 6 * NT * H:7 * NT * H]
        rq_tab = small[:, 7 * NT * H:7 * NT * H + NT]

        s_cst = dma_sem("constants_in")
        s_wc = dma_sem("conv_weights_in")
        s_wg = dma_sem("gate_weights_in")
        s_wo = dma_sem("out_weights_in")
        s_xt = [dma_sem(f"xt_in{g}") for g in range(NG)]
        s_xn = dma_sem("x_in")
        s_ctx = dma_sem("context_in")
        s_sc_out = [dma_sem(f"scores_out{u}") for u in range(2)]
        s_blk_in = dma_sem("blocks_in")
        s_inv_out = dma_sem("inverse_out")
        s_out = [dma_sem(f"out_done{u}") for u in range(2)]
        s_unit_in = [dma_sem(f"unit_in{u}") for u in range(2)]

        s_idb = counted("dve", "bf16_masks_ready")
        s_xs = counted("pool", "group_staged")
        s_gmm = counted("pe", "gate_projected")
        s_gev = counted("act", "gate_evacuated")
        s_proj = counted("pe", "channels_projected")
        s_tap0 = counted("act", "first_tap_done")
        s_tap = counted("dve", "taps_summed")
        s_conv = counted("dve", "convolved")
        s_silu = counted("act", "channels_activated")
        s_sq = counted("pool", "squares_ready")
        s_ss = counted("pe", "square_sums_ready")
        s_ssev = counted("act", "square_sums_evacuated")
        s_sst = counted("pe", "square_sums_turned")
        s_n2 = counted("dve", "square_sums_by_token")
        s_vtr = counted("pe", "values_turned")
        s_vev = counted("act", "values_by_token")
        s_gk = counted("act", "gating_act_step")
        s_gd = counted("dve", "gating_dve_step")
        s_pw = counted("pool", "pool_weight_step")

        xs = work[:, 0:KD * GT].rearrange("p (k n) -> p k n", k=KD)
        ybuf = work[:, 1024:1024 + 4 * GT].rearrange("p (j n) -> p j n", j=4)
        vs = work[:, 3072:3072 + 3 * GT].rearrange("p (j n) -> p j n", j=3)
        sqs = work[:, 4608:4608 + 4 * GT].rearrange("p (j n) -> p j n", j=4)
        ssb = work[:, 6656:6656 + GT]
        BANK = [0, 1, 2, 3, 0, 1, 2]
        taps = colp[:, W_TAP:W_TAP + NCH * KSZ].rearrange("p (j k) -> p j k", k=KSZ)

        def bank_free(j, g):
            return NCH * g + (j - 4 if j >= 4 else min(j + 4, 6 if j < 3 else 3) - NCH if j < 3 else 3 - NCH) + 1

        kst = work[:, 0:2 * 2 * P].rearrange("p (u f n) -> p u f n", u=2, f=2)
        blk = work[:, 512:512 + 2 * 2 * 2 * HH * P].rearrange("p (u f q h n) -> p u f q h n", u=2, f=2, q=2, h=HH)
        gst = work[:, 3584:3584 + 2 * H * T].rearrange("p (u h t) -> p u h t", u=2, h=H)
        est = work[:, 4352:4352 + 2 * H * T].rearrange("p (u h t) -> p u h t", u=2, h=H)
        rst = work[:, 5120:5120 + 2 * H * T].rearrange("p (u h t) -> p u h t", u=2, h=H)
        ast = work[:, 5888:5888 + 2 * H * T].rearrange("p (u h t) -> p u h t", u=2, h=H)
        s_kst = counted("act", "keys_staged")
        s_kblk = counted("pool", "key_blocks_ready")
        s_qblk = counted("dve", "query_blocks_ready")
        s_gst = counted("pool", "decays_spread")
        s_dmm = counted("pe", "decay_sums_ready")
        s_kmm = counted("pe", "products_ready")
        s_e = counted("act", "decay_factors_ready")
        s_ec = counted("dve", "weighted_factors_ready")
        s_rs = counted("dve", "system_ready")
        s_as = counted("dve", "attention_ready")
        rb = arena[:, 0:HH * BL * BL].rearrange("p (h i t) -> p h i t", h=HH, i=BL)
        nb = arena[:, HH * BL * BL:2 * HH * BL * BL].rearrange("p (h i t) -> p h i t", h=HH, i=BL)
        tmp_d = work[:, 7000:7000 + 2 * 256].rearrange("p (h n) -> p h n", h=2)
        tmp_p = work[:, 7512:7512 + 256].rearrange("p (h n) -> p h n", h=1)
        s_invd = counted("dve", "inversion_dve_step")
        s_invp = counted("pool", "inversion_pool_step")

        def invert(eng, sem, h0, nh, tmp):
            flat = arena[:, HH * BL * BL:2 * HH * BL * BL]
            eng.memset(nb[:, h0:h0 + nh], 0.0).then_inc(sem, 1)
            eng.wait_ge(sem, at(1))
            for h in range(h0, h0 + nh):
                ins = eng.memset(flat[:, h * BL * BL:(h + 1) * BL * BL:BL + 1], 1.0)
            ins.then_inc(sem, 1)
            for k, t in enumerate(range(BL - 1, 0, -1)):
                w = BL - t
                prod = tmp[:, 0:nh, 0:t * w].rearrange("p h (i c) -> p h i c", i=t)
                eng.wait_ge(sem, at(2 + 2 * k))
                eng.tensor_tensor(prod, over(rb[:, h0:h0 + nh, 0:t, t], 3, w), over(nb[:, h0:h0 + nh, t, t:BL], 2, t),
                                  ALU.mult).then_inc(sem, 1)
                eng.wait_ge(sem, at(3 + 2 * k))
                eng.tensor_tensor(nb[:, h0:h0 + nh, 0:t, t:BL], nb[:, h0:h0 + nh, 0:t, t:BL], prod,
                                  ALU.subtract).then_inc(sem, 1)

        at_s = xT[:, 0:768].rearrange("p (u h t) -> p u h t", u=2, h=H)
        roff = xT[:, 768:1152].rearrange("p (u h t) -> p u h t", u=2, h=H)
        n32 = xT[:, 1152:1536].rearrange("p (u h t) -> p u h t", u=2, h=H)
        vp = xT[:, 1536:2304].rearrange("p (u h t) -> p u h t", u=2, h=H)
        wsol = xT[:, 2304:3072].rearrange("p (u c) -> p u c", u=2)
        ysb = xT[:, 3072:3840].rearrange("p (u c) -> p u c", u=2)
        og = work[:, 7768:8536].rearrange("p (u c) -> p u c", u=2)
        osq = work[:, 8536:9304].rearrange("p (u c) -> p u c", u=2)
        ogT = work[:, 9304:10072].rearrange("p (u k n) -> p u k n", u=2, k=3)
        xr = work[:, 10072:10584].rearrange("p (u c) -> p u c", u=2)
        sgr = work[:, 10584:11352].rearrange("p (u c) -> p u c", u=2)
        ms = work[:, 11352:11364].rearrange("p (u c) -> p u c", u=2)
        rs = work[:, 11364:11376].rearrange("p (u c) -> p u c", u=2)
        bn = work[:, 11376:11388].rearrange("p (u c) -> p u c", u=2)
        mv = work[:, 11388:11392].rearrange("p (u c) -> p u c", u=2)
        sd = work[:, 11392:11394].rearrange("p (u c) -> p u c", u=2)
        rsd = work[:, 11394:11396].rearrange("p (u c) -> p u c", u=2)
        eps = work[:, 11396:11397]
        s_zero = counted("dve", "correction_banks_cleared")
        s_vp = counted("pool", "scaled_values_ready")
        s_sgr = counted("pool", "scaled_gate_ready")
        s_w0 = counted("pe", "block_solves_ready")
        s_w = counted("act", "block_solves_in_sbuf")
        s_y0 = counted("pe", "coupling_ready")
        s_y = counted("act", "coupling_in_sbuf")
        s_z = counted("pe", "correction_ready")
        s_w2 = counted("dve", "solution_ready")
        s_o = counted("pe", "attended_ready")
        s_og = counted("dve", "gated_ready")
        s_osq = counted("pool", "gated_squares_ready")
        s_ms = counted("dve", "gated_square_sums_ready")
        s_rms = counted("act", "gated_rms_ready")
        s_rr = counted("dve", "gated_scale_ready")
        s_og2 = counted("pool", "normed_ready")
        s_ot = counted("pe", "normed_turned")
        s_ote = counted("act", "normed_turned_in_sbuf")
        s_xo = counted("pe", "delta_output_ready")
        s_xr = counted("dve", "residual_added")
        s_bn = counted("dve", "layernorm_stats_step")
        s_sd = counted("act", "layernorm_deviation_ready")
        s_rsd = counted("dve", "layernorm_scale_ready")
        s_x1 = counted("dve", "first_layernorm_done")
        s_rq = counted("dve", "query_square_mean_ready")
        kblk = arena[:, 0:4096].rearrange("p (u f h n) -> p u f h n", u=2, f=2, h=8)
        prob = arena[:, 4096:6144].rearrange("p (u f h k) -> p u f h k", u=2, f=2, h=8)
        probT = arena[:, 6144:8192].rearrange("p (u f c) -> p u f c", u=2, f=2)
        kx = work[:, 0:512].rearrange("p (u c) -> p u c", u=2)
        qr = work[:, 512:1024].rearrange("p (u c) -> p u c", u=2)
        kqT = work[:, 1024:2048].rearrange("p (u w f n) -> p u w f n", u=2, w=2, f=2)
        qt1 = work[:, 2048:2560].rearrange("p (u c) -> p u c", u=2)
        qt2 = work[:, 2560:3072].rearrange("p (u c) -> p u c", u=2)
        vdup = work[:, 3072:3328].rearrange("p (u s c) -> p u s c", u=2, s=2)
        vblk = work[:, 3328:3840].rearrange("p (u s g c) -> p u s g c", u=2, s=2, g=NKV)
        oT = work[:, 3840:4352].rearrange("p (u f n) -> p u f n", u=2, f=2)
        mxs = work[:, 4352:4384].rearrange("p (u f h) -> p u f h", u=2, f=2)
        sms = work[:, 4384:4416].rearrange("p (u f h) -> p u f h", u=2, f=2)
        sri = work[:, 4416:4448].rearrange("p (u f h) -> p u f h", u=2, f=2)
        bn2 = work[:, 4448:4460].rearrange("p (u c) -> p u c", u=2)
        mv2 = stats[:, 0:2 * NT].rearrange("p (n c) -> p n c", c=2)
        sd2 = stats[:, 2 * NT:3 * NT]
        rk = stats[:, 3 * NT:4 * NT]
        eps16 = work[:, 11397:11398]
        ksq = work[:, 7768:7768 + NT * CKV]
        kt1 = work[:, 8792:8792 + NT * CKV]
        kt2 = work[:, 9816:9816 + NT * CKV]
        halves = "p (h z c) -> p h z c"
        rope_q = [ropes[:, 0:D], ropes[:, D:2 * D]]
        rope_k = [ropes[:, 2 * D:2 * D + CKV], ropes[:, 2 * D + CKV:2 * D + 2 * CKV]]
        causb = negb[:, T:2 * T]
        ctx3 = ctxn[:].rearrange("p (n c) -> p n c", c=CKV)
        s_vin = [dma_sem(f"context_pair_in{u}") for u in range(2)]
        s_kd = counted("dve", "context_dve_step")
        s_ka = counted("act", "context_act_step")
        s_kp = counted("pool", "rotary_pool_step")
        s_kx = counted("pool", "keys_spread")
        s_qr = counted("pool", "queries_rotated_step")
        s_kqt = counted("pe", "keys_queries_turned")
        s_kqe = counted("act", "keys_queries_turned_in_sbuf")
        s_kb = counted("pool", "softmax_key_blocks_ready")
        s_vb = counted("pool", "value_blocks_ready")
        s_sc = counted("pe", "scores_ready")
        s_mx = counted("dve", "row_maxima_ready")
        s_sub = counted("dve", "shifted_scores_ready")
        s_exp = counted("act", "exponentials_ready")
        s_sum = counted("dve", "row_sums_step")
        s_pr = counted("dve", "probabilities_ready")
        s_pt = counted("pe", "probabilities_turned")
        s_pte = counted("act", "probabilities_turned_in_sbuf")
        s_pv = counted("pe", "softmax_outputs_ready")
        s_ove = counted("act", "softmax_outputs_in_sbuf")
        s_xp = counted("pe", "softmax_projected")
        s_xr2 = counted("dve", "second_residual_added")
        mv2s = work[:, 4460:4464].rearrange("p (u c) -> p u c", u=2)
        mv2_flat = stats[:, 0:2 * NT]
        s_mv2 = counted("dve", "second_layernorm_stats_kept")
        s_x2c = counted("dve", "second_layernorm_rows_kept")
        s_bn2 = counted("dve", "second_layernorm_stats_step")
        s_rqa = counted("act", "query_scale_act_step")
        s_rqd = counted("dve", "query_scale_ready")
        s_ln2a = counted("act", "second_layernorm_deviation_ready")
        s_ln2d = counted("dve", "second_layernorm_scale_ready")

        x2T3 = xT3
        wbuf = vt[:, 0:2 * 768].rearrange("p (u c) -> p u c", u=2)
        hbuf = vt[:, 1536:1536 + 2 * GT].rearrange("p (u c) -> p u c", u=2)
        ybf = vt[:, 2560:2560 + 2 * GT].rearrange("p (u c) -> p u c", u=2)
        x2s = vt[:, 3584:3584 + 2 * D].rearrange("p (u c) -> p u c", u=2)
        x2Ts = vt[:, 4096:4096 + 2 * D].rearrange("p (u k n) -> p u k n", u=2, k=KD)
        wab = sb("wab", KD * E)
        b2s = sb("b2s", D)
        def route(k):
            return sg[:, k * NT * E:(k + 1) * NT * E].rearrange("p (n e) -> p n e", e=E)
        elog, aff, lower, pick, pick2, spare = (route(k) for k in range(6))
        elog_flat = sg[:, 0:NT * E]
        comb_flat = sg[:, 2048:2048 + NT * NE]
        best = sg[:, 6 * NT * E:6 * NT * E + 8 * NT].rearrange("p (k n) -> p k n", k=8)
        comb = sg[:, 2048:2048 + NT * NE].rearrange("p (n e) -> p n e", e=NE)
        combs = sg[:, 2400:2400 + 2 * NE].rearrange("p (u e) -> p u e", u=2)
        combT = sg[:, 2448:2448 + 2 * P].rearrange("p (u n) -> p u n", u=2)
        ob = sg[:, 2816:2816 + 2 * D].rearrange("p (u c) -> p u c", u=2)
        bn3 = sg[:, 3328:3340].rearrange("p (u c) -> p u c", u=2)
        mv3 = sg[:, 3340:3344].rearrange("p (u c) -> p u c", u=2)
        sd3 = sg[:, 3344:3346].rearrange("p (u c) -> p u c", u=2)
        ri3 = sg[:, 3346:3348].rearrange("p (u c) -> p u c", u=2)
        s_rw = dma_sem("router_weights_in")
        s_we = [dma_sem(f"expert_weights_in{u}") for u in range(2)]
        s_x2 = counted("dve", "second_layernorm_done")
        s_x2t = counted("pe", "tokens_turned")
        s_x2e = counted("act", "tokens_turned_in_sbuf")
        s_lg = counted("pe", "router_logits_ready")
        s_el = counted("act", "router_exponentials_ready")
        s_rt = counted("dve", "routing_step")
        s_cs = counted("pool", "combine_weights_staged")
        s_ct = counted("pe", "combine_weights_turned")
        s_cte = counted("act", "combine_weights_turned_in_sbuf")
        s_b2 = counted("pe", "output_bias_ready")
        s_acc0 = counted("dve", "outputs_started")
        s_h = counted("pe", "hidden_ready")
        s_ge = counted("act", "gate_branch_ready")
        s_yy = counted("dve", "hidden_product_ready")
        s_eo = counted("pe", "expert_output_ready")
        s_eot = counted("pe", "expert_output_tile_ready")
        s_ac = counted("dve", "expert_output_added")
        s_bn3 = counted("dve", "last_layernorm_stats_step")
        s_sd3 = counted("act", "last_layernorm_deviation_ready")
        s_ri3 = counted("dve", "last_layernorm_scale_ready")
        s_ob = counted("dve", "output_rows_ready")

        ROUTE_STEPS = 21
        UIN = 1 + 2 + 8

        block = ctx.enter_context(nc.Block())

        @block.sync
        def _(sp):
            for u in range(2):
                sp.sem_inc(s_out[u], 16)
                sp.sem_inc(s_sc_out[u], 16)
            sp.dma_start(consts[:], consts_d).then_inc(s_cst, 16)
            sp.dma_start(colp[:], col_d).then_inc(s_cst, 16)
            sp.dma_start(rowp[:], row_d.partition_broadcast(P)).then_inc(s_cst, 16)
            sp.dma_start(xT3[:, :, 0:GT], xt_d.rearrange("(k p) n -> p k n", k=KD)[:, :, 0:GT]).then_inc(s_xt[0], 16)
            sp.dma_start(wg3, wg_d.rearrange("(k p) c -> p k c", k=KD)).then_inc(s_wg, 16)
            sp.dma_start(wc3, wc_d.rearrange("(k p) c -> p k c", k=KD)).then_inc(s_wc, 16)
            for g in range(1, NG):
                sp.dma_start(xT3[:, :, g * GT:(g + 1) * GT],
                             xt_d.rearrange("(k p) n -> p k n", k=KD)[:, :, g * GT:(g + 1) * GT]).then_inc(s_xt[g], 16)
            sp.dma_start(wo3, wo_d.rearrange("(k p) c -> p k c", k=3)).then_inc(s_wo, 16)
            sp.dma_start(wout3, wout_d.rearrange("(k p) c -> p k c", k=KD)).then_inc(s_wo, 16)
            sp.dma_start(x3, x_d.rearrange("(n p) d -> p n d", p=P)).then_inc(s_xn, 16)
            sp.dma_start(ctxn[:].rearrange("p (n c) -> p n c", c=CKV),
                         ctx_d.rearrange("(n p) c -> p n c", p=P)).then_inc(s_ctx, 16)
            with sp.Fori(0, NT // 2) as i:
                for u in range(2):
                    n = 2 * i + u
                    sp.wait_ge(s_rs, at(n + 1))
                    sp.dma_start(scores_dr[bass.ds(n, 1)].rearrange("n p c -> p (n c)"),
                                 rst[:, u].rearrange("p h t -> p (h t)")).then_inc(s_sc_out[u], 16)
                    sp.wait_ge(s_as, at(n + 1))
                    sp.dma_start(attend_dr[bass.ds(n, 1)].rearrange("n p c -> p (n c)"),
                                 ast[:, u].rearrange("p h t -> p (h t)")).then_inc(s_sc_out[u], 16)
            for u in range(2):
                sp.wait_ge(s_sc_out[u], 32 * (NT // 2) + 16)
            rows = scores_dr.rearrange("n (s r i) (f h q t) -> r f q (n s) h i t", s=2, r=2, f=2, h=HH, q=2)
            for r in range(2):
                for f in range(2):
                    p0 = 64 * r + 32 * f
                    for h in range(HH):
                        sp.dma_start(rb[p0:p0 + 32, h], rows[r, f, r, :, h]).then_inc(s_blk_in, 16)
            sp.wait_ge(s_invd, at(64))
            sp.wait_ge(s_invp, at(64))
            sp.dma_start(inverse_dr.rearrange("r f b c -> (r f b) c"),
                         nb.rearrange("p h i t -> p (h i t)")).then_inc(s_inv_out, 16)
            sp.wait_ge(s_inv_out, 16)
            with sp.Fori(0, NT // 2) as i:
                for u in range(2):
                    n = 2 * i + u
                    sp.wait_ge(s_o, at(n - 1))
                    sp.dma_start(at_s[:, u].rearrange("p h t -> p (h t)"),
                                 attend_dr[bass.ds(n, 1)].rearrange("n p c -> p (n c)")).then_inc(s_unit_in[u], 16)
                    for s in range(2):
                        q = 64 * s
                        sp.dma_start(roff[q:q + BL, u],
                                     scores_dr[bass.ds(n, 1)].rearrange("n p (h q t) -> (n p) h q t", h=H, q=2)
                                     [q:q + BL, :, 1]).then_inc(s_unit_in[u], 16)
                        for r in range(2):
                            q = 64 * s + BL * r
                            for f in range(2):
                                sp.dma_start(n32[q:q + BL, u, HH * f:HH * (f + 1)],
                                             inverse_dr[r, f, bass.ds(2 * n + s, 1)].rearrange(
                                                 "b (h i t) -> (b i) h t", h=HH, i=BL)).then_inc(s_unit_in[u], 16)
            with sp.Fori(0, NT // 2) as i:
                for u in range(2):
                    n = 2 * i + u
                    sp.wait_ge(s_vb, at(n - 1))
                    sp.wait_ge(s_invp, at(64))
                    for z in range(2):
                        sp.dma_start(vdup[64 * z:64 * z + 64, u],
                                     ctx_d.rearrange("(n s k) c -> n k s c", s=2, k=T)[bass.ds(n, 1)]
                                     .rearrange("n k s c -> (n k) s c")).then_inc(s_vin[u], 16)
            sp.wait_ge(s_w0, at(NT))
            sp.dma_start(wab[:].rearrange("p (k e) -> p k e", k=KD),
                         wa_d.rearrange("(k p) e -> p k e", k=KD)).then_inc(s_rw, 16)
            sp.dma_start(b2s[0:NE, :], b2_d).then_inc(s_rw, 16)
            with sp.Fori(0, NE // 2) as i:
                for u in range(2):
                    e = 2 * i + u
                    sp.wait_ge(s_eo, at(4 * (e - 1)))
                    sp.dma_start(wbuf[:, u, :], wexp_d[bass.ds(e, 1)].rearrange("e p c -> p (e c)")).then_inc(s_we[u], 16)
            with sp.Fori(0, NT // 2) as i:
                for u in range(2):
                    n = 2 * i + u
                    sp.wait_ge(s_ob, at(n + 1))
                    sp.dma_start(out_d[bass.ds(n * P, P)], ob[:, u, :]).then_inc(s_out[u], 16)
            for u in range(2):
                sp.wait_ge(s_out[u], 16 * (NT // 2) + 16)

        @block.tensor
        def _(pe):
            start_counts(pe, "pe")
            pe.wait_ge(s_cst, 48)
            pe.wait_ge(s_wg, 16)
            pe.wait_ge(s_wc, 16)
            for g in range(NG):
                pe.wait_ge(s_xt[g], 16)
            with pe.Fori(0, NG) as g:
                pe.wait_ge(s_xs, at(g + 1))
                alone(pe)
                for m in range(SPG):
                    pe.wait_ge(s_gev, at(SPG * g + m - 1))
                    alone(pe)
                    for k in range(KD):
                        mm = pe.matmul(ps[:, 4 + m % 2, 0:NGATE], xs[:, k, m * P:(m + 1) * P], wg3[:, k, :],
                                       start=(k == 0), stop=(k == KD - 1))
                    mm.then_inc(s_gmm, 1)

                def turn_values(j):
                    pe.wait_ge(s_silu, at(NCH * g + 5 + j))
                    alone(pe)
                    if j == 0:
                        pe.wait_ge(s_n2, at(g))
                        alone(pe)
                    else:
                        pe.wait_ge(s_vev, at(3 * g + j))
                        alone(pe)
                    for m in range(SPG):
                        mm = pe.transpose(ps[:, 6, m * P:(m + 1) * P], vs[:, j, m * P:(m + 1) * P], ident)
                    mm.then_inc(s_vtr, 1)

                for j in range(NCH):
                    pe.wait_ge(s_conv, at(bank_free(j, g)))
                    alone(pe)
                    for k in range(KD):
                        mm = pe.matmul(ps[0:ROWS[j], BANK[j], :], wc3[:, k, CH0[j]:CH0[j] + ROWS[j]],
                                       xT3[:, k, bass.ds(g * GT, GT)], start=(k == 0), stop=(k == KD - 1))
                    mm.then_inc(s_proj, 1)
                pe.wait_ge(s_ssev, at(g))
                alone(pe)
                for j in range(4):
                    pe.wait_ge(s_sq, at(4 * g + j + 1))
                    alone(pe)
                    mm = pe.matmul(ps[32 * j:32 * j + 32, 7, :], consts[0:KR, C_HSEL:C_HSEL + 32], sqs[0:KR, j, :],
                                   start=True, stop=True)
                mm.then_inc(s_ss, 1)
                for j in range(3):
                    turn_values(j)
                pe.wait_ge(s_ssev, at(g + 1))
                pe.wait_ge(s_vev, at(3 * g + 3))
                alone(pe)
                for m in range(SPG):
                    mm = pe.transpose(ps[:, 6, m * P:(m + 1) * P], ssb[:, m * P:(m + 1) * P], ident)
                mm.then_inc(s_sst, 1)
            pe.wait_ge(s_n2, at(NG))
            pe.wait_ge(s_gev, at(NT))
            pe.wait_ge(s_conv, at(NCH * NG))
            pe.wait_ge(s_idb, at(2))
            alone(pe)
            with pe.Fori(0, NT // 2) as i:
                for u in range(2):
                    n = 2 * i + u
                    pe.wait_ge(s_gst, at(n + 1))
                    pe.wait_ge(s_e, at(n - 1))
                    alone(pe)
                    pe.matmul(ps[:, u, 0:H * T], consts[:, C_LTRI:C_LTRI + P],
                              gst[:, u].rearrange("p h t -> p (h t)"), start=True, stop=False)
                    pe.matmul(ps[:, u, 0:H * T], idb[:], over(negb[:, 0:T], 1, H),
                              start=False, stop=True).then_inc(s_dmm, 1)
                    pe.wait_ge(s_kst, at(n + 1))
                    pe.wait_ge(s_kblk, at(n + 1))
                    pe.wait_ge(s_qblk, at(n + 1))
                    pe.wait_ge(s_as, at(n - 1))
                    alone(pe)
                    for f in range(2):
                        for s in range(2):
                            mm = pe.matmul(ps[64 * s:64 * s + 64, 2 + 2 * u + f, 0:2 * HH * T],
                                           kst[0:KR, u, f, 64 * s:64 * s + 64],
                                           blk[0:KR, u, f, :, :, 64 * s:64 * s + 64].rearrange("p q h n -> p (q h) n"),
                                           start=True, stop=True)
                    mm.then_inc(s_kmm, 1)
            pe.wait_ge(s_as, at(NT))
            pe.wait_ge(s_pw, at(1))
            pe.wait_ge(s_zero, at(3))
            alone(pe)
            with pe.Fori(0, NT // 2) as i:
                for u in range(2):
                    n = 2 * i + u
                    pe.wait_ge(s_vp, at(n + 1))
                    pe.wait_ge(s_unit_in[u], 16 * UIN * (i + 1))
                    pe.wait_ge(s_ote, at(n - 1))
                    alone(pe)
                    for h in range(H):
                        for q in range(4):
                            r = slice(32 * q, 32 * q + 32)
                            mm = pe.matmul(ps[r, u, h * DV:(h + 1) * DV], n32[r, u, h, :], vp[r, u, h, :],
                                           start=True, stop=True)
                    mm.then_inc(s_w0, 1)
                for u in range(2):
                    n = 2 * i + u
                    pe.wait_ge(s_w, at(n + 1))
                    pe.wait_ge(s_xr, at(n - 1))
                    alone(pe)
                    for h in range(H):
                        for s in range(2):
                            mm = pe.matmul(ps[64 * s + 32:64 * s + 64, 2 + u, h * DV:(h + 1) * DV],
                                           roff[64 * s:64 * s + 32, u, h, :],
                                           wsol[64 * s:64 * s + 32, u, h * DV:(h + 1) * DV], start=True, stop=True)
                    mm.then_inc(s_y0, 1)
                for u in range(2):
                    n = 2 * i + u
                    pe.wait_ge(s_y, at(n + 1))
                    pe.wait_ge(s_w2, at(n - 1))
                    alone(pe)
                    for h in range(H):
                        for s in range(2):
                            r = slice(64 * s + 32, 64 * s + 64)
                            mm = pe.matmul(ps[r, 4 + u, h * DV:(h + 1) * DV], n32[r, u, h, :],
                                           ysb[r, u, h * DV:(h + 1) * DV], start=True, stop=True)
                    mm.then_inc(s_z, 1)
                for u in range(2):
                    n = 2 * i + u
                    pe.wait_ge(s_w2, at(n + 1))
                    pe.wait_ge(s_og, at(n - 1))
                    alone(pe)
                    for h in range(H):
                        for s in range(2):
                            r = slice(64 * s, 64 * s + 64)
                            mm = pe.matmul(ps[r, 6 + u, h * DV:(h + 1) * DV], at_s[r, u, h, :],
                                           wsol[r, u, h * DV:(h + 1) * DV], start=True, stop=True)
                    mm.then_inc(s_o, 1)
                for u in range(2):
                    n = 2 * i + u
                    pe.wait_ge(s_og2, at(n + 1))
                    alone(pe)
                    for k in range(3):
                        mm = pe.transpose(ps[:, u, k * P:(k + 1) * P], og[:, u, k * P:(k + 1) * P], ident)
                    mm.then_inc(s_ot, 1)
                for u in range(2):
                    n = 2 * i + u
                    pe.wait_ge(s_ote, at(n + 1))
                    alone(pe)
                    for k in range(3):
                        mm = pe.matmul(ps[:, 2 + u, 0:D], ogT[:, u, k, :], wo3[:, k, :], start=(k == 0), stop=(k == 2))
                    mm.then_inc(s_xo, 1)
            pe.wait_ge(s_xr, at(NT))
            pe.wait_ge(s_og, at(NT))
            pe.wait_ge(s_rqd, at(1))
            alone(pe)
            with pe.Fori(0, NT // 2) as i:
                for u in range(2):
                    n = 2 * i + u
                    pe.wait_ge(s_kx, at(n + 1))
                    pe.wait_ge(s_qr, at(3 * n + 3))
                    pe.wait_ge(s_xr2, at(n - 1))
                    alone(pe)
                    for w, src in enumerate((kx, qr)):
                        for f in range(2):
                            c = 2 * P * w + P * f
                            mm = pe.transpose(ps[:, u, c:c + P], src[:, u, f * P:(f + 1) * P], ident)
                    mm.then_inc(s_kqt, 1)
                for u in range(2):
                    n = 2 * i + u
                    pe.wait_ge(s_kqe, at(n + 1))
                    pe.wait_ge(s_kb, at(n + 1))
                    alone(pe)
                    for f in range(2):
                        pe.wait_ge(s_sub, at(2 * (n - 2) + f + 1))
                        alone(pe)
                        bank = 2 + 2 * u + f
                        pe.matmul(ps[:, bank, :], idb[:], over(causb, 1, 8), start=True, stop=False)
                        for s in range(2):
                            q = slice(64 * s, 64 * s + 64)
                            mm = pe.matmul(ps[q, bank, :], kqT[:, u, 1, f, q], kblk[:, u, f, :, q],
                                           start=False, stop=True)
                        mm.then_inc(s_sc, 1)
                for u in range(2):
                    n = 2 * i + u
                    for f in range(2):
                        pe.wait_ge(s_pr, at(2 * n + f + 1))
                        pe.wait_ge(s_pte, at(2 * n + f - 1))
                        alone(pe)
                        for c in range(4):
                            mm = pe.transpose(ps[:, 6 + f, c * P:(c + 1) * P],
                                              prob[:, u, f, 2 * c:2 * c + 2, :].rearrange("p h k -> p (h k)"), ident)
                        mm.then_inc(s_pt, 1)
                for u in range(2):
                    n = 2 * i + u
                    pe.wait_ge(s_vb, at(n + 1))
                    alone(pe)
                    for f in range(2):
                        pe.wait_ge(s_pte, at(2 * n + f + 1))
                        alone(pe)
                        for s in range(2):
                            for c in range(4):
                                q = slice(c * P + 64 * s, c * P + 64 * s + 64)
                                mm = pe.matmul(ps[32 * c:32 * c + 32, u, f * P + 64 * s:f * P + 64 * s + 64],
                                               vblk[:, u, s, 2 * f + c // 2, :], probT[:, u, f, q], start=True, stop=True)
                    mm.then_inc(s_pv, 1)
                for u in range(2):
                    n = 2 * i + u
                    pe.wait_ge(s_ove, at(n + 1))
                    alone(pe)
                    for k in range(KD):
                        mm = pe.matmul(ps[:, u, D:2 * D], oT[:, u, k, :], wout3[:, k, :], start=(k == 0), stop=(k == KD - 1))
                    mm.then_inc(s_xp, 1)
            pe.wait_ge(s_rw, 32)
            with pe.Fori(0, NT // 2) as i:
                for u in range(2):
                    n = 2 * i + u
                    pe.wait_ge(s_x2, at(n + 1))
                    pe.wait_ge(s_xr2, at(NT))
                    pe.wait_ge(s_x2e, at(n - 1))
                    alone(pe)
                    for k in range(KD):
                        mm = pe.transpose(ps[:, u, k * P:(k + 1) * P], x2s[:, u, k * P:(k + 1) * P], ident)
                    mm.then_inc(s_x2t, 1)
                for u in range(2):
                    n = 2 * i + u
                    pe.wait_ge(s_x2e, at(n + 1))
                    pe.wait_ge(s_el, at(n - 1))
                    alone(pe)
                    for k in range(KD):
                        mm = pe.matmul(ps[:, 2 + u, 0:E], x2Ts[:, u, k, :], wab[:, k * E:(k + 1) * E],
                                       start=(k == 0), stop=(k == KD - 1))
                    mm.then_inc(s_lg, 1)
            with pe.Fori(0, NT // 2) as i:
                for u in range(2):
                    n = 2 * i + u
                    pe.wait_ge(s_cs, at(n + 1))
                    pe.wait_ge(s_cte, at(n - 1))
                    alone(pe)
                    pe.transpose(ps[0:NE, u, 0:P], combs[:, u, :], ident).then_inc(s_ct, 1)
                for u in range(2):
                    n = 2 * i + u
                    pe.wait_ge(s_cte, at(n + 1))
                    pe.wait_ge(s_acc0, at(n - 1))
                    alone(pe)
                    pe.matmul(ps[:, 2 + u, 0:D], combT[0:NE, u, :], b2s[0:NE, :], start=True, stop=True).then_inc(s_b2, 1)
            pe.wait_ge(s_acc0, at(NT))
            alone(pe)
            with pe.Fori(0, NE // 2) as i:
                for k in range(2 * NG + 1):
                    if k < 2 * NG:
                        u, g = divmod(k, NG)
                        m = 2 * NG * i + k
                        if g == 0:
                            pe.wait_ge(s_we[u], 16 * (i + 1))
                        pe.wait_ge(s_yy, at(m - 1))
                        alone(pe)
                        for w in range(2):
                            for c in range(KD):
                                o = w * KD * F + c * F
                                mm = pe.matmul(ps[:, 2 * w + k % 2, :], wbuf[:, u, o:o + F], x2T3[:, c, g * GT:(g + 1) * GT],
                                               start=(c == 0), stop=(c == KD - 1))
                        mm.then_inc(s_h, 1)
                    if k > 0:
                        u, g = divmod(k - 1, NG)
                        m = 2 * NG * i + k - 1
                        pe.wait_ge(s_yy, at(m + 1))
                        alone(pe)
                        for t in range(SPG):
                            pe.wait_ge(s_ac, at(SPG * (m - 1) + t + 1))
                            alone(pe)
                            mm = pe.matmul(ps[:, 4 + t, 0:D], ybf[:, (k - 1) % 2, t * P:(t + 1) * P],
                                           wbuf[:, u, 2 * KD * F:2 * KD * F + D], start=True, stop=True)
                            if t < SPG - 1:
                                mm.then_inc(s_eot, 1)
                        mm.then_inc(s_eo, 1)

        @block.scalar
        def _(act):
            start_counts(act, "act")
            act.wait_ge(s_cst, 48)
            with act.Fori(0, NG) as g:
                def first_tap(j):
                    act.wait_ge(s_proj, at(NCH * g + j + 1))
                    act.wait_ge(s_silu, at(bank_free(j, g)))
                    act.activation(ybuf[0:ROWS[j], BANK[j], :], ps[0:ROWS[j], BANK[j], :], ACT.Copy,
                                   scale=taps[0:ROWS[j], j, KSZ - 1:KSZ]).then_inc(s_tap0, 1)

                def silu(j):
                    act.wait_ge(s_conv, at(NCH * g + j + 1))
                    if j < 4:
                        dst = arena[0:KR, bass.ds(g * GT + j * NTOK, GT)]
                    else:
                        dst = vs[:, j - 4, :]
                        act.wait_ge(s_vtr, at(3 * (g - 1) + j - 3))
                    act.activation(dst, ybuf[0:ROWS[j], BANK[j], :], ACT.Silu).then_inc(s_silu, 1)

                for m in range(SPG):
                    n = SPG * g + m
                    act.wait_ge(s_gmm, at(n + 1))
                    act.activation(sg[:, bass.ds(n * HV, HV)], ps[:, 4 + m % 2, 0:HV], ACT.Silu)
                    act.activation(ab[:, bass.ds(n * 2 * H, 2 * H)], ps[:, 4 + m % 2, HV:NGATE],
                                   ACT.Copy).then_inc(s_gev, 1)
                first_tap(0)
                for j in range(1, NCH):
                    first_tap(j)
                    silu(j - 1)
                silu(NCH - 1)
                act.wait_ge(s_ss, at(g + 1))
                act.wait_ge(s_sst, at(g))
                act.activation(ssb, ps[:, 7, :], ACT.Copy).then_inc(s_ssev, 1)
                for j in range(3):
                    act.wait_ge(s_vtr, at(3 * g + j + 1))
                    act.activation(
                        vt[:, bass.ds(SPG * HV * g, SPG * HV)].rearrange("p (m c) -> p m c", m=SPG)[:, :, j * P:(j + 1) * P],
                        ps[:, 6, :].rearrange("p (m c) -> p m c", m=SPG), ACT.Copy).then_inc(s_vev, 1)

            a_t, b_t = tab(T_A), tab(T_B)
            act.wait_ge(s_gd, at(2))
            act.activation(a_t, a_t, ACT.Exp, scale=-1.0).then_inc(s_gk, 1)
            act.activation(b_t, ab3[:, :, H:2 * H], ACT.Exp, scale=-1.0).then_inc(s_gk, 1)
            act.activation(rowp[:, R_ALOG:R_ALOG + H], rowp[:, R_ALOG:R_ALOG + H], ACT.Exp).then_inc(s_gk, 1)
            act.wait_ge(s_gk, at(1))
            act.activation(a_t, a_t, ACT.Ln, bias=1.0).then_inc(s_gk, 1)
            act.wait_ge(s_gd, at(5))
            act.activation(tab(T_NK).rearrange("p (n h) -> p n h", h=H), n23[:, :, H:2 * H],
                           ACT.Sqrt).then_inc(s_gk, 1)
            act.activation(tab(T_RQ).rearrange("p (n h) -> p n h", h=H), n23[:, :, 0:H],
                           ACT.Sqrt, scale=float(DK)).then_inc(s_gk, 1)
            with act.Fori(0, NT // 2) as i:
                for u in range(2):
                    n = 2 * i + u
                    act.wait_ge(s_kmm, at(n - 1))
                    for f in range(2):
                        ins = act.activation(kst[0:KR, u, f, :], arena[0:KR, bass.ds(n * P + (2 + f) * NTOK, P)], ACT.Copy)
                    ins.then_inc(s_kst, 1)
                    act.wait_ge(s_dmm, at(n + 1))
                    act.wait_ge(s_as, at(n - 1))
                    act.activation(est[:, u].rearrange("p h t -> p (h t)"), ps[:, u, 0:H * T], ACT.Exp).then_inc(s_e, 1)
            act.wait_ge(s_zero, at(2))
            act.wait_ge(s_kd, at(2))
            act.activation(rk, rk, ACT.Sqrt, bias=eps, scale=1.0 / CKV).then_inc(s_ka, 1)
            act.wait_ge(s_zero, at(3))
            with act.Fori(0, NT // 2) as i:
                for u in range(2):
                    n = 2 * i + u
                    act.wait_ge(s_w0, at(n + 1))
                    act.wait_ge(s_o, at(n - 1))
                    act.activation(wsol[:, u, :], ps[:, u, 0:HV], ACT.Copy).then_inc(s_w, 1)
                for u in range(2):
                    n = 2 * i + u
                    act.wait_ge(s_y0, at(n + 1))
                    act.wait_ge(s_z, at(n - 1))
                    act.activation(ysb[:, u, :], ps[:, 2 + u, 0:HV], ACT.Copy).then_inc(s_y, 1)
                for u in range(2):
                    n = 2 * i + u
                    act.wait_ge(s_ms, at(n + 1))
                    act.activation(ms[:, u, :], ms[:, u, :], ACT.Sqrt, bias=eps, scale=1.0 / DV).then_inc(s_rms, 1)
                for u in range(2):
                    n = 2 * i + u
                    act.wait_ge(s_ot, at(n + 1))
                    act.wait_ge(s_xo, at(n - 1))
                    act.activation(ogT[:, u].rearrange("p k n -> p (k n)"), ps[:, u, 0:3 * P], ACT.Copy).then_inc(s_ote, 1)
                for u in range(2):
                    n = 2 * i + u
                    act.wait_ge(s_bn, at(2 * n + 2))
                    act.activation(sd[:, u, :], mv[:, u, 1:2], ACT.Sqrt, bias=eps).then_inc(s_sd, 1)
            act.wait_ge(s_x1, at(NT))
            act.wait_ge(s_rq, at(NT))
            act.activation(rq_tab, rq_tab, ACT.Sqrt, bias=eps16, scale=float(HD)).then_inc(s_rqa, 1)
            with act.Fori(0, NT // 2) as i:
                for u in range(2):
                    n = 2 * i + u
                    act.wait_ge(s_kqt, at(n + 1))
                    act.wait_ge(s_kb, at(n - 1))
                    act.wait_ge(s_sc, at(2 * (n - 1)))
                    act.activation(kqT[:, u].rearrange("p w f n -> p (w f n)"), ps[:, u, :], ACT.Copy).then_inc(s_kqe, 1)
                for u in range(2):
                    n = 2 * i + u
                    for f in range(2):
                        act.wait_ge(s_sub, at(2 * n + f + 1))
                        alone(act)
                        act.activation(prob[:, u, f], prob[:, u, f], ACT.Exp,
                                       scale=rq_tab[:, bass.ds(n, 1)]).then_inc(s_exp, 1)
                for u in range(2):
                    n = 2 * i + u
                    for f in range(2):
                        act.wait_ge(s_pt, at(2 * n + f + 1))
                        act.wait_ge(s_pv, at(n - 1))
                        act.activation(probT[:, u, f, :], ps[:, 6 + f, :], ACT.Copy).then_inc(s_pte, 1)
                for u in range(2):
                    n = 2 * i + u
                    act.wait_ge(s_pv, at(n + 1))
                    act.wait_ge(s_xp, at(n - 1))
                    act.activation(oT[:, u].rearrange("p f n -> p (f n)"), ps[:, u, 0:D], ACT.Copy).then_inc(s_ove, 1)
            act.wait_ge(s_mv2, at(NT))
            act.activation(sd2, mv2[:, :, 1], ACT.Sqrt, bias=eps).then_inc(s_ln2a, 1)
            with act.Fori(0, NT // 2) as i:
                for u in range(2):
                    n = 2 * i + u
                    act.wait_ge(s_x2t, at(n + 1))
                    act.wait_ge(s_lg, at(n - 1))
                    src = ps[:, u, 0:D].rearrange("p (k n) -> p k n", k=KD)
                    act.activation(x2Ts[:, u], src, ACT.Copy)
                    act.activation(x2T3[:, :, bass.ds(n * P, P)], src, ACT.Copy).then_inc(s_x2e, 1)
                for u in range(2):
                    n = 2 * i + u
                    act.wait_ge(s_lg, at(n + 1))
                    alone(act)
                    act.activation(elog_flat[:, bass.ds(n * E, E)], ps[:, 2 + u, 0:E], ACT.Exp, scale=-1.0).then_inc(s_el, 1)
            with act.Fori(0, NT // 2) as i:
                for u in range(2):
                    n = 2 * i + u
                    act.wait_ge(s_ct, at(n + 1))
                    act.wait_ge(s_b2, at(n - 1))
                    act.activation(combT[0:NE, u, :], ps[0:NE, u, 0:P], ACT.Copy).then_inc(s_cte, 1)
            with act.Fori(0, NE // 2) as i:
                for k in range(2 * NG):
                    m = 2 * NG * i + k
                    e = 2 * i + k // NG
                    act.wait_ge(s_h, at(m + 1))
                    act.wait_ge(s_yy, at(m - 1))
                    alone(act)
                    act.activation(hbuf[:, k % 2, :], ps[:, k % 2, :], ACT.Gelu,
                                   bias=colp[:, bass.ds(e + W_GB, 1)]).then_inc(s_ge, 1)
            with act.Fori(0, NT // 2) as i:
                for u in range(2):
                    n = 2 * i + u
                    act.wait_ge(s_bn3, at(2 * n + 2))
                    act.wait_ge(s_ri3, at(n - 1))
                    act.activation(sd3[:, u, :], mv3[:, u, 1:2], ACT.Sqrt, bias=eps).then_inc(s_sd3, 1)

        @block.vector
        def _(dve):
            start_counts(dve, "dve")
            dve.wait_ge(s_cst, 48)
            dve.tensor_copy(idb[:], ident).then_inc(s_idb, 1)
            dve.tensor_copy(negb[:], consts[:, C_NEG:C_NEG + 2 * T]).then_inc(s_idb, 1)
            with dve.Fori(0, NG) as g:
                for j in range(NCH):
                    m = NCH * g + j
                    r = ROWS[j]
                    y = ybuf[0:r, BANK[j], :].rearrange("p (s t) -> p s t", t=T)
                    z = ps[0:r, BANK[j], :].rearrange("p (s t) -> p s t", t=T)
                    dve.wait_ge(s_tap0, at(m + 1))
                    for d in range(1, KSZ):
                        if d > 1:
                            dve.wait_ge(s_tap, at(2 * m + d - 1))
                        dve.scalar_tensor_tensor(y[:, :, d:T], z[:, :, 0:T - d], taps[0:r, j, KSZ - 1 - d:KSZ - d],
                                                 y[:, :, d:T], ALU.mult, ALU.add
                                                 ).then_inc(s_tap if d < KSZ - 1 else s_conv, 1)
                dve.wait_ge(s_sst, at(g + 1))
                for f in range(2):
                    ins = dve.tensor_copy(
                        n2[:, bass.ds(SPG * 2 * H * g, SPG * 2 * H)].rearrange(
                            "p (m q f h) -> p m q f h", m=SPG, q=2, f=2)[:, :, :, f, :],
                        ps[:, 6, :].rearrange("p (m q f c) -> p m q f c", m=SPG, q=2, f=2)[:, :, :, f, 0:HH])
                ins.then_inc(s_n2, 1)
            a_t = tab(T_A).rearrange("p (n h) -> p n h", h=H)
            g_t = tab(T_G).rearrange("p (n h) -> p n h", h=H)
            c_t, b_t = tab(T_C), tab(T_B)
            dve.wait_ge(s_gev, at(NT))
            dve.tensor_tensor(g_t, ab3[:, :, 0:H], over(rowp[:, R_DT:R_DT + H], 1, NT), ALU.add).then_inc(s_gd, 1)
            dve.wait_ge(s_gd, at(1))
            dve.scalar_tensor_tensor(a_t, g_t, -1.0, g_t, ALU.mult, ALU.max).then_inc(s_gd, 1)
            dve.wait_ge(s_gd, at(2))
            dve.tensor_scalar(g_t, g_t, 0.0, None, ALU.max).then_inc(s_gd, 1)
            dve.wait_ge(s_n2, at(NG))
            dve.tensor_scalar(n2[:], n2[:], 1e-6, None, ALU.add).then_inc(s_gd, 1)
            dve.wait_ge(s_gd, at(4))
            dve.tensor_copy(c_t.rearrange("p (n h) -> p n h", h=H), n23[:, :, H:2 * H]).then_inc(s_gd, 1)
            dve.wait_ge(s_gk, at(4))
            dve.tensor_tensor(g_t, g_t, a_t, ALU.add).then_inc(s_gd, 1)
            dve.wait_ge(s_gd, at(6))
            dve.scalar_tensor_tensor(g_t, g_t, -1.0, over(rowp[:, R_ALOG:R_ALOG + H], 1, NT),
                                     ALU.mult, ALU.mult).then_inc(s_gd, 1)
            dve.scalar_tensor_tensor(c_t, b_t, 1.0, c_t, ALU.add, ALU.mult).then_inc(s_gd, 1)
            dve.wait_ge(s_gd, at(8))
            dve.reciprocal(c_t, c_t).then_inc(s_gd, 1)
            dve.wait_ge(s_gk, at(6))
            dve.reciprocal(tab(T_RQ), tab(T_RQ)).then_inc(s_gd, 1)
            dve.wait_ge(s_gd, at(9))
            with dve.Fori(0, NT // 2) as i:
                for u in range(2):
                    n = 2 * i + u
                    dve.wait_ge(s_kmm, at(n - 1))
                    for f in range(2):
                        ins = dve.tensor_tensor(blk[0:KR, u, f, 1], over(arena[0:KR, bass.ds(n * P + f * NTOK, P)], 1, HH),
                                                over(consts[0:KR, C_HM:C_HM + HH], 2, P), ALU.mult)
                    ins.then_inc(s_qblk, 1)
                    dve.wait_ge(s_e, at(n + 1))
                    dve.tensor_tensor(est[:, u], est[:, u], over(small[:, bass.ds(n * H + T_C * NT * H, H)], 2, T),
                                      ALU.mult).then_inc(s_ec, 1)
                    dve.wait_ge(s_ec, at(n + 1))
                    dve.wait_ge(s_kmm, at(n + 1))
                    prod = ps[:, 2 + 2 * u:4 + 2 * u, 0:2 * HH * T].rearrange("p f (q c) -> p f q c", q=2)
                    e2 = est[:, u].rearrange("p (f h) t -> p f (h t)", f=2)
                    dve.wait_ge(s_sc_out[u], 32 * i + 16)
                    dve.tensor_tensor(rst[:, u].rearrange("p (f h) t -> p f (h t)", f=2), prod[:, :, 0], e2,
                                      ALU.mult).then_inc(s_rs, 1)
                    dve.tensor_tensor(ast[:, u].rearrange("p (f h) t -> p f (h t)", f=2), prod[:, :, 1], e2,
                                      ALU.mult).then_inc(s_as, 1)
            dve.wait_ge(s_ctx, 16)
            dve.memset(eps, 1e-5).then_inc(s_zero, 1)
            dve.memset(eps16, HD * 1e-5).then_inc(s_zero, 1)
            dve.tensor_tensor(ksq, ctxn[:], ctxn[:], ALU.mult).then_inc(s_kd, 1)
            dve.wait_ge(s_kd, at(1))
            dve.tensor_reduce(rk, ksq.rearrange("p (n c) -> p n c", c=CKV), AXX, ALU.add).then_inc(s_kd, 1)
            dve.wait_ge(s_ka, at(1))
            dve.reciprocal(rk, rk).then_inc(s_kd, 1)
            dve.wait_ge(s_kd, at(3))
            dve.tensor_tensor(ctx3, ctx3, over(rk, 2, CKV), ALU.mult).then_inc(s_kd, 1)
            dve.wait_ge(s_blk_in, 16 * 12)
            invert(dve, s_invd, 0, 2, tmp_d)
            dve.wait_ge(s_as, at(NT))
            dve.memset(ps[:, 4:6, :], 0.0).then_inc(s_zero, 1)
            dve.wait_ge(s_xn, 16)
            with dve.Fori(0, NT // 2) as i:
                for u in range(2):
                    n = 2 * i + u
                    dve.wait_ge(s_z, at(n + 1))
                    dve.tensor_tensor(wsol[:, u, :], wsol[:, u, :], ps[:, 4 + u, 0:HV], ALU.subtract).then_inc(s_w2, 1)
                for u in range(2):
                    n = 2 * i + u
                    dve.wait_ge(s_o, at(n + 1))
                    dve.wait_ge(s_sgr, at(n + 1))
                    dve.wait_ge(s_ot, at(n - 1))
                    dve.tensor_tensor(og[:, u, :], ps[:, 6 + u, 0:HV], sgr[:, u, :], ALU.mult).then_inc(s_og, 1)
                for u in range(2):
                    n = 2 * i + u
                    dve.wait_ge(s_osq, at(n + 1))
                    dve.wait_ge(s_rr, at(n - 1))
                    dve.tensor_reduce(ms[:, u, :], osq[:, u, :].rearrange("p (h t) -> p h t", h=H), AXX,
                                      ALU.add).then_inc(s_ms, 1)
                for u in range(2):
                    n = 2 * i + u
                    dve.wait_ge(s_rms, at(n + 1))
                    dve.wait_ge(s_og2, at(n - 1))
                    dve.reciprocal(rs[:, u, :], ms[:, u, :]).then_inc(s_rr, 1)
                for u in range(2):
                    n = 2 * i + u
                    dve.wait_ge(s_xo, at(n + 1))
                    dve.wait_ge(s_x1, at(n - 1))
                    dve.tensor_tensor(xr[:, u, :], ps[:, 2 + u, 0:D], xn[:, bass.ds(n * D, D)], ALU.add).then_inc(s_xr, 1)
                for u in range(2):
                    n = 2 * i + u
                    dve.wait_ge(s_xr, at(n + 1))
                    dve.wait_ge(s_sd, at(n - 1))
                    dve.bn_stats(bn[:, u, :], xr[:, u, :]).then_inc(s_bn, 1)
                    dve.wait_ge(s_bn, at(2 * n + 1))
                    alone(dve)
                    dve.bn_aggr(mv[:, u, :], bn[:, u, :]).then_inc(s_bn, 1)
                for u in range(2):
                    n = 2 * i + u
                    dve.wait_ge(s_sd, at(n + 1))
                    dve.reciprocal(rsd[:, u, :], sd[:, u, :]).then_inc(s_rsd, 1)
                    dve.wait_ge(s_rsd, at(n + 1))
                    dve.tensor_scalar(xn[:, bass.ds(n * D, D)], xr[:, u, :], mv[:, u, 0:1], rsd[:, u, :],
                                      ALU.subtract, ALU.mult).then_inc(s_x1, 1)
                    dve.scalar_tensor_tensor(rq_tab[:, bass.ds(n, 1)], mv[:, u, 1:2], rsd[:, u, :], rsd[:, u, :],
                                             ALU.mult, ALU.mult).then_inc(s_rq, 1)
            dve.wait_ge(s_rqa, at(1))
            dve.reciprocal(rq_tab, rq_tab).then_inc(s_rqd, 1)
            with dve.Fori(0, NT // 2) as i:
                for u in range(2):
                    n = 2 * i + u
                    for f in range(2):
                        sc = ps[:, 2 + 2 * u + f, :].rearrange("p (h k) -> p h k", h=8)
                        dve.wait_ge(s_sc, at(2 * n + f + 1))
                        dve.tensor_reduce(mxs[:, u, f], sc, AXX, ALU.max).then_inc(s_mx, 1)
                        dve.wait_ge(s_mx, at(2 * n + f + 1))
                        dve.wait_ge(s_pt, at(2 * (n - 2) + f + 1))
                        dve.tensor_tensor(prob[:, u, f], sc, over(mxs[:, u, f], 2, T), ALU.subtract).then_inc(s_sub, 1)
                for u in range(2):
                    n = 2 * i + u
                    for f in range(2):
                        m = 2 * n + f
                        dve.wait_ge(s_exp, at(m + 1))
                        dve.tensor_reduce(sms[:, u, f], prob[:, u, f], AXX, ALU.add).then_inc(s_sum, 1)
                        dve.wait_ge(s_sum, at(2 * m + 1))
                        dve.reciprocal(sri[:, u, f], sms[:, u, f]).then_inc(s_sum, 1)
                        dve.wait_ge(s_sum, at(2 * m + 2))
                        dve.tensor_tensor(prob[:, u, f], prob[:, u, f], over(sri[:, u, f], 2, T),
                                          ALU.mult).then_inc(s_pr, 1)
                for u in range(2):
                    n = 2 * i + u
                    dve.wait_ge(s_xp, at(n + 1))
                    dve.wait_ge(s_qr, at(3 * n + 3))
                    row = xn[:, bass.ds(n * D, D)]
                    dve.tensor_tensor(row, ps[:, u, D:2 * D], row, ALU.add).then_inc(s_xr2, 1)
                    dve.wait_ge(s_xr2, at(n + 1))
                    alone(dve)
                    dve.bn_stats(bn2[:, u, :], row).then_inc(s_bn2, 1)
                    dve.wait_ge(s_bn2, at(2 * n + 1))
                    alone(dve)
                    dve.bn_aggr(mv2s[:, u, :], bn2[:, u, :]).then_inc(s_bn2, 1)
                    dve.wait_ge(s_bn2, at(2 * n + 2))
                    alone(dve)
                    dve.tensor_copy(mv2_flat[:, bass.ds(2 * n, 2)], mv2s[:, u, :]).then_inc(s_mv2, 1)
            dve.wait_ge(s_ln2a, at(1))
            dve.reciprocal(sd2, sd2).then_inc(s_ln2d, 1)
            dve.wait_ge(s_ln2d, at(1))
            with dve.Fori(0, NT // 2) as i:
                for u in range(2):
                    n = 2 * i + u
                    row = xn[:, bass.ds(n * D, D)]
                    dve.wait_ge(s_x2t, at(n - 1))
                    dve.wait_ge(s_x2c, at(n - 1))
                    dve.tensor_scalar(x2s[:, u, :], row, mv2_flat[:, bass.ds(2 * n, 1)], sd2[:, bass.ds(n, 1)],
                                      ALU.subtract, ALU.mult).then_inc(s_x2, 1)
                    dve.wait_ge(s_x2, at(n + 1))
                    alone(dve)
                    dve.tensor_copy(row, x2s[:, u, :]).then_inc(s_x2c, 1)
            steps = [0]

            def routed(ins):
                ins.then_inc(s_rt, 1)
                steps[0] += 1
                dve.wait_ge(s_rt, at(steps[0]))

            iota = over(consts[:, C_IOTA:C_IOTA + E], 1, NT)
            dve.wait_ge(s_el, at(NT))
            routed(dve.tensor_scalar(aff, elog, 1.0, None, ALU.add))
            routed(dve.reciprocal(aff, aff))
            left = aff
            for k, sel in enumerate((pick, pick2)):
                routed(dve.tensor_reduce(best[:, k], left, AXX, ALU.max))
                routed(dve.tensor_tensor(lower, left, over(best[:, k], 2, E), ALU.is_lt))
                routed(dve.scalar_tensor_tensor(lower, lower, 64.0, iota, ALU.mult, ALU.add))
                routed(dve.tensor_reduce(best[:, 2], lower, AXX, ALU.min))
                routed(dve.tensor_tensor(sel, iota, over(best[:, 2], 2, E), ALU.is_equal))
                if k == 0:
                    routed(dve.scalar_tensor_tensor(spare, sel, -4.0, left, ALU.mult, ALU.add))
                    left = spare
            routed(dve.tensor_tensor(best[:, 3], best[:, 0], best[:, 1], ALU.add))
            routed(dve.reciprocal(best[:, 4], best[:, 3]))
            for k, sel in enumerate((pick, pick2)):
                routed(dve.tensor_tensor(best[:, 5 + k], best[:, k], best[:, 4], ALU.mult))
                routed(dve.tensor_tensor(sel, sel, over(best[:, 5 + k], 2, E), ALU.mult))
            routed(dve.memset(comb, 1.0))
            routed(dve.tensor_tensor(comb[:, :, 0:E], pick, pick2, ALU.add))
            dve.wait_ge(s_x2c, at(NT))
            with dve.Fori(0, NT // 2) as i:
                for u in range(2):
                    n = 2 * i + u
                    row = xn[:, bass.ds(n * D, D)]
                    dve.wait_ge(s_b2, at(n + 1))
                    dve.scalar_tensor_tensor(row, row, 2.0, ps[:, 2 + u, 0:D], ALU.mult, ALU.add).then_inc(s_acc0, 1)
            with dve.Fori(0, NE // 2) as i:
                def add_outputs(k):
                    g = k % NG
                    m = 2 * NG * i + k
                    e = 2 * i + k // NG
                    for t in range(SPG):
                        n = SPG * g + t
                        if t < SPG - 1:
                            dve.wait_ge(s_eot, at(3 * m + t + 1))
                        else:
                            dve.wait_ge(s_eo, at(m + 1))
                        dve.wait_ge(s_ac, at(2 * NG * SPG * i + k * SPG + t - NG * SPG + 1))
                        row = xn[:, n * D:(n + 1) * D]
                        dve.scalar_tensor_tensor(row, ps[:, 4 + t, 0:D], comb_flat[:, bass.ds(e + n * NE, 1)], row,
                                                 ALU.mult, ALU.add).then_inc(s_ac, 1)

                for k in range(2 * NG + 1):
                    if k < 2 * NG:
                        m = 2 * NG * i + k
                        e = 2 * i + k // NG
                        dve.wait_ge(s_ge, at(m + 1))
                        dve.wait_ge(s_eo, at(m - 1))
                        dve.scalar_tensor_tensor(ybf[:, k % 2, :], ps[:, 2 + k % 2, :], colp[:, bass.ds(e + W_B1, 1)],
                                                 hbuf[:, k % 2, :], ALU.add, ALU.mult).then_inc(s_yy, 1)
                    if k > 0:
                        add_outputs(k - 1)
            dve.wait_ge(s_ac, at(NE * NT))
            with dve.Fori(0, NT // 2) as i:
                for u in range(2):
                    n = 2 * i + u
                    row = xn[:, bass.ds(n * D, D)]
                    dve.wait_ge(s_ob, at(n - 1))
                    alone(dve)
                    dve.bn_stats(bn3[:, u, :], row).then_inc(s_bn3, 1)
                    dve.wait_ge(s_bn3, at(2 * n + 1))
                    alone(dve)
                    dve.bn_aggr(mv3[:, u, :], bn3[:, u, :]).then_inc(s_bn3, 1)
                for u in range(2):
                    n = 2 * i + u
                    row = xn[:, bass.ds(n * D, D)]
                    dve.wait_ge(s_sd3, at(n + 1))
                    dve.reciprocal(ri3[:, u, :], sd3[:, u, :]).then_inc(s_ri3, 1)
                    dve.wait_ge(s_ri3, at(n + 1))
                    dve.wait_ge(s_out[u], 16 * i + 16)
                    dve.tensor_scalar(ob[:, u, :], row, mv3[:, u, 0:1], ri3[:, u, :],
                                      ALU.subtract, ALU.mult).then_inc(s_ob, 1)

        @block.gpsimd
        def _(pool):
            start_counts(pool, "pool")
            pool.wait_ge(s_cst, 48)
            for g in range(NG):
                pool.wait_ge(s_xt[g], 16)
            pool.wait_ge(s_wo, 32)
            pool.tensor_scalar(wo[:], wo[:], colp[:, W_NORM:W_NORM + 1], None, ALU.mult).then_inc(s_pw, 1)
            with pool.Fori(0, NG) as g:
                pool.wait_ge(s_gmm, at(SPG * g))
                pool.tensor_copy(xs, xT3[:, :, bass.ds(g * GT, GT)]).then_inc(s_xs, 1)
                for j in range(4):
                    pool.wait_ge(s_silu, at(NCH * g + j + 1))
                    pool.wait_ge(s_ss, at(g))
                    src = arena[0:KR, bass.ds(g * GT + j * NTOK, GT)]
                    pool.tensor_tensor(sqs[0:KR, j, :], src, src, ALU.mult).then_inc(s_sq, 1)
            pool.wait_ge(s_gd, at(9))
            pool.wait_ge(s_ss, at(NG))
            with pool.Fori(0, NT // 2) as i:
                for u in range(2):
                    n = 2 * i + u
                    pool.wait_ge(s_dmm, at(n - 1))
                    pool.tensor_tensor(gst[:, u], over(small[:, bass.ds(n * H + T_G * NT * H, H)], 2, T),
                                       over(tmask, 1, H), ALU.mult).then_inc(s_gst, 1)
                    pool.wait_ge(s_kmm, at(n - 1))
                    for f in range(2):
                        ins = pool.tensor_tensor(blk[0:KR, u, f, 0],
                                                 over(arena[0:KR, bass.ds(n * P + (2 + f) * NTOK, P)], 1, HH),
                                                 over(consts[0:KR, C_HM:C_HM + HH], 2, P), ALU.mult)
                    ins.then_inc(s_kblk, 1)
            def turned(ins):
                ins.then_inc(s_kp, 1)

            for w0, nh, (cosw, sinw) in ((R_QN, NH, rope_q), (R_KN, NKV, rope_k)):
                w = rowp[:, w0:w0 + nh * HD]
                turned(pool.tensor_tensor(cosw.rearrange("p (h c) -> p h c", h=nh), w.rearrange("p (h c) -> p h c", h=nh),
                                          over(consts[:, C_COS:C_COS + HD], 1, nh), ALU.mult))
                for z in range(2):
                    turned(pool.tensor_tensor(sinw.rearrange(halves, h=nh, z=2)[:, :, z],
                                              w.rearrange(halves, h=nh, z=2)[:, :, 1 - z],
                                              over(consts[:, C_SIN + 8 * z:C_SIN + 8 * z + 8], 1, nh), ALU.mult))
            pool.wait_ge(s_kp, at(6))
            pool.wait_ge(s_kd, at(4))
            turned(pool.tensor_tensor(kt1.rearrange("p (n c) -> p n c", c=CKV), ctx3, over(rope_k[0], 1, NT), ALU.mult))
            for h in range(NKV):
                for z in range(2):
                    a, b = HD * h + 8 * z, HD * h + 8 * (1 - z)
                    turned(pool.tensor_tensor(kt2.rearrange("p (n c) -> p n c", c=CKV)[:, :, a:a + 8], ctx3[:, :, b:b + 8],
                                              over(rope_k[1][:, a:a + 8], 1, NT), ALU.mult))
            pool.wait_ge(s_kp, at(15))
            turned(pool.tensor_tensor(krope[:], kt1, kt2, ALU.add))
            pool.wait_ge(s_blk_in, 16 * 12)
            invert(pool, s_invp, 2, 1, tmp_p)
            with pool.Fori(0, NT // 2) as i:
                for u in range(2):
                    n = 2 * i + u
                    pool.wait_ge(s_w0, at(n - 1))
                    pool.tensor_tensor(vp[:, u], vt[:, bass.ds(n * HV, HV)].rearrange("p (h t) -> p h t", h=H),
                                       over(small[:, bass.ds(n * H + T_NK * NT * H, H)], 2, DV), ALU.mult).then_inc(s_vp, 1)
                    pool.wait_ge(s_og, at(n - 1))
                    pool.tensor_tensor(sgr[:, u, :].rearrange("p (h t) -> p h t", h=H),
                                       sg[:, bass.ds(n * HV, HV)].rearrange("p (h t) -> p h t", h=H),
                                       over(small[:, bass.ds(n * H + T_RQ * NT * H, H)], 2, DV), ALU.mult).then_inc(s_sgr, 1)
                for u in range(2):
                    n = 2 * i + u
                    pool.wait_ge(s_og, at(n + 1))
                    pool.wait_ge(s_ms, at(n - 1))
                    pool.tensor_tensor(osq[:, u, :], og[:, u, :], og[:, u, :], ALU.mult).then_inc(s_osq, 1)
                for u in range(2):
                    n = 2 * i + u
                    pool.wait_ge(s_rr, at(n + 1))
                    o3 = og[:, u, :].rearrange("p (h t) -> p h t", h=H)
                    pool.wait_ge(s_osq, at(n + 1))
                    pool.tensor_tensor(o3, o3, over(rs[:, u, :], 2, DV), ALU.mult).then_inc(s_og2, 1)
            pool.wait_ge(s_kp, at(16))
            with pool.Fori(0, NT // 2) as i:
                for u in range(2):
                    n = 2 * i + u
                    pool.wait_ge(s_kqt, at(n - 1))
                    pool.tensor_copy(kx[:, u, :].rearrange("p (g r c) -> p g r c", g=NKV, r=4),
                                     over(krope[:, bass.ds(n * CKV, CKV)].rearrange("p (g c) -> p g c", g=NKV), 2, 4)
                                     ).then_inc(s_kx, 1)
                    pool.wait_ge(s_x1, at(n + 1))
                    row = xn[:, bass.ds(n * D, D)]
                    pool.tensor_tensor(qt1[:, u, :], row, rope_q[0], ALU.mult)
                    for z in range(2):
                        ins = pool.tensor_tensor(qt2[:, u, :].rearrange(halves, h=NH, z=2)[:, :, z],
                                                 row.rearrange(halves, h=NH, z=2)[:, :, 1 - z],
                                                 rope_q[1].rearrange(halves, h=NH, z=2)[:, :, z], ALU.mult)
                        ins.then_inc(s_qr, 1)
                    pool.wait_ge(s_qr, at(3 * n + 2))
                    pool.tensor_tensor(qr[:, u, :], qt1[:, u, :], qt2[:, u, :], ALU.add).then_inc(s_qr, 1)
                    pool.wait_ge(s_vin[u], 32 * (i + 1))
                    pool.wait_ge(s_pv, at(n - 1))
                    for s in range(2):
                        ins = pool.tensor_tensor(vblk[:, u, s].rearrange("p g (z c) -> p g z c", z=2),
                                                 over(vdup[:, u, s].rearrange("p (g c) -> p g c", g=NKV), 2, 2),
                                                 over(consts[:, C_VM:C_VM + 32].rearrange("p (z c) -> p z c", z=2), 1, NKV),
                                                 ALU.mult)
                    ins.then_inc(s_vb, 1)
                for u in range(2):
                    n = 2 * i + u
                    pool.wait_ge(s_kqe, at(n + 1))
                    pool.wait_ge(s_sc, at(2 * (n - 1)))
                    for f in range(2):
                        ins = pool.tensor_tensor(kblk[:, u, f], over(kqT[:, u, 0, f, :], 1, 8),
                                                 over(consts[:, C_KM:C_KM + 8], 2, P), ALU.mult)
                    ins.then_inc(s_kb, 1)
            pool.wait_ge(s_rt, at(ROUTE_STEPS))
            with pool.Fori(0, NT // 2) as i:
                for u in range(2):
                    n = 2 * i + u
                    pool.wait_ge(s_ct, at(n - 1))
                    pool.tensor_copy(combs[:, u, :], comb_flat[:, bass.ds(n * NE, NE)]).then_inc(s_cs, 1)


def kernel(**inputs):
    import numpy as _np
    import concourse.bacc as _bacc
    from concourse.bass_utils import run_bass_kernel_spmd as _run

    a = {k: _np.asarray(v) for k, v in inputs.items()}
    x = _np.ascontiguousarray(a["x"]).reshape(NTOK, D)
    wq, wk, wv = a["L0_attn_Wq"], a["L0_attn_Wk"], a["L0_attn_Wv"]
    cat = _np.concatenate
    conv = cat([a["L0_attn_conv_q_w"], a["L0_attn_conv_k_w"], a["L0_attn_conv_v_w"]])[:, 0, :]
    col = _np.zeros((P, NCOL), _np.float32)
    for j in range(NCH):
        col[0:ROWS[j], W_TAP + j * KSZ:W_TAP + (j + 1) * KSZ] = conv[CH0[j]:CH0[j] + ROWS[j]]
    col[:, W_NORM] = _np.tile(a["L0_attn_norm_w"], 2)
    col[:, W_GB:W_GB + NE] = cat([a["L0_ffn_rgb"], a["L0_ffn_sgb"]]).T
    col[:, W_B1:W_B1 + NE] = cat([a["L0_ffn_rb1"], a["L0_ffn_sb1"]]).T
    row = cat([a["L0_attn_A_log"], a["L0_attn_dt_bias"], a["L0_xattn_q_norm_w"], a["L0_xattn_k_norm_w"]])
    g = cat([a["L0_ffn_rg"], a["L0_ffn_sg"]])
    w1 = cat([a["L0_ffn_rw1"], a["L0_ffn_sw1"]])
    w2 = cat([a["L0_ffn_rw2"], a["L0_ffn_sw2"]])
    lay = lambda w: w.reshape(NE, KD, P, F).transpose(0, 2, 1, 3).reshape(NE, P, KD * F)
    arrays = {
        "xt": x.T, "x": x, "ctx": a["ctx_512"].reshape(NTOK, CKV), "consts": constants(),
        "row": row.reshape(NROW), "col": col,
        "wc": cat([wq, wk, wv]).T, "wg": cat([a["L0_attn_Wg"], a["L0_attn_Wa"], a["L0_attn_Wb"]]).T,
        "wo": a["L0_attn_Wo"].T, "wout": a["L0_xattn_w_out"].T, "wa": a["L0_ffn_wa"],
        "wexp": cat([lay(g), lay(w1), w2], axis=2), "b2": cat([a["L0_ffn_rb2"], a["L0_ffn_sb2"]]),
    }
    nc = _bacc.Bacc("TRN2", target_bir_lowering=False, num_devices=1)
    args = []
    for name in arrays:
        arrays[name] = _np.ascontiguousarray(arrays[name], dtype=_np.float32)
        args.append(nc.dram_tensor(name + "_dram", arrays[name].shape, F32, kind="ExternalInput").ap())
    out = nc.dram_tensor("out_dram", (NTOK, D), F32, kind="ExternalOutput").ap()
    build(nc, *args, out)
    r = _run(nc, [{k + "_dram": v for k, v in arrays.items()}], core_ids=[0])
    return r.results[0]["out_dram"].reshape(B, T, D)
```

```python
from contextlib import ExitStack

import numpy as np

import concourse.bass as bass
from concourse import mybir

F32 = mybir.dt.float32
BF16 = mybir.dt.bfloat16
U32 = mybir.dt.uint32
ALU = mybir.AluOpType
ACT = mybir.ActivationFunctionType
AXX = mybir.AxisListType.X

B, T, D = 32, 64, 256
NTOK = B * T
P = 128
NT = NTOK // P
KD = D // P
H, DK, DV = 6, 32, 64
HH = H // 2
KR = HH * DK
HV = H * DV
KSZ = 4
GT = 512
NG = NTOK // GT
SPG = GT // P
SEQG = GT // T
NCH = 7
ROWS = [KR] * 4 + [P] * 3
CH0 = [0, KR, 2 * KR, 3 * KR, 4 * KR, 4 * KR + P, 4 * KR + 2 * P]
NCHAN = 4 * KR + 3 * P
NGATE = HV + 2 * H
NH, NKV, HD = 16, 4, 16
CKV = NKV * HD
E, SH, F = 16, 2, 128
NE = E + SH
NSLOT = 48
EW = 2 * KD * F + D
BL = 32
HEAD = 16
NEG = -1e30

C_ID = 0
C_LTRI = C_ID + P
C_TM = C_LTRI + P
C_NEG = C_TM + T
C_CAUS = C_NEG + T
C_HSEL = C_CAUS + T
C_HM = C_HSEL + 32
C_KM = C_HM + HH
C_VM = C_KM + 8
C_COS = C_VM + 32
C_SIN = C_COS + HD
C_IOTA = C_SIN + HD
C_K128 = C_IOTA + NE
C_TILE = C_K128 + NT
C_PRE = C_TILE + NSLOT
C_ONE = C_PRE + P
NCONST = C_ONE + P


def constants():
    c = np.zeros((P, NCONST), np.float32)
    p = np.arange(P)[:, None]
    f = np.arange(P)[None, :]
    t = np.arange(T)[None, :]
    c[:, C_ID:C_ID + P] = p == f
    c[:, C_LTRI:C_LTRI + P] = (p > f) & (p // T == f // T)
    c[:, C_TM:C_TM + T] = p % T <= t
    c[:, C_NEG:C_NEG + T] = np.where(t < p % T, NEG, 0.0)
    c[:, C_CAUS:C_CAUS + T] = np.where(t > p % T, NEG, 0.0)
    a = np.arange(32)[None, :]
    c[:, C_HSEL:C_HSEL + 32] = (p // DK == a) & (a < HH) & (p < KR)
    c[:, C_HM:C_HM + HH] = p // DK == np.arange(HH)[None, :]
    c[:, C_KM:C_KM + 8] = p // HD == np.arange(8)[None, :]
    c[:, C_VM:C_VM + 32] = p // T == a // HD
    inv = (1.0 / np.float32(10000.0) ** (np.arange(0, HD, 2, dtype=np.float32) / np.float32(HD))).astype(np.float32)
    fr = np.outer(np.arange(T, dtype=np.float32), inv)
    emb = np.concatenate([fr, fr], -1)
    sign = np.where(np.arange(HD) < HD // 2, -1.0, 1.0)
    c[:, C_COS:C_COS + HD] = np.tile(np.cos(emb), (2, 1))
    c[:, C_SIN:C_SIN + HD] = np.tile(np.sin(emb) * sign, (2, 1))
    c[:, C_IOTA:C_IOTA + NE] = np.arange(NE)[None, :]
    c[:, C_K128:C_K128 + NT] = P * np.arange(NT)[None, :]
    c[:, C_TILE:C_TILE + NSLOT] = np.arange(NSLOT)[None, :]
    c[:, C_PRE:C_PRE + P] = p < f
    c[:, C_ONE:C_ONE + P] = 1.0
    return c


R_ALOG = 0
R_DT = R_ALOG + H
R_QN = R_DT + H
R_KN = R_QN + D
NROW = R_KN + CKV

W_TAP = 0
W_NORM = W_TAP + NCH * KSZ
W_GB = W_NORM + 1
W_B1 = W_GB + NE
NCOL = W_B1 + NE


def at(count):
    return count + HEAD


def alone(eng):
    eng.nop(nofuse=True)


def over(ap, axis, n):
    ap = ap.unsqueeze(axis)
    shape = list(ap.shape)
    shape[axis] = n
    return ap.to_broadcast(shape)


def build(nc, xt_d, x_d, ctx_d, consts_d, row_d, col_d, wc_d, wg_d, wo_d, wout_d, wa_d, wexp_d, b2_d, bias_d, out_d):
    with ExitStack() as ctx:
        def sb(name, cols, dt=F32):
            return ctx.enter_context(nc.sbuf_tensor(name, [P, cols], dt))

        engine_sems = {"pe": [], "act": [], "dve": [], "pool": []}

        def counted(engine, name):
            s = ctx.enter_context(nc.semaphore(name))
            engine_sems[engine].append(s)
            return s

        def dma_sem(name):
            return ctx.enter_context(nc.semaphore(name))

        def start_counts(eng, name):
            for s in engine_sems[name]:
                eng.sem_inc(s, HEAD)

        scores_dr = nc.dram_tensor("scores_dr", [NT, P, H * T], F32, kind="Internal").ap()
        attend_dr = nc.dram_tensor("attend_dr", [NT, P, H * T], F32, kind="Internal").ap()
        bias_dr = nc.dram_tensor("bias_dr", [3, E * 2 * F], BF16, kind="Internal").ap()
        slots_dr = nc.dram_tensor("slots_dr", [(NSLOT + 4) * P, D], F32, kind="Internal").ap()
        expert_dr = nc.dram_tensor("expert_dr", [NSLOT * P, D], F32, kind="Internal").ap()
        inverse_dr = nc.dram_tensor("inverse_dr", [B, 2, BL, 2, HH * BL], F32, kind="Internal").ap()

        BPC = E * 2 * F // P
        consts = sb("consts", NCONST)
        rowp = sb("rowp", NROW)
        colp = sb("colp", NCOL)
        idb = sb("idb", P, BF16)
        onesb = sb("onesb", P, BF16)
        negb = sb("negb", 2 * T, BF16)
        xT = sb("xT", KD * NTOK)
        xn = sb("xn", NT * D)
        arena = sb("arena", 4 * NTOK)
        vsg = sb("vsg", 2 * NT * HV)
        vt = vsg[:, 0:NT * HV]
        sg = vsg[:, NT * HV:2 * NT * HV]
        ab = sb("ab", NT * 2 * H)
        wc = sb("wc", KD * NCHAN)
        wg = sb("wg", KD * NGATE)
        wo = sb("wo", 3 * D)
        wout = sb("wout", KD * D)
        ctxn = sb("ctxn", NT * CKV)
        zero = sb("zero", D)
        brow = sb("brow", E * 2 * F, BF16)
        bsp = sb("bsp", 3 * BPC)
        bsb = sb("bsb", 3 * BPC, BF16)
        krope = sb("krope", NT * CKV)
        ropes = sb("ropes", 2 * D + 2 * CKV)
        n2 = sb("n2", NT * 2 * H)
        small = sb("small", 8 * NT * H)
        work = sb("work", 12 * 1024)

        ident = consts[:, C_ID:C_ID + P]
        tmask = consts[:, C_TM:C_TM + T]

        ps = ctx.enter_context(nc.psum_tensor("ps", [P, 8, 512], F32))

        x3 = xn[:].rearrange("p (n d) -> p n d", d=D)
        xT3 = xT[:].rearrange("p (k n) -> p k n", k=KD)
        wc3 = wc[:].rearrange("p (k c) -> p k c", k=KD)
        wg3 = wg[:].rearrange("p (k c) -> p k c", k=KD)
        wo3 = wo[:].rearrange("p (k c) -> p k c", k=3)
        wout3 = wout[:].rearrange("p (k c) -> p k c", k=KD)
        ab3 = ab[:].rearrange("p (n c) -> p n c", c=2 * H)
        n23 = n2[:].rearrange("p (n c) -> p n c", c=2 * H)

        def tab(k):
            return small[:, k * NT * H:(k + 1) * NT * H]
        T_G, T_C, T_NK, T_RQ, T_A, T_B = range(6)
        stats = small[:, 6 * NT * H:7 * NT * H]
        rq_tab = small[:, 7 * NT * H:7 * NT * H + NT]

        s_cst = dma_sem("constants_in")
        s_wg = dma_sem("projection_weights_in")
        s_wo = dma_sem("out_weights_in")
        s_xt = [dma_sem(f"xt_in{g}") for g in range(NG)]
        s_xn = dma_sem("x_and_context_in")
        s_sc_out = [dma_sem(f"scores_out{u}") for u in range(2)]
        s_blk_in = dma_sem("blocks_in")
        s_inv_out = dma_sem("inverse_out")
        s_out = [dma_sem(f"out_done{u}") for u in range(2)]
        s_unit_in = [dma_sem(f"unit_in{u}") for u in range(2)]

        s_idb = counted("dve", "bf16_masks_ready")
        s_xs = counted("pool", "group_staged")
        s_gmm = counted("pe", "gate_projected")
        s_gev = counted("act", "gate_evacuated")
        s_proj = counted("pe", "channels_projected")
        s_tap0 = counted("act", "first_tap_done")
        s_tap = counted("dve", "taps_summed")
        s_conv = counted("dve", "convolved")
        s_silu = counted("act", "channels_activated")
        s_sq = counted("pool", "squares_ready")
        s_ss = counted("pe", "square_sums_ready")
        s_ssev = counted("act", "square_sums_evacuated")
        s_sst = counted("pe", "square_sums_turned")
        s_n2 = counted("dve", "square_sums_by_token")
        s_vtr = counted("pe", "values_turned")
        s_vev = counted("act", "values_by_token")
        s_gk = counted("act", "gating_act_step")
        s_gd = counted("dve", "gating_dve_step")
        s_pw = counted("pool", "pool_weight_step")

        xs = work[:, 0:KD * GT].rearrange("p (k n) -> p k n", k=KD)
        ybuf = work[:, 1024:1024 + 4 * GT].rearrange("p (j n) -> p j n", j=4)
        vs = work[:, 3072:3072 + 3 * GT].rearrange("p (j n) -> p j n", j=3)
        sqs = work[:, 4608:4608 + 4 * GT].rearrange("p (j n) -> p j n", j=4)
        ssb = work[:, 6656:6656 + GT]
        BANK = [0, 1, 2, 3, 0, 1, 2]
        taps = colp[:, W_TAP:W_TAP + NCH * KSZ].rearrange("p (j k) -> p j k", k=KSZ)

        def bank_free(j, g):
            return NCH * g + (j - 4 if j >= 4 else min(j + 4, 6 if j < 3 else 3) - NCH if j < 3 else 3 - NCH) + 1

        kst = work[:, 0:2 * 2 * P].rearrange("p (u f n) -> p u f n", u=2, f=2)
        blk = work[:, 512:512 + 2 * 2 * 2 * HH * P].rearrange("p (u f q h n) -> p u f q h n", u=2, f=2, q=2, h=HH)
        gst = work[:, 3584:3584 + 2 * H * T].rearrange("p (u h t) -> p u h t", u=2, h=H)
        est = work[:, 4352:4352 + 2 * H * T].rearrange("p (u h t) -> p u h t", u=2, h=H)
        rst = work[:, 5120:5120 + 2 * H * T].rearrange("p (u h t) -> p u h t", u=2, h=H)
        ast = work[:, 5888:5888 + 2 * H * T].rearrange("p (u h t) -> p u h t", u=2, h=H)
        s_kst = counted("act", "keys_staged")
        s_kblk = counted("pool", "key_blocks_ready")
        s_qblk = counted("dve", "query_blocks_ready")
        s_gst = counted("pool", "decays_spread")
        s_dmm = counted("pe", "decay_sums_ready")
        s_kmm = counted("pe", "products_ready")
        s_e = counted("act", "decay_factors_ready")
        s_ec = counted("dve", "weighted_factors_ready")
        s_rs = counted("dve", "system_ready")
        s_as = counted("dve", "attention_ready")
        rb = arena[:, 0:HH * BL * BL].rearrange("p (h i t) -> p h i t", h=HH, i=BL)
        nb_flat = arena[:, HH * BL * BL:2 * HH * BL * BL]
        nb = nb_flat.rearrange("p (i h t) -> p h i t", h=HH, i=BL)
        tmp_d = work[:, 7000:7000 + 2 * 256].rearrange("p (h n) -> p h n", h=2)
        tmp_p = work[:, 7512:7512 + 256].rearrange("p (h n) -> p h n", h=1)
        s_invd = counted("dve", "inversion_dve_step")
        s_invp = counted("pool", "inversion_pool_step")

        def invert(eng, sem, h0, nh, tmp):
            eng.memset(nb[:, h0:h0 + nh], 0.0).then_inc(sem, 1)
            eng.wait_ge(sem, at(1))
            for h in range(h0, h0 + nh):
                ins = eng.memset(nb_flat[:, h * BL:h * BL + (HH * BL + 1) * (BL - 1) + 1:HH * BL + 1], 1.0)
            ins.then_inc(sem, 1)
            for k, t in enumerate(range(BL - 1, 0, -1)):
                w = BL - t
                prod = tmp[:, 0:nh, 0:t * w].rearrange("p h (i c) -> p h i c", i=t)
                eng.wait_ge(sem, at(2 + 2 * k))
                eng.tensor_tensor(prod, over(rb[:, h0:h0 + nh, 0:t, t], 3, w), over(nb[:, h0:h0 + nh, t, t:BL], 2, t),
                                  ALU.mult).then_inc(sem, 1)
                eng.wait_ge(sem, at(3 + 2 * k))
                eng.tensor_tensor(nb[:, h0:h0 + nh, 0:t, t:BL], nb[:, h0:h0 + nh, 0:t, t:BL], prod,
                                  ALU.subtract).then_inc(sem, 1)

        at_s = xT[:, 0:768].rearrange("p (u h t) -> p u h t", u=2, h=H)
        roff = xT[:, 768:1152].rearrange("p (u h t) -> p u h t", u=2, h=H)
        n32 = xT[:, 1152:1536].rearrange("p (u h t) -> p u h t", u=2, h=H)
        vp = xT[:, 1536:2304].rearrange("p (u h t) -> p u h t", u=2, h=H)
        wsol = xT[:, 2304:3072].rearrange("p (u c) -> p u c", u=2)
        ysb = xT[:, 3072:3840].rearrange("p (u c) -> p u c", u=2)
        og = work[:, 7768:8536].rearrange("p (u c) -> p u c", u=2)
        osq = work[:, 8536:9304].rearrange("p (u c) -> p u c", u=2)
        ogT = work[:, 9304:10072].rearrange("p (u k n) -> p u k n", u=2, k=3)
        xr = work[:, 10072:10584].rearrange("p (u c) -> p u c", u=2)
        sgr = work[:, 10584:11352].rearrange("p (u c) -> p u c", u=2)
        ms = work[:, 11352:11364].rearrange("p (u c) -> p u c", u=2)
        rs = work[:, 11364:11376].rearrange("p (u c) -> p u c", u=2)
        bn = work[:, 11376:11388].rearrange("p (u c) -> p u c", u=2)
        mv = work[:, 11388:11392].rearrange("p (u c) -> p u c", u=2)
        sd = work[:, 11392:11394].rearrange("p (u c) -> p u c", u=2)
        rsd = work[:, 11394:11396].rearrange("p (u c) -> p u c", u=2)
        eps = work[:, 11396:11397]
        s_zero = counted("dve", "correction_banks_cleared")
        s_vp = counted("pool", "scaled_values_ready")
        s_sgr = counted("pool", "scaled_gate_ready")
        s_w0 = counted("pe", "block_solves_ready")
        s_w = counted("act", "block_solves_in_sbuf")
        s_y0 = counted("pe", "coupling_ready")
        s_y = counted("act", "coupling_in_sbuf")
        s_z = counted("pe", "correction_ready")
        s_w2 = counted("dve", "solution_ready")
        s_o = counted("pe", "attended_ready")
        s_og = counted("dve", "gated_ready")
        s_osq = counted("pool", "gated_squares_ready")
        s_ms = counted("dve", "gated_square_sums_ready")
        s_rms = counted("act", "gated_rms_ready")
        s_rr = counted("dve", "gated_scale_ready")
        s_og2 = counted("pool", "normed_ready")
        s_ot = counted("pe", "normed_turned")
        s_ote = counted("act", "normed_turned_in_sbuf")
        s_xo = counted("pe", "delta_output_ready")
        s_xr = counted("dve", "residual_added")
        s_bn = counted("dve", "layernorm_stats_step")
        s_sd = counted("act", "layernorm_deviation_ready")
        s_rsd = counted("dve", "layernorm_scale_ready")
        s_x1 = counted("dve", "first_layernorm_done")
        s_rq = counted("dve", "query_square_mean_ready")
        kblk = arena[:, 0:4096].rearrange("p (u f h n) -> p u f h n", u=2, f=2, h=8)
        prob = arena[:, 4096:6144].rearrange("p (u f h k) -> p u f h k", u=2, f=2, h=8)
        probT = arena[:, 6144:8192].rearrange("p (u f c) -> p u f c", u=2, f=2)
        kx = work[:, 0:512].rearrange("p (u c) -> p u c", u=2)
        qr = work[:, 512:1024].rearrange("p (u c) -> p u c", u=2)
        kqT = work[:, 1024:2048].rearrange("p (u w f n) -> p u w f n", u=2, w=2, f=2)
        qt1 = work[:, 2048:2560].rearrange("p (u c) -> p u c", u=2)
        qt2 = work[:, 2560:3072].rearrange("p (u c) -> p u c", u=2)
        vdup = work[:, 3072:3328].rearrange("p (u s c) -> p u s c", u=2, s=2)
        vblk = work[:, 3328:3840].rearrange("p (u s g c) -> p u s g c", u=2, s=2, g=NKV)
        oT = work[:, 3840:4352].rearrange("p (u f n) -> p u f n", u=2, f=2)
        mxs = work[:, 4352:4384].rearrange("p (u f h) -> p u f h", u=2, f=2)
        sms = work[:, 4384:4416].rearrange("p (u f h) -> p u f h", u=2, f=2)
        sri = work[:, 4416:4448].rearrange("p (u f h) -> p u f h", u=2, f=2)
        bn2 = work[:, 4448:4460].rearrange("p (u c) -> p u c", u=2)
        mv2 = stats[:, 0:2 * NT].rearrange("p (n c) -> p n c", c=2)
        sd2 = stats[:, 2 * NT:3 * NT]
        rk = stats[:, 3 * NT:4 * NT]
        eps16 = work[:, 11397:11398]
        ksq = work[:, 7768:7768 + NT * CKV]
        kt1 = work[:, 8792:8792 + NT * CKV]
        kt2 = work[:, 9816:9816 + NT * CKV]
        halves = "p (h z c) -> p h z c"
        rope_q = [ropes[:, 0:D], ropes[:, D:2 * D]]
        rope_k = [ropes[:, 2 * D:2 * D + CKV], ropes[:, 2 * D + CKV:2 * D + 2 * CKV]]
        causb = negb[:, T:2 * T]
        ctx3 = ctxn[:].rearrange("p (n c) -> p n c", c=CKV)
        s_vin = [dma_sem(f"context_pair_in{u}") for u in range(2)]
        s_kd = counted("dve", "context_dve_step")
        s_ka = counted("act", "context_act_step")
        s_kp = counted("pool", "rotary_pool_step")
        s_kx = counted("pool", "keys_spread")
        s_qr = counted("pool", "queries_rotated_step")
        s_kqt = counted("pe", "keys_queries_turned")
        s_kqe = counted("act", "keys_queries_turned_in_sbuf")
        s_kb = counted("pool", "softmax_key_blocks_ready")
        s_vb = counted("pool", "value_blocks_ready")
        s_sc = counted("pe", "scores_ready")
        s_mx = counted("dve", "row_maxima_ready")
        s_sub = counted("dve", "shifted_scores_ready")
        s_exp = counted("act", "exponentials_ready")
        s_sum = counted("dve", "row_sums_step")
        s_pr = counted("dve", "probabilities_ready")
        s_pt = counted("pe", "probabilities_turned")
        s_pte = counted("act", "probabilities_turned_in_sbuf")
        s_pv = counted("pe", "softmax_outputs_ready")
        s_ove = counted("act", "softmax_outputs_in_sbuf")
        s_xp = counted("pe", "softmax_projected")
        s_xr2 = counted("dve", "second_residual_added")
        mv2s = work[:, 4460:4464].rearrange("p (u c) -> p u c", u=2)
        mv2_flat = stats[:, 0:2 * NT]
        s_mv2 = counted("dve", "second_layernorm_stats_kept")
        s_x2c = counted("dve", "second_layernorm_rows_kept")
        s_bn2 = counted("dve", "second_layernorm_stats_step")
        s_rqa = counted("act", "query_scale_act_step")
        s_rqd = counted("dve", "query_scale_ready")
        s_ln2a = counted("act", "second_layernorm_deviation_ready")
        s_ln2d = counted("dve", "second_layernorm_scale_ready")

        x2T3 = xT3
        wres = vsg
        wsh = work[:, 7768:7768 + SH * EW].rearrange("p (u c) -> p u c", u=SH)
        hbuf = arena[:, 0:2 * GT].rearrange("p (u c) -> p u c", u=2)
        ybf = arena[:, 1024:1024 + 2 * GT].rearrange("p (u c) -> p u c", u=2)
        x2s = arena[:, 2048:2048 + 2 * D].rearrange("p (u c) -> p u c", u=2)
        x2Ts = arena[:, 2560:2560 + 2 * D].rearrange("p (u k n) -> p u k n", u=2, k=KD)
        wab = sb("wab", KD * E)
        b2s = sb("b2s", D)

        def route(k):
            return arena[:, 3072 + k * NT * E:3072 + (k + 1) * NT * E].rearrange("p (n e) -> p n e", e=E)
        elog, aff, lower, pick, pick2, spare, chosen, cum, cum2, slot = (route(k) for k in range(10))
        elog_flat = arena[:, 3072:3072 + NT * E]
        best = arena[:, 5632:5632 + 8 * NT].rearrange("p (k n) -> p k n", k=8)
        w_flat = arena[:, 5632 + 5 * NT:5632 + 7 * NT]
        byexp = arena[:, 5760:5760 + 8 * E].rearrange("p (k e) -> p k e", k=8)
        comb_flat = arena[:, 5888:5888 + NT * NE]
        comb = comb_flat.rearrange("p (n e) -> p n e", e=NE)
        combs = arena[:, 6176:6176 + 2 * NE].rearrange("p (u e) -> p u e", u=2)
        combT = arena[:, 6212:6212 + 2 * P].rearrange("p (u n) -> p u n", u=2)
        by_tile = arena[:, 6468:6468 + NSLOT * E].rearrange("p (j e) -> p j e", e=E)
        expert_f = arena[:, 7236:7236 + NSLOT]
        bn3 = arena[:, 7284:7296].rearrange("p (u c) -> p u c", u=2)
        mv3 = arena[:, 7296:7300].rearrange("p (u c) -> p u c", u=2)
        sd3 = arena[:, 7300:7302].rearrange("p (u c) -> p u c", u=2)
        ri3 = arena[:, 7302:7304].rearrange("p (u c) -> p u c", u=2)
        ob = arena[:, 7304:7304 + 2 * D].rearrange("p (u c) -> p u c", u=2)
        slots_i = sb("slots_i", 2 * NT, U32)
        idxs = sb("idxs", 2 * 8, U32)
        expert_i = sb("expert_i", NSLOT, U32)
        W4 = 4
        xg = work[:, 0:W4 * D].rearrange("p (v c) -> p v c", v=W4)
        xgT = work[:, 1024:1024 + W4 * D].rearrange("p (v k n) -> p v k n", v=W4, k=KD)
        geb = work[:, 2048:2048 + W4 * F].rearrange("p (v c) -> p v c", v=W4)
        yhb = work[:, 2560:2560 + W4 * F].rearrange("p (v c) -> p v c", v=W4)
        yTb = work[:, 3072:3072 + W4 * F].rearrange("p (v c) -> p v c", v=W4)
        yob = work[:, 3584:3584 + W4 * D].rearrange("p (v c) -> p v c", v=W4)
        xst = work[:, 9304:9304 + 2 * 4 * D].rearrange("p (b c) -> p b c", b=2)
        got = vsg[:, 0:2 * 8 * D].rearrange("p (b k c) -> p b k c", b=2, k=8)
        s_zero_in = dma_sem("slots_cleared")
        s_brow = dma_sem("biases_in_then_parts_out_then_rows_in")
        s_wr = dma_sem("routed_weights_in")
        s_scat = [dma_sem(f"rows_scattered{b}") for b in range(2)]
        s_xg = [dma_sem(f"slot_rows_in{v}") for v in range(W4)]
        s_yout = [dma_sem(f"slot_rows_out{v}") for v in range(W4)]
        s_got = [dma_sem(f"expert_rows_in{b}") for b in range(2)]
        s_bs = counted("dve", "bias_parts_ready")
        s_mask = counted("dve", "chosen_experts_ready")
        s_pre = counted("pe", "prefix_counts_ready")
        s_comb = counted("dve", "combine_weights_ready")
        s_slots = counted("dve", "slots_ready")
        s_xst = counted("act", "rows_staged")
        s_ix = counted("pool", "slot_numbers_staged")
        s_xgt = counted("pe", "slot_rows_turned")
        s_xge = counted("act", "slot_rows_turned_in_sbuf")
        s_hh = counted("pe", "slot_hidden_ready")
        s_gg = counted("act", "slot_gate_ready")
        s_yh = counted("dve", "slot_product_ready")
        s_yt = counted("pe", "slot_product_turned")
        s_yte = counted("dve", "slot_product_turned_in_sbuf")
        s_yo = counted("pe", "slot_output_ready")
        s_yoe = counted("act", "slot_output_in_sbuf")
        s_f1 = counted("dve", "expert_rows_added")
        s_rw = dma_sem("router_weights_in")
        s_x2 = counted("dve", "second_layernorm_done")
        s_x2t = counted("pe", "tokens_turned")
        s_x2e = counted("act", "tokens_turned_in_sbuf")
        s_lg = counted("pe", "router_logits_ready")
        s_el = counted("act", "router_exponentials_ready")
        s_rt = counted("dve", "routing_step")
        s_cs = counted("pool", "combine_weights_staged")
        s_ct = counted("pe", "combine_weights_turned")
        s_cte = counted("act", "combine_weights_turned_in_sbuf")
        s_b2 = counted("pe", "output_bias_ready")
        s_acc0 = counted("dve", "outputs_started")
        s_h = counted("pe", "hidden_ready")
        s_ge = counted("act", "gate_branch_ready")
        s_yy = counted("dve", "hidden_product_ready")
        s_eo = counted("pe", "expert_output_ready")
        s_eot = counted("pe", "expert_output_tile_ready")
        s_ac = counted("dve", "expert_output_added")
        s_bn3 = counted("dve", "last_layernorm_stats_step")
        s_sd3 = counted("act", "last_layernorm_deviation_ready")
        s_ri3 = counted("dve", "last_layernorm_scale_ready")
        s_ob = counted("dve", "output_rows_ready")

        UIN = 3

        block = ctx.enter_context(nc.Block())

        @block.sync
        def _(sp):
            for v in range(W4):
                sp.sem_inc(s_yout[v], 16)
            for u in range(2):
                sp.sem_inc(s_out[u], 16)
                sp.sem_inc(s_sc_out[u], 16)
            sp.dma_start(consts[:], consts_d).then_inc(s_cst, 16)
            sp.dma_start(colp[:], col_d).then_inc(s_cst, 16)
            sp.dma_start(rowp[:], row_d.partition_broadcast(P)).then_inc(s_cst, 16)
            sp.dma_start(xT3[:, :, 0:GT], xt_d.rearrange("(k p) n -> p k n", k=KD)[:, :, 0:GT]).then_inc(s_xt[0], 16)
            sp.dma_start(wg3, wg_d.rearrange("(k p) c -> p k c", k=KD)).then_inc(s_wg, 16)
            sp.dma_start(wc3, wc_d.rearrange("(k p) c -> p k c", k=KD)).then_inc(s_wg, 16)
            for g in range(1, NG):
                sp.dma_start(xT3[:, :, g * GT:(g + 1) * GT],
                             xt_d.rearrange("(k p) n -> p k n", k=KD)[:, :, g * GT:(g + 1) * GT]).then_inc(s_xt[g], 16)
            sp.dma_start(wo3, wo_d.rearrange("(k p) c -> p k c", k=3)).then_inc(s_wo, 16)
            sp.dma_start(wout3, wout_d.rearrange("(k p) c -> p k c", k=KD)).then_inc(s_wo, 16)
            sp.dma_start(x3, x_d.rearrange("(n p) d -> p n d", p=P)).then_inc(s_xn, 16)
            sp.dma_start(ctxn[:].rearrange("p (n c) -> p n c", c=CKV),
                         ctx_d.rearrange("(n p) c -> p n c", p=P)).then_inc(s_xn, 16)
            sp.dma_start(bsp[:, 0:BPC], bias_d).then_inc(s_brow, 16)
            sp.wait_ge(s_bs, at(1))
            for j in range(NSLOT + 2):
                sp.dma_start(slots_dr[j * P:(j + 1) * P], zero[:]).then_inc(s_zero_in, 16)
            sp.wait_ge(s_bs, at(6))
            sp.dma_start(bias_dr.rearrange("k (p c) -> p k c", p=P), bsb[:].rearrange("p (k c) -> p k c", k=3)).then_inc(s_brow, 16)
            sp.wait_ge(s_brow, 32)
            sp.dma_start(brow[0:3, :], bias_dr).then_inc(s_brow, 16)
            with sp.Fori(0, NT // 2) as i:
                for u in range(2):
                    n = 2 * i + u
                    sp.wait_ge(s_rs, at(n + 1))
                    sp.dma_start(scores_dr[bass.ds(n, 1)].rearrange("n p c -> p (n c)"),
                                 rst[:, u].rearrange("p h t -> p (h t)")).then_inc(s_sc_out[u], 16)
                    sp.wait_ge(s_as, at(n + 1))
                    sp.dma_start(attend_dr[bass.ds(n, 1)].rearrange("n p c -> p (n c)"),
                                 ast[:, u].rearrange("p h t -> p (h t)")).then_inc(s_sc_out[u], 16)
            for u in range(2):
                sp.wait_ge(s_sc_out[u], 32 * (NT // 2) + 16)
            rows = scores_dr.rearrange("n (s r i) (f h q t) -> r f q (n s) h i t", s=2, r=2, f=2, h=HH, q=2)
            for r in range(2):
                for f in range(2):
                    p0 = 64 * r + 32 * f
                    for h in range(HH):
                        sp.dma_start(rb[p0:p0 + 32, h], rows[r, f, r, :, h]).then_inc(s_blk_in, 16)
            sp.wait_ge(s_invd, at(64))
            sp.wait_ge(s_invp, at(64))
            for r in range(2):
                for f in range(2):
                    p0 = 64 * r + 32 * f
                    sp.dma_start(inverse_dr[:, r, :, f, :], nb_flat[p0:p0 + 32].rearrange("p (i c) -> p i c", i=BL)
                                 ).then_inc(s_inv_out, 16)
            sp.wait_ge(s_inv_out, 16 * 4)
            with sp.Fori(0, NT // 2) as i:
                for u in range(2):
                    n = 2 * i + u
                    sp.wait_ge(s_o, at(n - 1))
                    sp.dma_start(at_s[:, u].rearrange("p h t -> p (h t)"),
                                 attend_dr[bass.ds(n, 1)].rearrange("n p c -> p (n c)")).then_inc(s_unit_in[u], 16)
                    sp.dma_start(roff[:, u], scores_dr[bass.ds(n, 1)].rearrange("n p (h q t) -> (n p) h q t", h=H, q=2)
                                 [:, :, 1]).then_inc(s_unit_in[u], 16)
                    sp.dma_start(n32[:, u].rearrange("p h t -> p (h t)"),
                                 inverse_dr[bass.ds(2 * n, 2)].rearrange("b r i f c -> (b r i) (f c)")
                                 ).then_inc(s_unit_in[u], 16)
            with sp.Fori(0, NT // 2) as i:
                for u in range(2):
                    n = 2 * i + u
                    sp.wait_ge(s_vb, at(n - 1))
                    sp.wait_ge(s_invp, at(64))
                    for z in range(2):
                        sp.dma_start(vdup[64 * z:64 * z + 64, u],
                                     ctx_d.rearrange("(n s k) c -> n k s c", s=2, k=T)[bass.ds(n, 1)]
                                     .rearrange("n k s c -> (n k) s c")).then_inc(s_vin[u], 16)
            sp.wait_ge(s_og, at(NT))
            sp.wait_ge(s_rsd, at(NT))
            for e in range(0, E, 4):
                sp.dma_start(wres[:, e * EW:(e + 4) * EW].rearrange("p (e c) -> p e c", e=4),
                             wexp_d[e:e + 4].rearrange("e p c -> p e c")).then_inc(s_wr, 16)
            sp.dma_start(wsh, wexp_d[E:NE].rearrange("e p c -> p e c")).then_inc(s_rw, 16)
            sp.dma_start(wab[:].rearrange("p (k e) -> p k e", k=KD),
                         wa_d.rearrange("(k p) e -> p k e", k=KD)).then_inc(s_rw, 16)
            sp.dma_start(b2s[0:NE, :], b2_d).then_inc(s_rw, 16)
            for b in range(2):
                sp.wait_ge(s_scat[b], 16 + 16 * NT)
            for v in range(W4):
                sp.dma_start(xg[:, v, :], slots_dr[v * P:(v + 1) * P]).then_inc(s_xg[v], 16)
            with sp.Fori(0, NSLOT // W4) as i:
                for v in range(W4):
                    j = W4 * i + v
                    sp.wait_ge(s_xgt, at(j + 1))
                    sp.dma_start(xg[:, v, :], slots_dr[bass.ds((j + W4) * P, P)]).then_inc(s_xg[v], 16)
                for v in range(W4):
                    j = W4 * i + v
                    sp.wait_ge(s_yoe, at(j + 1))
                    sp.dma_start(expert_dr[bass.ds(j * P, P)], yob[:, v, :]).then_inc(s_yout[v], 16)
            with sp.Fori(0, NT // 2) as i:
                for u in range(2):
                    n = 2 * i + u
                    sp.wait_ge(s_ob, at(n + 1))
                    sp.dma_start(out_d[bass.ds(n * P, P)], ob[:, u, :]).then_inc(s_out[u], 16)
            for u in range(2):
                sp.wait_ge(s_out[u], 16 * (NT // 2) + 16)
            for v in range(W4):
                sp.wait_ge(s_xg[v], 16 * (NSLOT // W4 + 1))

        @block.tensor
        def _(pe):
            start_counts(pe, "pe")
            pe.wait_ge(s_cst, 48)
            pe.wait_ge(s_wg, 32)
            for g in range(NG):
                pe.wait_ge(s_xt[g], 16)
            with pe.Fori(0, NG) as g:
                pe.wait_ge(s_xs, at(g + 1))
                alone(pe)
                for m in range(SPG):
                    pe.wait_ge(s_gev, at(SPG * g + m - 1))
                    alone(pe)
                    for k in range(KD):
                        mm = pe.matmul(ps[:, 4 + m % 2, 0:NGATE], xs[:, k, m * P:(m + 1) * P], wg3[:, k, :],
                                       start=(k == 0), stop=(k == KD - 1))
                    mm.then_inc(s_gmm, 1)

                def turn_values(j):
                    pe.wait_ge(s_silu, at(NCH * g + 5 + j))
                    alone(pe)
                    if j == 0:
                        pe.wait_ge(s_n2, at(g))
                        alone(pe)
                    else:
                        pe.wait_ge(s_vev, at(3 * g + j))
                        alone(pe)
                    for m in range(SPG):
                        mm = pe.transpose(ps[:, 6, m * P:(m + 1) * P], vs[:, j, m * P:(m + 1) * P], ident)
                    mm.then_inc(s_vtr, 1)

                for j in range(NCH):
                    pe.wait_ge(s_conv, at(bank_free(j, g)))
                    alone(pe)
                    for k in range(KD):
                        mm = pe.matmul(ps[0:ROWS[j], BANK[j], :], wc3[:, k, CH0[j]:CH0[j] + ROWS[j]],
                                       xT3[:, k, bass.ds(g * GT, GT)], start=(k == 0), stop=(k == KD - 1))
                    mm.then_inc(s_proj, 1)
                pe.wait_ge(s_ssev, at(g))
                alone(pe)
                for j in range(4):
                    pe.wait_ge(s_sq, at(4 * g + j + 1))
                    alone(pe)
                    mm = pe.matmul(ps[32 * j:32 * j + 32, 7, :], consts[0:KR, C_HSEL:C_HSEL + 32], sqs[0:KR, j, :],
                                   start=True, stop=True)
                mm.then_inc(s_ss, 1)
                for j in range(3):
                    turn_values(j)
                pe.wait_ge(s_ssev, at(g + 1))
                pe.wait_ge(s_vev, at(3 * g + 3))
                alone(pe)
                for m in range(SPG):
                    mm = pe.transpose(ps[:, 6, m * P:(m + 1) * P], ssb[:, m * P:(m + 1) * P], ident)
                mm.then_inc(s_sst, 1)
            pe.wait_ge(s_n2, at(NG))
            pe.wait_ge(s_gev, at(NT))
            pe.wait_ge(s_conv, at(NCH * NG))
            pe.wait_ge(s_idb, at(3))
            alone(pe)
            with pe.Fori(0, NT // 2) as i:
                for u in range(2):
                    n = 2 * i + u
                    pe.wait_ge(s_gst, at(n + 1))
                    pe.wait_ge(s_e, at(n - 1))
                    alone(pe)
                    pe.matmul(ps[:, u, 0:H * T], consts[:, C_LTRI:C_LTRI + P],
                              gst[:, u].rearrange("p h t -> p (h t)"), start=True, stop=False)
                    pe.matmul(ps[:, u, 0:H * T], idb[:], over(negb[:, 0:T], 1, H),
                              start=False, stop=True).then_inc(s_dmm, 1)
                    pe.wait_ge(s_kst, at(n + 1))
                    pe.wait_ge(s_kblk, at(n + 1))
                    pe.wait_ge(s_qblk, at(n + 1))
                    pe.wait_ge(s_as, at(n - 1))
                    alone(pe)
                    for f in range(2):
                        for s in range(2):
                            mm = pe.matmul(ps[64 * s:64 * s + 64, 2 + 2 * u + f, 0:2 * HH * T],
                                           kst[0:KR, u, f, 64 * s:64 * s + 64],
                                           blk[0:KR, u, f, :, :, 64 * s:64 * s + 64].rearrange("p q h n -> p (q h) n"),
                                           start=True, stop=True)
                    mm.then_inc(s_kmm, 1)
            pe.wait_ge(s_as, at(NT))
            pe.wait_ge(s_pw, at(1))
            pe.wait_ge(s_zero, at(3))
            alone(pe)
            def solve_blocks(i):
                for u in range(2):
                    n = 2 * i + u
                    pe.wait_ge(s_vp, at(n + 1))
                    pe.wait_ge(s_unit_in[u], 16 * UIN * (i + 1))
                    pe.wait_ge(s_xr, at(n - 3))
                    alone(pe)
                    for h in range(H):
                        for q in range(4):
                            r = slice(32 * q, 32 * q + 32)
                            mm = pe.matmul(ps[r, u, h * DV:(h + 1) * DV], n32[r, u, h, :], vp[r, u, h, :],
                                           start=True, stop=True)
                    mm.then_inc(s_w0, 1)

            def couple(i):
                for u in range(2):
                    n = 2 * i + u
                    pe.wait_ge(s_w, at(n + 1))
                    pe.wait_ge(s_y, at(n - 1))
                    alone(pe)
                    for h in range(H):
                        for s in range(2):
                            mm = pe.matmul(ps[64 * s + 32:64 * s + 64, 2 + u, h * DV:(h + 1) * DV],
                                           roff[64 * s:64 * s + 32, u, h, :],
                                           wsol[64 * s:64 * s + 32, u, h * DV:(h + 1) * DV], start=True, stop=True)
                    mm.then_inc(s_y0, 1)

            def correct(i):
                for u in range(2):
                    n = 2 * i + u
                    pe.wait_ge(s_y, at(n + 1))
                    pe.wait_ge(s_w2, at(n - 1))
                    alone(pe)
                    for h in range(H):
                        for s in range(2):
                            r = slice(64 * s + 32, 64 * s + 64)
                            mm = pe.matmul(ps[r, 4 + u, h * DV:(h + 1) * DV], n32[r, u, h, :],
                                           ysb[r, u, h * DV:(h + 1) * DV], start=True, stop=True)
                    mm.then_inc(s_z, 1)

            def attend(i):
                for u in range(2):
                    n = 2 * i + u
                    pe.wait_ge(s_w2, at(n + 1))
                    pe.wait_ge(s_ote, at(n - 1))
                    alone(pe)
                    for h in range(H):
                        for s in range(2):
                            r = slice(64 * s, 64 * s + 64)
                            mm = pe.matmul(ps[r, 6 + u, h * DV:(h + 1) * DV], at_s[r, u, h, :],
                                           wsol[r, u, h * DV:(h + 1) * DV], start=True, stop=True)
                    mm.then_inc(s_o, 1)

            def turn_heads(i):
                for u in range(2):
                    n = 2 * i + u
                    pe.wait_ge(s_og2, at(n + 1))
                    alone(pe)
                    for k in range(3):
                        mm = pe.transpose(ps[:, 6 + u, k * P:(k + 1) * P], og[:, u, k * P:(k + 1) * P], ident)
                    mm.then_inc(s_ot, 1)

            def project(i):
                for u in range(2):
                    n = 2 * i + u
                    pe.wait_ge(s_ote, at(n + 1))
                    alone(pe)
                    for k in range(3):
                        mm = pe.matmul(ps[:, u, 0:D], ogT[:, u, k, :], wo3[:, k, :], start=(k == 0), stop=(k == 2))
                    mm.then_inc(s_xo, 1)

            solve_blocks(0)
            couple(0)
            correct(0)
            attend(0)
            with pe.Fori(0, NT // 2 - 1) as i:
                solve_blocks(i + 1)
                couple(i + 1)
                turn_heads(i)
                correct(i + 1)
                project(i)
                attend(i + 1)
            turn_heads(NT // 2 - 1)
            project(NT // 2 - 1)
            pe.wait_ge(s_xr, at(NT))
            pe.wait_ge(s_og, at(NT))
            pe.wait_ge(s_rqd, at(1))
            alone(pe)
            def turn_keys_queries(i):
                for u in range(2):
                    n = 2 * i + u
                    pe.wait_ge(s_kx, at(n + 1))
                    pe.wait_ge(s_qr, at(3 * n + 3))
                    pe.wait_ge(s_xr2, at(n - 3))
                    alone(pe)
                    for w, src in enumerate((kx, qr)):
                        for f in range(2):
                            c = 2 * P * w + P * f
                            mm = pe.transpose(ps[:, u, c:c + P], src[:, u, f * P:(f + 1) * P], ident)
                    mm.then_inc(s_kqt, 1)

            def score(i):
                for u in range(2):
                    n = 2 * i + u
                    pe.wait_ge(s_kqe, at(n + 1))
                    pe.wait_ge(s_kb, at(n + 1))
                    alone(pe)
                    for f in range(2):
                        pe.wait_ge(s_sub, at(2 * (n - 2) + f + 1))
                        alone(pe)
                        bank = 2 + 2 * u + f
                        pe.matmul(ps[:, bank, :], idb[:], over(causb, 1, 8), start=True, stop=False)
                        for s in range(2):
                            q = slice(64 * s, 64 * s + 64)
                            mm = pe.matmul(ps[q, bank, :], kqT[:, u, 1, f, q], kblk[:, u, f, :, q],
                                           start=False, stop=True)
                        mm.then_inc(s_sc, 1)

            def turn_probabilities(i):
                for u in range(2):
                    n = 2 * i + u
                    for f in range(2):
                        pe.wait_ge(s_pr, at(2 * n + f + 1))
                        pe.wait_ge(s_pte, at(2 * n + f - 1))
                        alone(pe)
                        for c in range(4):
                            mm = pe.transpose(ps[:, 6 + f, c * P:(c + 1) * P],
                                              prob[:, u, f, 2 * c:2 * c + 2, :].rearrange("p h k -> p (h k)"), ident)
                        mm.then_inc(s_pt, 1)

            def attend_softmax(i):
                for u in range(2):
                    n = 2 * i + u
                    pe.wait_ge(s_vb, at(n + 1))
                    alone(pe)
                    for f in range(2):
                        pe.wait_ge(s_pte, at(2 * n + f + 1))
                        alone(pe)
                        for s in range(2):
                            for c in range(4):
                                q = slice(c * P + 64 * s, c * P + 64 * s + 64)
                                mm = pe.matmul(ps[32 * c:32 * c + 32, u, f * P + 64 * s:f * P + 64 * s + 64],
                                               vblk[:, u, s, 2 * f + c // 2, :], probT[:, u, f, q], start=True, stop=True)
                    mm.then_inc(s_pv, 1)

            def project_softmax(i):
                for u in range(2):
                    n = 2 * i + u
                    pe.wait_ge(s_ove, at(n + 1))
                    alone(pe)
                    for k in range(KD):
                        mm = pe.matmul(ps[:, u, D:2 * D], oT[:, u, k, :], wout3[:, k, :], start=(k == 0), stop=(k == KD - 1))
                    mm.then_inc(s_xp, 1)

            turn_keys_queries(0)
            score(0)
            turn_keys_queries(1)
            with pe.Fori(0, NT // 2 - 2) as i:
                score(i + 1)
                turn_probabilities(i)
                attend_softmax(i)
                project_softmax(i)
                turn_keys_queries(i + 2)
            score(NT // 2 - 1)
            turn_probabilities(NT // 2 - 2)
            attend_softmax(NT // 2 - 2)
            project_softmax(NT // 2 - 2)
            turn_probabilities(NT // 2 - 1)
            attend_softmax(NT // 2 - 1)
            project_softmax(NT // 2 - 1)
            pe.wait_ge(s_rw, 48)
            with pe.Fori(0, NT // 2) as i:
                for u in range(2):
                    n = 2 * i + u
                    pe.wait_ge(s_x2, at(n + 1))
                    pe.wait_ge(s_xr2, at(NT))
                    pe.wait_ge(s_x2e, at(n - 1))
                    alone(pe)
                    for k in range(KD):
                        mm = pe.transpose(ps[:, u, k * P:(k + 1) * P], x2s[:, u, k * P:(k + 1) * P], ident)
                    mm.then_inc(s_x2t, 1)
                for u in range(2):
                    n = 2 * i + u
                    pe.wait_ge(s_x2e, at(n + 1))
                    pe.wait_ge(s_el, at(n - 1))
                    alone(pe)
                    for k in range(KD):
                        mm = pe.matmul(ps[:, 2 + u, 0:E], x2Ts[:, u, k, :], wab[:, k * E:(k + 1) * E],
                                       start=(k == 0), stop=(k == KD - 1))
                    mm.then_inc(s_lg, 1)
            pe.wait_ge(s_mask, at(1))
            pe.matmul(ps[:, 6, 0:NT * E], consts[:, C_PRE:C_PRE + P], chosen.rearrange("p n e -> p (n e)"),
                      start=True, stop=True)
            pe.matmul(ps[:, 7, 0:NT * E], consts[:, C_ONE:C_ONE + P], chosen.rearrange("p n e -> p (n e)"),
                      start=True, stop=True).then_inc(s_pre, 1)
            with pe.Fori(0, NT // 2) as i:
                for u in range(2):
                    n = 2 * i + u
                    pe.wait_ge(s_cs, at(n + 1))
                    pe.wait_ge(s_cte, at(n - 1))
                    alone(pe)
                    pe.transpose(ps[0:NE, u, 0:P], combs[:, u, :], ident).then_inc(s_ct, 1)
                for u in range(2):
                    n = 2 * i + u
                    pe.wait_ge(s_cte, at(n + 1))
                    pe.wait_ge(s_acc0, at(n - 1))
                    alone(pe)
                    pe.matmul(ps[:, 2 + u, 0:D], combT[0:NE, u, :], b2s[0:NE, :], start=True, stop=True).then_inc(s_b2, 1)
            pe.wait_ge(s_acc0, at(NT))

            def shared_expert(u):
                for g in range(NG + 1):
                    m = NG * u + g
                    if g < NG:
                        if m >= 2:
                            pe.wait_ge(s_yy, at(m - 1))
                        for w in range(2):
                            for c in range(KD):
                                o = w * KD * F + c * F
                                mm = pe.matmul(ps[:, 2 * w + g % 2, :], wsh[:, u, o:o + F], x2T3[:, c, g * GT:(g + 1) * GT],
                                               start=(c == 0), stop=(c == KD - 1))
                        mm.then_inc(s_h, 1)
                    if g > 0:
                        m = NG * u + g - 1
                        pe.wait_ge(s_yy, at(m + 1))
                        for t in range(SPG):
                            if m > 0:
                                pe.wait_ge(s_ac, at(SPG * (m - 1) + t + 1))
                            mm = pe.matmul(ps[:, 4 + t, 0:D], ybf[:, (g - 1) % 2, t * P:(t + 1) * P],
                                           wsh[:, u, 2 * KD * F:EW], start=True, stop=True)
                            if t < SPG - 1:
                                mm.then_inc(s_eot, 1)
                        mm.then_inc(s_eo, 1)

            shared_expert(0)
            pe.wait_ge(s_ac, at(NT))
            pe.wait_ge(s_yy, at(NG))
            pe.wait_ge(s_wr, 64)
            pe.wait_ge(s_brow, 48)
            pe.wait_ge(s_slots, at(1))
            with pe.Fori(0, NSLOT // W4) as i:
                for v in range(W4):
                    j = W4 * i + v
                    pe.wait_ge(s_xg[v], 16 * (i + 1))
                    pe.wait_ge(s_yte, at(j - W4 + 1))
                    alone(pe)
                    for k in range(KD):
                        mm = pe.transpose(ps[:, 2 * v, k * P:(k + 1) * P], xg[:, v, k * P:(k + 1) * P], ident)
                    mm.then_inc(s_xgt, 1)
                which = []
                for v in range(W4):
                    j = W4 * i + v
                    e = pe.value_load(expert_i[0:1, bass.ds(j, 1)], min_val=0, max_val=E - 1)
                    which.append(e)
                    pe.wait_ge(s_xge, at(j + 1))
                    pe.wait_ge(s_yoe, at(j - W4 + 1))
                    alone(pe)
                    h = ps[:, 2 * v + 1, 0:2 * F]
                    pe.matmul(h, onesb[0:3, :], brow[0:3, bass.ds(e * (2 * F), 2 * F)], start=True, stop=False)
                    for k in range(KD):
                        mm = pe.matmul(h, xgT[:, v, k, :],
                                       wres[:, bass.ds(e * EW + k * 2 * F, 2 * F)], start=False, stop=(k == KD - 1))
                    mm.then_inc(s_hh, 1)
                for v in range(W4):
                    j = W4 * i + v
                    pe.wait_ge(s_yh, at(j + 1))
                    alone(pe)
                    pe.transpose(ps[:, 2 * v, 2 * P:3 * P], yhb[:, v, :], ident).then_inc(s_yt, 1)
                for v in range(W4):
                    j = W4 * i + v
                    pe.wait_ge(s_yte, at(j + 1))
                    alone(pe)
                    pe.matmul(ps[:, 2 * v + 1, D:2 * D], yTb[:, v, :], wres[:, bass.ds(which[v] * EW + 2 * KD * F, D)],
                              start=True, stop=True).then_inc(s_yo, 1)
            pe.wait_ge(s_yoe, at(NSLOT))
            shared_expert(1)

        @block.scalar
        def _(act):
            start_counts(act, "act")
            act.wait_ge(s_cst, 48)
            with act.Fori(0, NG) as g:
                def first_tap(j):
                    act.wait_ge(s_proj, at(NCH * g + j + 1))
                    act.wait_ge(s_silu, at(bank_free(j, g)))
                    act.activation(ybuf[0:ROWS[j], BANK[j], :], ps[0:ROWS[j], BANK[j], :], ACT.Copy,
                                   scale=taps[0:ROWS[j], j, KSZ - 1:KSZ]).then_inc(s_tap0, 1)

                def silu(j):
                    act.wait_ge(s_conv, at(NCH * g + j + 1))
                    if j < 4:
                        dst = arena[0:KR, bass.ds(g * GT + j * NTOK, GT)]
                    else:
                        dst = vs[:, j - 4, :]
                        act.wait_ge(s_vtr, at(3 * (g - 1) + j - 3))
                    act.activation(dst, ybuf[0:ROWS[j], BANK[j], :], ACT.Silu).then_inc(s_silu, 1)

                for m in range(SPG):
                    n = SPG * g + m
                    act.wait_ge(s_gmm, at(n + 1))
                    act.activation(sg[:, bass.ds(n * HV, HV)], ps[:, 4 + m % 2, 0:HV], ACT.Silu)
                    act.activation(ab[:, bass.ds(n * 2 * H, 2 * H)], ps[:, 4 + m % 2, HV:NGATE],
                                   ACT.Copy).then_inc(s_gev, 1)
                first_tap(0)
                for j in range(1, NCH):
                    first_tap(j)
                    silu(j - 1)
                silu(NCH - 1)
                act.wait_ge(s_ss, at(g + 1))
                act.wait_ge(s_sst, at(g))
                act.activation(ssb, ps[:, 7, :], ACT.Copy).then_inc(s_ssev, 1)
                for j in range(3):
                    act.wait_ge(s_vtr, at(3 * g + j + 1))
                    act.activation(
                        vt[:, bass.ds(SPG * HV * g, SPG * HV)].rearrange("p (m c) -> p m c", m=SPG)[:, :, j * P:(j + 1) * P],
                        ps[:, 6, :].rearrange("p (m c) -> p m c", m=SPG), ACT.Copy).then_inc(s_vev, 1)

            a_t, b_t = tab(T_A), tab(T_B)
            act.wait_ge(s_gd, at(2))
            act.activation(a_t, a_t, ACT.Exp, scale=-1.0).then_inc(s_gk, 1)
            act.activation(b_t, ab3[:, :, H:2 * H], ACT.Exp, scale=-1.0).then_inc(s_gk, 1)
            act.activation(rowp[:, R_ALOG:R_ALOG + H], rowp[:, R_ALOG:R_ALOG + H], ACT.Exp).then_inc(s_gk, 1)
            act.wait_ge(s_gk, at(1))
            act.activation(a_t, a_t, ACT.Ln, bias=1.0).then_inc(s_gk, 1)
            act.wait_ge(s_gd, at(5))
            act.activation(tab(T_NK).rearrange("p (n h) -> p n h", h=H), n23[:, :, H:2 * H],
                           ACT.Sqrt).then_inc(s_gk, 1)
            act.activation(tab(T_RQ).rearrange("p (n h) -> p n h", h=H), n23[:, :, 0:H],
                           ACT.Sqrt, scale=float(DK)).then_inc(s_gk, 1)
            with act.Fori(0, NT // 2) as i:
                for u in range(2):
                    n = 2 * i + u
                    act.wait_ge(s_kmm, at(n - 1))
                    for f in range(2):
                        ins = act.activation(kst[0:KR, u, f, :], arena[0:KR, bass.ds(n * P + (2 + f) * NTOK, P)], ACT.Copy)
                    ins.then_inc(s_kst, 1)
                    act.wait_ge(s_dmm, at(n + 1))
                    act.wait_ge(s_as, at(n - 1))
                    act.activation(est[:, u].rearrange("p h t -> p (h t)"), ps[:, u, 0:H * T], ACT.Exp).then_inc(s_e, 1)
            act.wait_ge(s_zero, at(2))
            act.wait_ge(s_kd, at(2))
            act.activation(rk, rk, ACT.Sqrt, bias=eps, scale=1.0 / CKV).then_inc(s_ka, 1)
            act.wait_ge(s_zero, at(3))
            def keep_solves(i):
                for u in range(2):
                    n = 2 * i + u
                    act.wait_ge(s_w0, at(n + 1))
                    act.wait_ge(s_o, at(n - 1))
                    act.activation(wsol[:, u, :], ps[:, u, 0:HV], ACT.Copy).then_inc(s_w, 1)

            def keep_coupling(i):
                for u in range(2):
                    n = 2 * i + u
                    act.wait_ge(s_y0, at(n + 1))
                    act.wait_ge(s_z, at(n - 1))
                    act.activation(ysb[:, u, :], ps[:, 2 + u, 0:HV], ACT.Copy).then_inc(s_y, 1)

            def head_roots(i):
                for u in range(2):
                    n = 2 * i + u
                    act.wait_ge(s_ms, at(n + 1))
                    act.activation(ms[:, u, :], ms[:, u, :], ACT.Sqrt, bias=eps, scale=1.0 / DV).then_inc(s_rms, 1)

            def keep_heads(i):
                for u in range(2):
                    n = 2 * i + u
                    act.wait_ge(s_ot, at(n + 1))
                    act.wait_ge(s_xo, at(n - 1))
                    act.activation(ogT[:, u].rearrange("p k n -> p (k n)"), ps[:, 6 + u, 0:3 * P], ACT.Copy).then_inc(s_ote, 1)

            def deviations(i):
                for u in range(2):
                    n = 2 * i + u
                    act.wait_ge(s_bn, at(2 * n + 2))
                    act.activation(sd[:, u, :], mv[:, u, 1:2], ACT.Sqrt, bias=eps).then_inc(s_sd, 1)

            keep_solves(0)
            keep_coupling(0)
            head_roots(0)
            with act.Fori(0, NT // 2 - 1) as i:
                keep_solves(i + 1)
                keep_coupling(i + 1)
                keep_heads(i)
                deviations(i)
                head_roots(i + 1)
            keep_heads(NT // 2 - 1)
            deviations(NT // 2 - 1)
            act.wait_ge(s_x1, at(NT))
            act.wait_ge(s_rq, at(NT))
            act.activation(rq_tab, rq_tab, ACT.Sqrt, bias=eps16, scale=float(HD)).then_inc(s_rqa, 1)
            def keep_keys_queries(i):
                for u in range(2):
                    n = 2 * i + u
                    act.wait_ge(s_kqt, at(n + 1))
                    act.wait_ge(s_kb, at(n - 1))
                    act.wait_ge(s_sc, at(2 * (n - 1)))
                    act.activation(kqT[:, u].rearrange("p w f n -> p (w f n)"), ps[:, u, :], ACT.Copy).then_inc(s_kqe, 1)

            def exponentials(i):
                for u in range(2):
                    n = 2 * i + u
                    for f in range(2):
                        act.wait_ge(s_sub, at(2 * n + f + 1))
                        alone(act)
                        act.activation(prob[:, u, f], prob[:, u, f], ACT.Exp,
                                       scale=rq_tab[:, bass.ds(n, 1)]).then_inc(s_exp, 1)

            def keep_probabilities(i):
                for u in range(2):
                    n = 2 * i + u
                    for f in range(2):
                        act.wait_ge(s_pt, at(2 * n + f + 1))
                        act.wait_ge(s_pv, at(n - 1))
                        act.activation(probT[:, u, f, :], ps[:, 6 + f, :], ACT.Copy).then_inc(s_pte, 1)

            def keep_attended(i):
                for u in range(2):
                    n = 2 * i + u
                    act.wait_ge(s_pv, at(n + 1))
                    act.wait_ge(s_xp, at(n - 1))
                    act.activation(oT[:, u].rearrange("p f n -> p (f n)"), ps[:, u, 0:D], ACT.Copy).then_inc(s_ove, 1)

            keep_keys_queries(0)
            exponentials(0)
            keep_keys_queries(1)
            with act.Fori(0, NT // 2 - 2) as i:
                keep_probabilities(i)
                exponentials(i + 1)
                keep_attended(i)
                keep_keys_queries(i + 2)
            keep_probabilities(NT // 2 - 2)
            exponentials(NT // 2 - 1)
            keep_attended(NT // 2 - 2)
            keep_probabilities(NT // 2 - 1)
            keep_attended(NT // 2 - 1)
            act.wait_ge(s_mv2, at(NT))
            act.activation(sd2, mv2[:, :, 1], ACT.Sqrt, bias=eps).then_inc(s_ln2a, 1)
            with act.Fori(0, NT // 2) as i:
                for u in range(2):
                    n = 2 * i + u
                    act.wait_ge(s_x2t, at(n + 1))
                    act.wait_ge(s_lg, at(n - 1))
                    src = ps[:, u, 0:D].rearrange("p (k n) -> p k n", k=KD)
                    act.activation(x2Ts[:, u], src, ACT.Copy)
                    act.activation(x2T3[:, :, bass.ds(n * P, P)], src, ACT.Copy).then_inc(s_x2e, 1)
                for u in range(2):
                    n = 2 * i + u
                    act.wait_ge(s_lg, at(n + 1))
                    alone(act)
                    act.activation(elog_flat[:, bass.ds(n * E, E)], ps[:, 2 + u, 0:E], ACT.Exp, scale=-1.0).then_inc(s_el, 1)
            act.wait_ge(s_x2c, at(NT))
            with act.Fori(0, NT // 8) as i:
                for b in range(2):
                    act.wait_ge(s_scat[b], 128 * i + 16)
                    alone(act)
                    act.activation(xst[:, b, :], xn[:, bass.ds((2 * i + b) * 4 * D, 4 * D)], ACT.Copy).then_inc(s_xst, 1)
            with act.Fori(0, NT // 2) as i:
                for u in range(2):
                    n = 2 * i + u
                    act.wait_ge(s_ct, at(n + 1))
                    act.wait_ge(s_b2, at(n - 1))
                    act.activation(combT[0:NE, u, :], ps[0:NE, u, 0:P], ACT.Copy).then_inc(s_cte, 1)

            def shared_expert(u):
                for g in range(NG):
                    m = NG * u + g
                    act.wait_ge(s_h, at(m + 1))
                    if m >= 2:
                        act.wait_ge(s_yy, at(m - 1))
                    act.activation(hbuf[:, g % 2, :], ps[:, g % 2, :], ACT.Gelu,
                                   bias=colp[:, E + u + W_GB:E + u + W_GB + 1]).then_inc(s_ge, 1)

            shared_expert(0)
            with act.Fori(0, NSLOT // W4) as i:
                for v in range(W4):
                    j = W4 * i + v
                    act.wait_ge(s_xgt, at(j + 1))
                    act.wait_ge(s_hh, at(j - W4 + 1))
                    act.activation(xgT[:, v].rearrange("p k n -> p (k n)"), ps[:, 2 * v, 0:D], ACT.Copy).then_inc(s_xge, 1)
                for v in range(W4):
                    j = W4 * i + v
                    act.wait_ge(s_hh, at(j + 1))
                    act.wait_ge(s_yh, at(j - W4 + 1))
                    act.activation(geb[:, v, :], ps[:, 2 * v + 1, 0:F], ACT.Gelu).then_inc(s_gg, 1)
                for v in range(W4):
                    j = W4 * i + v
                    act.wait_ge(s_yo, at(j + 1))
                    act.wait_ge(s_yout[v], 16 * i + 16)
                    act.activation(yob[:, v, :], ps[:, 2 * v + 1, D:2 * D], ACT.Copy).then_inc(s_yoe, 1)
            shared_expert(1)
            with act.Fori(0, NT // 2) as i:
                for u in range(2):
                    n = 2 * i + u
                    act.wait_ge(s_bn3, at(2 * n + 2))
                    act.wait_ge(s_ri3, at(n - 1))
                    act.activation(sd3[:, u, :], mv3[:, u, 1:2], ACT.Sqrt, bias=eps).then_inc(s_sd3, 1)

        @block.vector
        def _(dve):
            start_counts(dve, "dve")
            dve.wait_ge(s_cst, 48)
            dve.memset(zero[:], 0.0).then_inc(s_bs, 1)
            dve.memset(onesb[:], 1.0).then_inc(s_idb, 1)
            dve.tensor_copy(idb[:], ident).then_inc(s_idb, 1)
            dve.tensor_copy(negb[:], consts[:, C_NEG:C_NEG + 2 * T]).then_inc(s_idb, 1)
            dve.wait_ge(s_brow, 16)
            for k in range(3):
                if k > 0:
                    dve.wait_ge(s_bs, at(2 * k))
                    dve.tensor_tensor(bsp[:, k * BPC:(k + 1) * BPC], bsp[:, (k - 1) * BPC:k * BPC],
                                      bsb[:, (k - 1) * BPC:k * BPC], ALU.subtract).then_inc(s_bs, 1)
                    dve.wait_ge(s_bs, at(2 * k + 1))
                dve.tensor_copy(bsb[:, k * BPC:(k + 1) * BPC], bsp[:, k * BPC:(k + 1) * BPC]).then_inc(s_bs, 1)
            with dve.Fori(0, NG) as g:
                for j in range(NCH):
                    m = NCH * g + j
                    r = ROWS[j]
                    y = ybuf[0:r, BANK[j], :].rearrange("p (s t) -> p s t", t=T)
                    z = ps[0:r, BANK[j], :].rearrange("p (s t) -> p s t", t=T)
                    dve.wait_ge(s_tap0, at(m + 1))
                    for d in range(1, KSZ):
                        if d > 1:
                            dve.wait_ge(s_tap, at(2 * m + d - 1))
                        dve.scalar_tensor_tensor(y[:, :, d:T], z[:, :, 0:T - d], taps[0:r, j, KSZ - 1 - d:KSZ - d],
                                                 y[:, :, d:T], ALU.mult, ALU.add
                                                 ).then_inc(s_tap if d < KSZ - 1 else s_conv, 1)
                dve.wait_ge(s_sst, at(g + 1))
                for f in range(2):
                    ins = dve.tensor_copy(
                        n2[:, bass.ds(SPG * 2 * H * g, SPG * 2 * H)].rearrange(
                            "p (m q f h) -> p m q f h", m=SPG, q=2, f=2)[:, :, :, f, :],
                        ps[:, 6, :].rearrange("p (m q f c) -> p m q f c", m=SPG, q=2, f=2)[:, :, :, f, 0:HH])
                ins.then_inc(s_n2, 1)
            a_t = tab(T_A).rearrange("p (n h) -> p n h", h=H)
            g_t = tab(T_G).rearrange("p (n h) -> p n h", h=H)
            c_t, b_t = tab(T_C), tab(T_B)
            dve.wait_ge(s_gev, at(NT))
            dve.tensor_tensor(g_t, ab3[:, :, 0:H], over(rowp[:, R_DT:R_DT + H], 1, NT), ALU.add).then_inc(s_gd, 1)
            dve.wait_ge(s_gd, at(1))
            dve.scalar_tensor_tensor(a_t, g_t, -1.0, g_t, ALU.mult, ALU.max).then_inc(s_gd, 1)
            dve.wait_ge(s_gd, at(2))
            dve.tensor_scalar(g_t, g_t, 0.0, None, ALU.max).then_inc(s_gd, 1)
            dve.wait_ge(s_n2, at(NG))
            dve.tensor_scalar(n2[:], n2[:], 1e-6, None, ALU.add).then_inc(s_gd, 1)
            dve.wait_ge(s_gd, at(4))
            dve.tensor_copy(c_t.rearrange("p (n h) -> p n h", h=H), n23[:, :, H:2 * H]).then_inc(s_gd, 1)
            dve.wait_ge(s_gk, at(4))
            dve.tensor_tensor(g_t, g_t, a_t, ALU.add).then_inc(s_gd, 1)
            dve.wait_ge(s_gd, at(6))
            dve.scalar_tensor_tensor(g_t, g_t, -1.0, over(rowp[:, R_ALOG:R_ALOG + H], 1, NT),
                                     ALU.mult, ALU.mult).then_inc(s_gd, 1)
            dve.scalar_tensor_tensor(c_t, b_t, 1.0, c_t, ALU.add, ALU.mult).then_inc(s_gd, 1)
            dve.wait_ge(s_gd, at(8))
            dve.reciprocal(c_t, c_t).then_inc(s_gd, 1)
            dve.wait_ge(s_gk, at(6))
            dve.reciprocal(tab(T_RQ), tab(T_RQ)).then_inc(s_gd, 1)
            dve.wait_ge(s_gd, at(9))
            with dve.Fori(0, NT // 2) as i:
                for u in range(2):
                    n = 2 * i + u
                    dve.wait_ge(s_kmm, at(n - 1))
                    for f in range(2):
                        ins = dve.tensor_tensor(blk[0:KR, u, f, 1], over(arena[0:KR, bass.ds(n * P + f * NTOK, P)], 1, HH),
                                                over(consts[0:KR, C_HM:C_HM + HH], 2, P), ALU.mult)
                    ins.then_inc(s_qblk, 1)
                    dve.wait_ge(s_e, at(n + 1))
                    dve.tensor_tensor(est[:, u], est[:, u], over(small[:, bass.ds(n * H + T_C * NT * H, H)], 2, T),
                                      ALU.mult).then_inc(s_ec, 1)
                    dve.wait_ge(s_ec, at(n + 1))
                    dve.wait_ge(s_kmm, at(n + 1))
                    prod = ps[:, 2 + 2 * u:4 + 2 * u, 0:2 * HH * T].rearrange("p f (q c) -> p f q c", q=2)
                    e2 = est[:, u].rearrange("p (f h) t -> p f (h t)", f=2)
                    dve.wait_ge(s_sc_out[u], 32 * i + 16)
                    dve.tensor_tensor(rst[:, u].rearrange("p (f h) t -> p f (h t)", f=2), prod[:, :, 0], e2,
                                      ALU.mult).then_inc(s_rs, 1)
                    dve.tensor_tensor(ast[:, u].rearrange("p (f h) t -> p f (h t)", f=2), prod[:, :, 1], e2,
                                      ALU.mult).then_inc(s_as, 1)
            dve.wait_ge(s_xn, 32)
            dve.memset(eps, 1e-5).then_inc(s_zero, 1)
            dve.memset(eps16, HD * 1e-5).then_inc(s_zero, 1)
            dve.tensor_tensor(ksq, ctxn[:], ctxn[:], ALU.mult).then_inc(s_kd, 1)
            dve.wait_ge(s_kd, at(1))
            dve.tensor_reduce(rk, ksq.rearrange("p (n c) -> p n c", c=CKV), AXX, ALU.add).then_inc(s_kd, 1)
            dve.wait_ge(s_ka, at(1))
            dve.reciprocal(rk, rk).then_inc(s_kd, 1)
            dve.wait_ge(s_kd, at(3))
            dve.tensor_tensor(ctx3, ctx3, over(rk, 2, CKV), ALU.mult).then_inc(s_kd, 1)
            dve.wait_ge(s_blk_in, 16 * 12)
            invert(dve, s_invd, 0, 2, tmp_d)
            dve.wait_ge(s_as, at(NT))
            dve.memset(ps[:, 4:6, :], 0.0).then_inc(s_zero, 1)
            dve.wait_ge(s_xn, 32)
            def finish_solution(i):
                for u in range(2):
                    n = 2 * i + u
                    dve.wait_ge(s_z, at(n + 1))
                    dve.tensor_tensor(wsol[:, u, :], wsol[:, u, :], ps[:, 4 + u, 0:HV], ALU.subtract).then_inc(s_w2, 1)

            def gate_values(i):
                for u in range(2):
                    n = 2 * i + u
                    dve.wait_ge(s_o, at(n + 1))
                    dve.wait_ge(s_sgr, at(n + 1))
                    dve.wait_ge(s_ot, at(n - 1))
                    dve.tensor_tensor(og[:, u, :], ps[:, 6 + u, 0:HV], sgr[:, u, :], ALU.mult).then_inc(s_og, 1)

            def head_squares(i):
                for u in range(2):
                    n = 2 * i + u
                    dve.wait_ge(s_osq, at(n + 1))
                    dve.wait_ge(s_rr, at(n - 1))
                    dve.tensor_reduce(ms[:, u, :], osq[:, u, :].rearrange("p (h t) -> p h t", h=H), AXX,
                                      ALU.add).then_inc(s_ms, 1)

            def head_scales(i):
                for u in range(2):
                    n = 2 * i + u
                    dve.wait_ge(s_rms, at(n + 1))
                    dve.wait_ge(s_og2, at(n - 1))
                    dve.reciprocal(rs[:, u, :], ms[:, u, :]).then_inc(s_rr, 1)

            def add_residual(i):
                for u in range(2):
                    n = 2 * i + u
                    dve.wait_ge(s_xo, at(n + 1))
                    dve.wait_ge(s_x1, at(n - 1))
                    dve.tensor_tensor(xr[:, u, :], ps[:, u, 0:D], xn[:, bass.ds(n * D, D)], ALU.add).then_inc(s_xr, 1)

            def row_moments(i):
                for u in range(2):
                    n = 2 * i + u
                    dve.wait_ge(s_xr, at(n + 1))
                    dve.wait_ge(s_sd, at(n - 1))
                    dve.bn_stats(bn[:, u, :], xr[:, u, :]).then_inc(s_bn, 1)
                    dve.wait_ge(s_bn, at(2 * n + 1))
                    alone(dve)
                    dve.bn_aggr(mv[:, u, :], bn[:, u, :]).then_inc(s_bn, 1)

            def norm_rows(i):
                for u in range(2):
                    n = 2 * i + u
                    dve.wait_ge(s_sd, at(n + 1))
                    dve.reciprocal(rsd[:, u, :], sd[:, u, :]).then_inc(s_rsd, 1)
                    dve.wait_ge(s_rsd, at(n + 1))
                    dve.tensor_scalar(xn[:, bass.ds(n * D, D)], xr[:, u, :], mv[:, u, 0:1], rsd[:, u, :],
                                      ALU.subtract, ALU.mult).then_inc(s_x1, 1)
                    dve.scalar_tensor_tensor(rq_tab[:, bass.ds(n, 1)], mv[:, u, 1:2], rsd[:, u, :], rsd[:, u, :],
                                             ALU.mult, ALU.mult).then_inc(s_rq, 1)

            finish_solution(0)
            gate_values(0)
            head_squares(0)
            head_scales(0)
            with dve.Fori(0, NT // 2 - 1) as i:
                finish_solution(i + 1)
                add_residual(i)
                row_moments(i)
                gate_values(i + 1)
                norm_rows(i)
                head_squares(i + 1)
                head_scales(i + 1)
            add_residual(NT // 2 - 1)
            row_moments(NT // 2 - 1)
            norm_rows(NT // 2 - 1)
            dve.wait_ge(s_rqa, at(1))
            dve.reciprocal(rq_tab, rq_tab).then_inc(s_rqd, 1)
            def shift_scores(i):
                for u in range(2):
                    n = 2 * i + u
                    for f in range(2):
                        sc = ps[:, 2 + 2 * u + f, :].rearrange("p (h k) -> p h k", h=8)
                        dve.wait_ge(s_sc, at(2 * n + f + 1))
                        dve.tensor_reduce(mxs[:, u, f], sc, AXX, ALU.max).then_inc(s_mx, 1)
                        dve.wait_ge(s_mx, at(2 * n + f + 1))
                        dve.wait_ge(s_pt, at(2 * (n - 2) + f + 1))
                        dve.tensor_tensor(prob[:, u, f], sc, over(mxs[:, u, f], 2, T), ALU.subtract).then_inc(s_sub, 1)

            def normalise(i):
                for u in range(2):
                    n = 2 * i + u
                    for f in range(2):
                        m = 2 * n + f
                        dve.wait_ge(s_exp, at(m + 1))
                        dve.tensor_reduce(sms[:, u, f], prob[:, u, f], AXX, ALU.add).then_inc(s_sum, 1)
                        dve.wait_ge(s_sum, at(2 * m + 1))
                        dve.reciprocal(sri[:, u, f], sms[:, u, f]).then_inc(s_sum, 1)
                        dve.wait_ge(s_sum, at(2 * m + 2))
                        dve.tensor_tensor(prob[:, u, f], prob[:, u, f], over(sri[:, u, f], 2, T),
                                          ALU.mult).then_inc(s_pr, 1)

            def add_softmax(i):
                for u in range(2):
                    n = 2 * i + u
                    dve.wait_ge(s_xp, at(n + 1))
                    dve.wait_ge(s_qr, at(3 * n + 3))
                    row = xn[:, bass.ds(n * D, D)]
                    dve.tensor_tensor(row, ps[:, u, D:2 * D], row, ALU.add).then_inc(s_xr2, 1)
                    dve.wait_ge(s_xr2, at(n + 1))
                    alone(dve)
                    dve.bn_stats(bn2[:, u, :], row).then_inc(s_bn2, 1)
                    dve.wait_ge(s_bn2, at(2 * n + 1))
                    alone(dve)
                    dve.bn_aggr(mv2s[:, u, :], bn2[:, u, :]).then_inc(s_bn2, 1)
                    dve.wait_ge(s_bn2, at(2 * n + 2))
                    alone(dve)
                    dve.tensor_copy(mv2_flat[:, bass.ds(2 * n, 2)], mv2s[:, u, :]).then_inc(s_mv2, 1)

            shift_scores(0)
            with dve.Fori(0, NT // 2 - 1) as i:
                normalise(i)
                shift_scores(i + 1)
                add_softmax(i)
            normalise(NT // 2 - 1)
            add_softmax(NT // 2 - 1)
            dve.wait_ge(s_ln2a, at(1))
            dve.reciprocal(sd2, sd2).then_inc(s_ln2d, 1)
            dve.wait_ge(s_ln2d, at(1))
            with dve.Fori(0, NT // 2) as i:
                for u in range(2):
                    n = 2 * i + u
                    row = xn[:, bass.ds(n * D, D)]
                    dve.wait_ge(s_x2t, at(n - 1))
                    dve.wait_ge(s_x2c, at(n - 1))
                    dve.tensor_scalar(x2s[:, u, :], row, mv2_flat[:, bass.ds(2 * n, 1)], sd2[:, bass.ds(n, 1)],
                                      ALU.subtract, ALU.mult).then_inc(s_x2, 1)
                    dve.wait_ge(s_x2, at(n + 1))
                    alone(dve)
                    dve.tensor_copy(row, x2s[:, u, :]).then_inc(s_x2c, 1)
            steps = [0]

            def routed(ins):
                ins.then_inc(s_rt, 1)
                steps[0] += 1
                dve.wait_ge(s_rt, at(steps[0]))

            iota = over(consts[:, C_IOTA:C_IOTA + E], 1, NT)
            dve.wait_ge(s_el, at(NT))
            routed(dve.tensor_scalar(aff, elog, 1.0, None, ALU.add))
            routed(dve.reciprocal(aff, aff))
            left = aff
            for k, sel in enumerate((pick, pick2)):
                routed(dve.tensor_reduce(best[:, k], left, AXX, ALU.max))
                routed(dve.tensor_tensor(lower, left, over(best[:, k], 2, E), ALU.is_lt))
                routed(dve.scalar_tensor_tensor(lower, lower, 64.0, iota, ALU.mult, ALU.add))
                routed(dve.tensor_reduce(best[:, 2], lower, AXX, ALU.min))
                routed(dve.tensor_tensor(sel, iota, over(best[:, 2], 2, E), ALU.is_equal))
                if k == 0:
                    routed(dve.scalar_tensor_tensor(spare, sel, -4.0, left, ALU.mult, ALU.add))
                    left = spare
            dve.tensor_tensor(chosen, pick, pick2, ALU.add).then_inc(s_mask, 1)
            dve.wait_ge(s_pre, at(1))
            routed(dve.tensor_copy(slot, ps[:, 6, 0:NT * E].rearrange("p (n e) -> p n e", e=E)))
            routed(dve.tensor_copy(cum, ps[:, 7, 0:NT * E].rearrange("p (n e) -> p n e", e=E)))
            routed(dve.tensor_tensor(slot, slot, cum, ALU.subtract))

            def running_sum(a, b, n):
                d = 1
                while d < n:
                    dve.tensor_copy(b[:, 0:d], a[:, 0:d])
                    routed(dve.tensor_tensor(b[:, d:n], a[:, d:n], a[:, 0:n - d], ALU.add))
                    a, b, d = b, a, 2 * d
                return a

            upto = running_sum(cum, cum2, NT)
            routed(dve.tensor_tensor(slot, slot, upto, ALU.add))
            routed(dve.tensor_tensor(spare, over(upto[:, NT - 1], 2, NT), over(consts[:, C_K128:C_K128 + NT], 1, E), ALU.is_gt))
            routed(dve.tensor_reduce(byexp[:, 0], spare, AXX, ALU.add))
            routed(dve.tensor_copy(byexp[:, 1], byexp[:, 0]))
            last = running_sum(byexp[:, 1], byexp[:, 2], E)
            routed(dve.tensor_tensor(byexp[:, 3], last, byexp[:, 0], ALU.subtract))
            routed(dve.tensor_scalar(byexp[:, 3], byexp[:, 3], float(P), None, ALU.mult))
            routed(dve.tensor_tensor(slot, slot, over(byexp[:, 3], 1, NT), ALU.add))
            for k, sel in enumerate((pick, pick2)):
                routed(dve.tensor_tensor(lower, sel, slot, ALU.mult))
                routed(dve.tensor_reduce(best[:, 3 + k], lower, AXX, ALU.add))
                routed(dve.tensor_copy(slots_i[:].rearrange("p (n k) -> p n k", k=2)[:, :, k], best[:, 3 + k]))
            routed(dve.tensor_tensor(by_tile, over(last, 1, NSLOT), over(consts[:, C_TILE:C_TILE + NSLOT], 2, E), ALU.is_le))
            routed(dve.tensor_reduce(expert_f, by_tile, AXX, ALU.add))
            routed(dve.tensor_scalar(expert_f, expert_f, float(E - 1), None, ALU.min))
            dve.tensor_copy(expert_i[:], expert_f).then_inc(s_slots, 1)
            routed(dve.tensor_tensor(best[:, 3], best[:, 0], best[:, 1], ALU.add))
            routed(dve.reciprocal(best[:, 4], best[:, 3]))
            for k, sel in enumerate((pick, pick2)):
                routed(dve.tensor_tensor(best[:, 5 + k], best[:, k], best[:, 4], ALU.mult))
                routed(dve.tensor_tensor(sel, sel, over(best[:, 5 + k], 2, E), ALU.mult))
            dve.wait_ge(s_mask, at(1))
            dve.tensor_tensor(comb[:, :, 0:E], pick, pick2, ALU.add).then_inc(s_comb, 1)
            dve.memset(comb[:, :, E:NE], 1.0).then_inc(s_comb, 1)
            dve.wait_ge(s_x2c, at(NT))
            with dve.Fori(0, NT // 2) as i:
                for u in range(2):
                    n = 2 * i + u
                    row = xn[:, bass.ds(n * D, D)]
                    dve.wait_ge(s_b2, at(n + 1))
                    dve.wait_ge(s_xst, at(NT // 4))
                    dve.scalar_tensor_tensor(row, row, 2.0, ps[:, 2 + u, 0:D], ALU.mult, ALU.add).then_inc(s_acc0, 1)

            def shared_expert(u):
                for g in range(NG + 1):
                    if g < NG:
                        m = NG * u + g
                        dve.wait_ge(s_ge, at(m + 1))
                        if m >= 2:
                            dve.wait_ge(s_eo, at(m - 1))
                        dve.scalar_tensor_tensor(ybf[:, g % 2, :], ps[:, 2 + g % 2, :], colp[:, E + u + W_B1:E + u + W_B1 + 1],
                                                 hbuf[:, g % 2, :], ALU.add, ALU.mult).then_inc(s_yy, 1)
                    if g > 0:
                        m = NG * u + g - 1
                        for t in range(SPG):
                            n = SPG * (g - 1) + t
                            if t < SPG - 1:
                                dve.wait_ge(s_eot, at(3 * m + t + 1))
                            else:
                                dve.wait_ge(s_eo, at(m + 1))
                            if u > 0:
                                dve.wait_ge(s_ac, at(n + 1))
                            row = xn[:, n * D:(n + 1) * D]
                            dve.tensor_tensor(row, ps[:, 4 + t, 0:D], row, ALU.add).then_inc(s_ac, 1)

            dve.wait_ge(s_acc0, at(NT))
            shared_expert(0)
            with dve.Fori(0, NSLOT // W4) as i:
                for v in range(W4):
                    j = W4 * i + v
                    dve.wait_ge(s_gg, at(j + 1))
                    dve.wait_ge(s_yt, at(j - W4 + 1))
                    dve.tensor_tensor(yhb[:, v, :], ps[:, 2 * v + 1, F:2 * F], geb[:, v, :], ALU.mult).then_inc(s_yh, 1)
                for v in range(W4):
                    j = W4 * i + v
                    dve.wait_ge(s_yt, at(j + 1))
                    dve.wait_ge(s_yo, at(j - W4 + 1))
                    dve.tensor_copy(yTb[:, v, :], ps[:, 2 * v, 2 * P:3 * P]).then_inc(s_yte, 1)
            shared_expert(1)
            dve.wait_ge(s_ac, at(2 * NT))
            with dve.Fori(0, NT // 8) as i:
                for b in range(2):
                    dve.wait_ge(s_got[b], 128 * (i + 1))
                    for t in range(4):
                        n = 8 * i + 4 * b + t
                        row = xn[:, bass.ds(n * D, D)]
                        for k in range(2):
                            if k > 0:
                                dve.wait_ge(s_f1, at(2 * n + 1))
                            dve.scalar_tensor_tensor(row, got[:, b, 2 * t + k, :], w_flat[:, bass.ds(n + k * NT, 1)], row,
                                                     ALU.mult, ALU.add).then_inc(s_f1, 1)
            dve.wait_ge(s_f1, at(2 * NT))
            with dve.Fori(0, NT // 2) as i:
                for u in range(2):
                    n = 2 * i + u
                    row = xn[:, bass.ds(n * D, D)]
                    dve.wait_ge(s_ob, at(n - 1))
                    alone(dve)
                    dve.bn_stats(bn3[:, u, :], row).then_inc(s_bn3, 1)
                    dve.wait_ge(s_bn3, at(2 * n + 1))
                    alone(dve)
                    dve.bn_aggr(mv3[:, u, :], bn3[:, u, :]).then_inc(s_bn3, 1)
                for u in range(2):
                    n = 2 * i + u
                    row = xn[:, bass.ds(n * D, D)]
                    dve.wait_ge(s_sd3, at(n + 1))
                    dve.reciprocal(ri3[:, u, :], sd3[:, u, :]).then_inc(s_ri3, 1)
                    dve.wait_ge(s_ri3, at(n + 1))
                    dve.wait_ge(s_out[u], 16 * i + 16)
                    dve.tensor_scalar(ob[:, u, :], row, mv3[:, u, 0:1], ri3[:, u, :],
                                      ALU.subtract, ALU.mult).then_inc(s_ob, 1)

        @block.gpsimd
        def _(pool):
            start_counts(pool, "pool")
            pool.wait_ge(s_cst, 48)
            for g in range(NG):
                pool.wait_ge(s_xt[g], 16)
            pool.wait_ge(s_wo, 32)
            pool.tensor_scalar(wo[:], wo[:], colp[:, W_NORM:W_NORM + 1], None, ALU.mult).then_inc(s_pw, 1)
            pool.wait_ge(s_bs, at(1))
            for b in range(2):
                pool.dma_start(slots_dr[(NSLOT + 2 + b) * P:(NSLOT + 3 + b) * P], zero[:]).then_inc(s_scat[b], 16)
            with pool.Fori(0, NG) as g:
                pool.wait_ge(s_gmm, at(SPG * g))
                pool.tensor_copy(xs, xT3[:, :, bass.ds(g * GT, GT)]).then_inc(s_xs, 1)
                for j in range(4):
                    pool.wait_ge(s_silu, at(NCH * g + j + 1))
                    pool.wait_ge(s_ss, at(g))
                    src = arena[0:KR, bass.ds(g * GT + j * NTOK, GT)]
                    pool.tensor_tensor(sqs[0:KR, j, :], src, src, ALU.mult).then_inc(s_sq, 1)
            pool.wait_ge(s_gd, at(9))
            pool.wait_ge(s_ss, at(NG))
            with pool.Fori(0, NT // 2) as i:
                for u in range(2):
                    n = 2 * i + u
                    pool.wait_ge(s_dmm, at(n - 1))
                    pool.tensor_tensor(gst[:, u], over(small[:, bass.ds(n * H + T_G * NT * H, H)], 2, T),
                                       over(tmask, 1, H), ALU.mult).then_inc(s_gst, 1)
                    pool.wait_ge(s_kmm, at(n - 1))
                    for f in range(2):
                        ins = pool.tensor_tensor(blk[0:KR, u, f, 0],
                                                 over(arena[0:KR, bass.ds(n * P + (2 + f) * NTOK, P)], 1, HH),
                                                 over(consts[0:KR, C_HM:C_HM + HH], 2, P), ALU.mult)
                    ins.then_inc(s_kblk, 1)
            def turned(ins):
                ins.then_inc(s_kp, 1)

            for w0, nh, (cosw, sinw) in ((R_QN, NH, rope_q), (R_KN, NKV, rope_k)):
                w = rowp[:, w0:w0 + nh * HD]
                turned(pool.tensor_tensor(cosw.rearrange("p (h c) -> p h c", h=nh), w.rearrange("p (h c) -> p h c", h=nh),
                                          over(consts[:, C_COS:C_COS + HD], 1, nh), ALU.mult))
                for z in range(2):
                    turned(pool.tensor_tensor(sinw.rearrange(halves, h=nh, z=2)[:, :, z],
                                              w.rearrange(halves, h=nh, z=2)[:, :, 1 - z],
                                              over(consts[:, C_SIN + 8 * z:C_SIN + 8 * z + 8], 1, nh), ALU.mult))
            pool.wait_ge(s_kp, at(6))
            pool.wait_ge(s_kd, at(4))
            turned(pool.tensor_tensor(kt1.rearrange("p (n c) -> p n c", c=CKV), ctx3, over(rope_k[0], 1, NT), ALU.mult))
            for h in range(NKV):
                for z in range(2):
                    a, b = HD * h + 8 * z, HD * h + 8 * (1 - z)
                    turned(pool.tensor_tensor(kt2.rearrange("p (n c) -> p n c", c=CKV)[:, :, a:a + 8], ctx3[:, :, b:b + 8],
                                              over(rope_k[1][:, a:a + 8], 1, NT), ALU.mult))
            pool.wait_ge(s_kp, at(15))
            turned(pool.tensor_tensor(krope[:], kt1, kt2, ALU.add))
            pool.wait_ge(s_blk_in, 16 * 12)
            invert(pool, s_invp, 2, 1, tmp_p)
            def scale_values(i):
                for u in range(2):
                    n = 2 * i + u
                    pool.wait_ge(s_w0, at(n - 1))
                    pool.tensor_tensor(vp[:, u], vt[:, bass.ds(n * HV, HV)].rearrange("p (h t) -> p h t", h=H),
                                       over(small[:, bass.ds(n * H + T_NK * NT * H, H)], 2, DV), ALU.mult).then_inc(s_vp, 1)

            def scale_gate(i):
                for u in range(2):
                    n = 2 * i + u
                    pool.wait_ge(s_og, at(n - 1))
                    pool.tensor_tensor(sgr[:, u, :].rearrange("p (h t) -> p h t", h=H),
                                       sg[:, bass.ds(n * HV, HV)].rearrange("p (h t) -> p h t", h=H),
                                       over(small[:, bass.ds(n * H + T_RQ * NT * H, H)], 2, DV), ALU.mult).then_inc(s_sgr, 1)

            def square_heads(i):
                for u in range(2):
                    n = 2 * i + u
                    pool.wait_ge(s_og, at(n + 1))
                    pool.wait_ge(s_ms, at(n - 1))
                    pool.tensor_tensor(osq[:, u, :], og[:, u, :], og[:, u, :], ALU.mult).then_inc(s_osq, 1)

            def norm_heads(i):
                for u in range(2):
                    n = 2 * i + u
                    pool.wait_ge(s_rr, at(n + 1))
                    o3 = og[:, u, :].rearrange("p (h t) -> p h t", h=H)
                    pool.wait_ge(s_osq, at(n + 1))
                    pool.tensor_tensor(o3, o3, over(rs[:, u, :], 2, DV), ALU.mult).then_inc(s_og2, 1)

            scale_values(0)
            scale_gate(0)
            with pool.Fori(0, NT // 2 - 1) as i:
                scale_values(i + 1)
                square_heads(i)
                norm_heads(i)
                scale_gate(i + 1)
            square_heads(NT // 2 - 1)
            norm_heads(NT // 2 - 1)
            pool.wait_ge(s_kp, at(16))
            with pool.Fori(0, NT // 2) as i:
                for u in range(2):
                    n = 2 * i + u
                    pool.wait_ge(s_kqt, at(n - 1))
                    pool.tensor_copy(kx[:, u, :].rearrange("p (g r c) -> p g r c", g=NKV, r=4),
                                     over(krope[:, bass.ds(n * CKV, CKV)].rearrange("p (g c) -> p g c", g=NKV), 2, 4)
                                     ).then_inc(s_kx, 1)
                    pool.wait_ge(s_x1, at(n + 1))
                    row = xn[:, bass.ds(n * D, D)]
                    pool.tensor_tensor(qt1[:, u, :], row, rope_q[0], ALU.mult)
                    for z in range(2):
                        ins = pool.tensor_tensor(qt2[:, u, :].rearrange(halves, h=NH, z=2)[:, :, z],
                                                 row.rearrange(halves, h=NH, z=2)[:, :, 1 - z],
                                                 rope_q[1].rearrange(halves, h=NH, z=2)[:, :, z], ALU.mult)
                        ins.then_inc(s_qr, 1)
                    pool.wait_ge(s_qr, at(3 * n + 2))
                    pool.tensor_tensor(qr[:, u, :], qt1[:, u, :], qt2[:, u, :], ALU.add).then_inc(s_qr, 1)
                for u in range(2):
                    n = 2 * i + u
                    pool.wait_ge(s_kqe, at(n + 1))
                    pool.wait_ge(s_sc, at(2 * (n - 1)))
                    for f in range(2):
                        ins = pool.tensor_tensor(kblk[:, u, f], over(kqT[:, u, 0, f, :], 1, 8),
                                                 over(consts[:, C_KM:C_KM + 8], 2, P), ALU.mult)
                    ins.then_inc(s_kb, 1)
                for u in range(2):
                    n = 2 * i + u
                    pool.wait_ge(s_vin[u], 32 * (i + 1))
                    pool.wait_ge(s_pv, at(n - 1))
                    for s in range(2):
                        ins = pool.tensor_tensor(vblk[:, u, s].rearrange("p g (z c) -> p g z c", z=2),
                                                 over(vdup[:, u, s].rearrange("p (g c) -> p g c", g=NKV), 2, 2),
                                                 over(consts[:, C_VM:C_VM + 32].rearrange("p (z c) -> p z c", z=2), 1, NKV),
                                                 ALU.mult)
                    ins.then_inc(s_vb, 1)
            pool.wait_ge(s_slots, at(1))
            pool.wait_ge(s_zero_in, 16 * (NSLOT + 2))
            with pool.Fori(0, NT // 8) as i:
                for b in range(2):
                    pool.wait_ge(s_scat[b], 128 * i + 16)
                    pool.tensor_copy(idxs[:, 8 * b:8 * b + 8], slots_i[:, bass.ds((2 * i + b) * 8, 8)]).then_inc(s_ix, 1)
                    pool.wait_ge(s_xst, at(2 * i + b + 1))
                    pool.wait_ge(s_ix, at(2 * i + b + 1))
                    alone(pool)
                    for c in range(8):
                        pool.indirect_dma_start(
                            out=slots_dr, out_offset=bass.IndirectOffsetOnAxis(ap=idxs[:, 8 * b + c:8 * b + c + 1], axis=0),
                            in_=xst[:, b, c // 2 * D:(c // 2 + 1) * D], in_offset=None).then_inc(s_scat[b], 16)
            pool.wait_ge(s_comb, at(2))
            with pool.Fori(0, NT // 2) as i:
                for u in range(2):
                    n = 2 * i + u
                    pool.wait_ge(s_ct, at(n - 1))
                    pool.tensor_copy(combs[:, u, :], comb_flat[:, bass.ds(n * NE, NE)]).then_inc(s_cs, 1)
            for v in range(W4):
                pool.wait_ge(s_yout[v], 16 * (NSLOT // W4) + 16)
            pool.wait_ge(s_yo, at(NSLOT))
            with pool.Fori(0, NT // 8) as i:
                for b in range(2):
                    m = NT // 4 + 2 * i + b
                    pool.wait_ge(s_f1, at(8 * (2 * i + b - 2) + 8))
                    pool.tensor_copy(idxs[:, 8 * b:8 * b + 8], slots_i[:, bass.ds((2 * i + b) * 8, 8)]).then_inc(s_ix, 1)
                    pool.wait_ge(s_ix, at(m + 1))
                    alone(pool)
                    for c in range(8):
                        pool.indirect_dma_start(
                            out=got[:, b, c, :], out_offset=None, in_=expert_dr,
                            in_offset=bass.IndirectOffsetOnAxis(ap=idxs[:, 8 * b + c:8 * b + c + 1], axis=0)
                        ).then_inc(s_got[b], 16)


def kernel(**inputs):
    import numpy as _np
    import concourse.bacc as _bacc
    from concourse.bass_utils import run_bass_kernel_spmd as _run

    a = {k: _np.asarray(v) for k, v in inputs.items()}
    x = _np.ascontiguousarray(a["x"]).reshape(NTOK, D)
    wq, wk, wv = a["L0_attn_Wq"], a["L0_attn_Wk"], a["L0_attn_Wv"]
    cat = _np.concatenate
    conv = cat([a["L0_attn_conv_q_w"], a["L0_attn_conv_k_w"], a["L0_attn_conv_v_w"]])[:, 0, :]
    col = _np.zeros((P, NCOL), _np.float32)
    for j in range(NCH):
        col[0:ROWS[j], W_TAP + j * KSZ:W_TAP + (j + 1) * KSZ] = conv[CH0[j]:CH0[j] + ROWS[j]]
    col[:, W_NORM] = _np.tile(a["L0_attn_norm_w"], 2)
    col[:, W_GB:W_GB + NE] = cat([a["L0_ffn_rgb"], a["L0_ffn_sgb"]]).T
    col[:, W_B1:W_B1 + NE] = cat([a["L0_ffn_rb1"], a["L0_ffn_sb1"]]).T
    row = cat([a["L0_attn_A_log"], a["L0_attn_dt_bias"], a["L0_xattn_q_norm_w"], a["L0_xattn_k_norm_w"]])
    g = cat([a["L0_ffn_rg"], a["L0_ffn_sg"]])
    w1 = cat([a["L0_ffn_rw1"], a["L0_ffn_sw1"]])
    w2 = cat([a["L0_ffn_rw2"], a["L0_ffn_sw2"]])
    lay = lambda w: w.reshape(-1, KD, P, F).transpose(0, 2, 1, 3).reshape(-1, P, KD * F)
    pair = lambda u, w: cat([u.reshape(-1, KD, P, F), w.reshape(-1, KD, P, F)], axis=3).transpose(0, 2, 1, 3).reshape(-1, P, 2 * KD * F)
    arrays = {
        "xt": x.T, "x": x, "ctx": a["ctx_512"].reshape(NTOK, CKV), "consts": constants(),
        "row": row.reshape(NROW), "col": col,
        "wc": cat([wq, wk, wv]).T, "wg": cat([a["L0_attn_Wg"], a["L0_attn_Wa"], a["L0_attn_Wb"]]).T,
        "wo": a["L0_attn_Wo"].T, "wout": a["L0_xattn_w_out"].T, "wa": a["L0_ffn_wa"],
        "wexp": cat([cat([pair(g[0:E], w1[0:E]), w2[0:E]], axis=2), cat([lay(g[E:NE]), lay(w1[E:NE]), w2[E:NE]], axis=2)]),
        "b2": cat([a["L0_ffn_rb2"], a["L0_ffn_sb2"]]),
        "bias": cat([a["L0_ffn_rgb"], a["L0_ffn_rb1"]], axis=1).reshape(P, E * 2 * F // P),
    }
    nc = _bacc.Bacc("TRN2", target_bir_lowering=False, num_devices=1)
    args = []
    for name in arrays:
        arrays[name] = _np.ascontiguousarray(arrays[name], dtype=_np.float32)
        args.append(nc.dram_tensor(name + "_dram", arrays[name].shape, F32, kind="ExternalInput").ap())
    out = nc.dram_tensor("out_dram", (NTOK, D), F32, kind="ExternalOutput").ap()
    build(nc, *args, out)
    r = _run(nc, [{k + "_dram": v for k, v in arrays.items()}], core_ids=[0])
    return r.results[0]["out_dram"].reshape(B, T, D)
```

```python
from contextlib import ExitStack

import numpy as np

import concourse.bass as bass
from concourse import mybir

F32 = mybir.dt.float32
BF16 = mybir.dt.bfloat16
U32 = mybir.dt.uint32
ALU = mybir.AluOpType
ACT = mybir.ActivationFunctionType
AXX = mybir.AxisListType.X

B, T, D = 32, 64, 256
NTOK = B * T
P = 128
NT = NTOK // P
KD = D // P
H, DK, DV = 6, 32, 64
HH = H // 2
KR = HH * DK
HV = H * DV
KSZ = 4
GT = 512
NG = NTOK // GT
SPG = GT // P
SEQG = GT // T
NCH = 7
ROWS = [KR] * 4 + [P] * 3
CH0 = [0, KR, 2 * KR, 3 * KR, 4 * KR, 4 * KR + P, 4 * KR + 2 * P]
NCHAN = 4 * KR + 3 * P
NGATE = HV + 2 * H
NH, NKV, HD = 16, 4, 16
CKV = NKV * HD
E, SH, F = 16, 2, 128
NE = E + SH
NSLOT = 2 * NTOK // P + E
EW = 2 * KD * F + D
BL = 32
HEAD = 16
NEG = -1e30

C_ID = 0
C_LTRI = C_ID + P
C_TM = C_LTRI + P
C_NEG = C_TM + T
C_CAUS = C_NEG + T
C_HSEL = C_CAUS + T
C_HM = C_HSEL + 32
C_KM = C_HM + HH
C_VM = C_KM + 8
C_COS = C_VM + 32
C_SIN = C_COS + HD
C_IOTA = C_SIN + HD
C_K128 = C_IOTA + NE
C_TILE = C_K128 + NT
C_PRE = C_TILE + NSLOT
C_ONE = C_PRE + P
NCONST = C_ONE + P


def constants():
    c = np.zeros((P, NCONST), np.float32)
    p = np.arange(P)[:, None]
    f = np.arange(P)[None, :]
    t = np.arange(T)[None, :]
    c[:, C_ID:C_ID + P] = p == f
    c[:, C_LTRI:C_LTRI + P] = (p > f) & (p // T == f // T)
    c[:, C_TM:C_TM + T] = p % T <= t
    c[:, C_NEG:C_NEG + T] = np.where(t < p % T, NEG, 0.0)
    c[:, C_CAUS:C_CAUS + T] = np.where(t > p % T, NEG, 0.0)
    a = np.arange(32)[None, :]
    c[:, C_HSEL:C_HSEL + 32] = (p // DK == a) & (a < HH) & (p < KR)
    c[:, C_HM:C_HM + HH] = p // DK == np.arange(HH)[None, :]
    c[:, C_KM:C_KM + 8] = p // HD == np.arange(8)[None, :]
    c[:, C_VM:C_VM + 32] = p // T == a // HD
    inv = (1.0 / np.float32(10000.0) ** (np.arange(0, HD, 2, dtype=np.float32) / np.float32(HD))).astype(np.float32)
    fr = np.outer(np.arange(T, dtype=np.float32), inv)
    emb = np.concatenate([fr, fr], -1)
    sign = np.where(np.arange(HD) < HD // 2, -1.0, 1.0)
    c[:, C_COS:C_COS + HD] = np.tile(np.cos(emb), (2, 1))
    c[:, C_SIN:C_SIN + HD] = np.tile(np.sin(emb) * sign, (2, 1))
    c[:, C_IOTA:C_IOTA + NE] = np.arange(NE)[None, :]
    c[:, C_K128:C_K128 + NT] = P * np.arange(NT)[None, :]
    c[:, C_TILE:C_TILE + NSLOT] = np.arange(NSLOT)[None, :]
    c[:, C_PRE:C_PRE + P] = p < f
    c[:, C_ONE:C_ONE + P] = 1.0
    return c


R_ALOG = 0
R_DT = R_ALOG + H
R_QN = R_DT + H
R_KN = R_QN + D
NROW = R_KN + CKV

W_TAP = 0
W_NORM = W_TAP + NCH * KSZ
W_GB = W_NORM + 1
W_B1 = W_GB + NE
NCOL = W_B1 + NE


def at(count):
    return count + HEAD


def alone(eng):
    eng.nop(nofuse=True)


def over(ap, axis, n):
    ap = ap.unsqueeze(axis)
    shape = list(ap.shape)
    shape[axis] = n
    return ap.to_broadcast(shape)


def build(nc, xt_d, x_d, ctx_d, consts_d, row_d, col_d, wc_d, wg_d, wo_d, wout_d, wa_d, wexp_d, bias_d, out_d):
    with ExitStack() as ctx:
        def sb(name, cols, dt=F32):
            return ctx.enter_context(nc.sbuf_tensor(name, [P, cols], dt))

        engine_sems = {"pe": [], "act": [], "dve": [], "pool": []}

        def counted(engine, name):
            s = ctx.enter_context(nc.semaphore(name))
            engine_sems[engine].append(s)
            return s

        def dma_sem(name):
            return ctx.enter_context(nc.semaphore(name))

        def start_counts(eng, name):
            for s in engine_sems[name]:
                eng.sem_inc(s, HEAD)

        scores_dr = nc.dram_tensor("scores_dr", [NT, P, H * T], F32, kind="Internal").ap()
        attend_dr = nc.dram_tensor("attend_dr", [NT, P, H * T], F32, kind="Internal").ap()
        bias_dr = nc.dram_tensor("bias_dr", [3, E * 2 * F + NE * D], BF16, kind="Internal").ap()
        slots_dr = nc.dram_tensor("slots_dr", [(NSLOT + 4) * P, D], F32, kind="Internal").ap()
        expert_dr = nc.dram_tensor("expert_dr", [NSLOT * P, D], F32, kind="Internal").ap()
        inverse_dr = nc.dram_tensor("inverse_dr", [B, 2, BL, 2, HH * BL], F32, kind="Internal").ap()

        BPC = (E * 2 * F + NE * D) // P
        consts = sb("consts", NCONST)
        rowp = sb("rowp", NROW)
        colp = sb("colp", NCOL)
        idb = sb("idb", P, BF16)
        onesb = sb("onesb", P, BF16)
        negb = sb("negb", 2 * T, BF16)
        xT = sb("xT", KD * NTOK)
        xn = sb("xn", NT * D)
        arena = sb("arena", 4 * NTOK)
        vsg = sb("vsg", 2 * NT * HV)
        vt = vsg[:, 0:NT * HV]
        sg = vsg[:, NT * HV:2 * NT * HV]
        ab = sb("ab", NT * 2 * H)
        wc = sb("wc", KD * NCHAN)
        wg = sb("wg", KD * NGATE)
        wo = sb("wo", 3 * D)
        wout = sb("wout", KD * D)
        ctxn = sb("ctxn", NT * CKV)
        zero = sb("zero", D)
        brow = sb("brow", E * 2 * F, BF16)
        bsp = sb("bsp", 3 * BPC)
        bsb = sb("bsb", 3 * BPC, BF16)
        krope = sb("krope", NT * CKV)
        ropes = sb("ropes", 2 * D + 2 * CKV)
        n2 = sb("n2", NT * 2 * H)
        small = sb("small", 8 * NT * H)
        work = sb("work", 12 * 1024)

        ident = consts[:, C_ID:C_ID + P]
        tmask = consts[:, C_TM:C_TM + T]

        ps = ctx.enter_context(nc.psum_tensor("ps", [P, 8, 512], F32))

        x3 = xn[:].rearrange("p (n d) -> p n d", d=D)
        xT3 = xT[:].rearrange("p (k n) -> p k n", k=KD)
        wc3 = wc[:].rearrange("p (k c) -> p k c", k=KD)
        wg3 = wg[:].rearrange("p (k c) -> p k c", k=KD)
        wo3 = wo[:].rearrange("p (k c) -> p k c", k=3)
        wout3 = wout[:].rearrange("p (k c) -> p k c", k=KD)
        ab3 = ab[:].rearrange("p (n c) -> p n c", c=2 * H)
        n23 = n2[:].rearrange("p (n c) -> p n c", c=2 * H)

        def tab(k):
            return small[:, k * NT * H:(k + 1) * NT * H]
        T_G, T_C, T_NK, T_RQ, T_A, T_B = range(6)
        stats = small[:, 6 * NT * H:7 * NT * H]
        rq_tab = small[:, 7 * NT * H:7 * NT * H + NT]

        s_cst = dma_sem("weights_and_constants_in")
        s_wg = dma_sem("gate_weights_in")
        s_wo = dma_sem("out_weights_in")
        s_xt = [dma_sem(f"xt_in{g}") for g in range(NG)]
        s_xn = dma_sem("x_and_context_in")
        s_sc_out = [dma_sem(f"scores_out{u}") for u in range(2)]
        s_blk_in = dma_sem("blocks_in")
        s_inv_out = [dma_sem(f"inverse_out{k}") for k in range(2)]
        s_out = [dma_sem(f"out_done{u}") for u in range(2)]
        s_pair_in = [dma_sem(f"pair_in{b}") for b in range(2)]

        s_idb = counted("dve", "bf16_masks_ready")
        s_xs = counted("pool", "group_staged")
        s_gmm = counted("pe", "gate_projected")
        s_gev = counted("act", "gate_evacuated")
        s_proj = counted("pe", "channels_projected")
        s_tap0 = counted("act", "first_tap_done")
        s_tap = counted("dve", "taps_summed")
        s_conv = counted("dve", "convolved")
        s_silu = counted("act", "channels_activated")
        s_sq = counted("pool", "squares_ready")
        s_ss = counted("pe", "square_sums_ready")
        s_ssev = counted("act", "square_sums_evacuated")
        s_sst = counted("pe", "square_sums_turned")
        s_n2 = counted("dve", "square_sums_by_token")
        s_vtr = counted("pe", "values_turned")
        s_vev = counted("act", "values_by_token")
        s_gk = counted("act", "gating_act_step")
        s_gd = counted("dve", "gating_dve_step")
        s_pw = counted("pool", "pool_weight_step")

        xs = work[:, 0:KD * GT].rearrange("p (k n) -> p k n", k=KD)
        ybuf = work[:, 1024:1024 + 4 * GT].rearrange("p (j n) -> p j n", j=4)
        vs = work[:, 3072:3072 + 3 * GT].rearrange("p (j n) -> p j n", j=3)
        sqs = work[:, 4608:4608 + 4 * GT].rearrange("p (j n) -> p j n", j=4)
        ssb = work[:, 6656:6656 + GT]
        BANK = [0, 1, 2, 3, 0, 1, 2]
        taps = colp[:, W_TAP:W_TAP + NCH * KSZ].rearrange("p (j k) -> p j k", k=KSZ)

        def bank_free(j, g):
            return NCH * g + (j - 4 if j >= 4 else min(j + 4, 6 if j < 3 else 3) - NCH if j < 3 else 3 - NCH) + 1

        kst = work[:, 0:2 * 2 * P].rearrange("p (u f n) -> p u f n", u=2, f=2)
        blk = work[:, 512:512 + 2 * 2 * 2 * HH * P].rearrange("p (u f q h n) -> p u f q h n", u=2, f=2, q=2, h=HH)
        gst = work[:, 3584:3584 + 2 * H * T].rearrange("p (u h t) -> p u h t", u=2, h=H)
        est = work[:, 4352:4352 + 2 * H * T].rearrange("p (u h t) -> p u h t", u=2, h=H)
        rst = work[:, 5120:5120 + 2 * H * T].rearrange("p (u q f h t) -> p u q f h t", u=2, q=2, f=2, h=HH)
        ast = work[:, 5888:5888 + 2 * H * T].rearrange("p (u h t) -> p u h t", u=2, h=H)
        s_kst = counted("act", "keys_staged")
        s_kblk = counted("pool", "key_blocks_ready")
        s_qblk = counted("dve", "query_blocks_ready")
        s_gst = counted("pool", "decays_spread")
        s_dmm = counted("pe", "decay_sums_ready")
        s_kmm = counted("pe", "products_ready")
        s_e = counted("act", "decay_factors_ready")
        s_ec = counted("dve", "weighted_factors_ready")
        s_rs = counted("dve", "system_ready")
        s_as = counted("dve", "attention_ready")
        rb_flat = xT[:, 0:HH * BL * BL]
        rb = rb_flat.rearrange("p (i h t) -> p h i t", h=HH, i=BL)
        nb_flat = arena[:, HH * BL * BL:2 * HH * BL * BL]
        nb = nb_flat.rearrange("p (i h t) -> p h i t", h=HH, i=BL)
        tmp_d = work[:, 7000:7000 + 2 * 256].rearrange("p (h n) -> p h n", h=2)
        tmp_p = work[:, 7512:7512 + 256].rearrange("p (h n) -> p h n", h=1)
        s_invd = counted("dve", "inversion_dve_step")
        s_invp = counted("pool", "inversion_pool_step")

        def invert(eng, sem, h0, nh, tmp):
            eng.memset(nb[:, h0:h0 + nh], 0.0).then_inc(sem, 1)
            eng.wait_ge(sem, at(1))
            for h in range(h0, h0 + nh):
                ins = eng.memset(nb_flat[:, h * BL:h * BL + (HH * BL + 1) * (BL - 1) + 1:HH * BL + 1], 1.0)
            ins.then_inc(sem, 1)
            for k, t in enumerate(range(BL - 1, 0, -1)):
                w = BL - t
                prod = tmp[:, 0:nh, 0:t * w].rearrange("p h (i c) -> p h i c", i=t)
                eng.wait_ge(sem, at(2 + 2 * k))
                eng.tensor_tensor(prod, over(rb[:, h0:h0 + nh, 0:t, t], 3, w), over(nb[:, h0:h0 + nh, t, t:BL], 2, t),
                                  ALU.mult).then_inc(sem, 1)
                eng.wait_ge(sem, at(3 + 2 * k))
                eng.tensor_tensor(nb[:, h0:h0 + nh, 0:t, t:BL], nb[:, h0:h0 + nh, 0:t, t:BL], prod,
                                  ALU.subtract).then_inc(sem, 1)

        at_s = xT[:, 0:1536].rearrange("p (b u h t) -> p b u h t", b=2, u=2, h=H)
        roff = xT[:, 1536:2304].rearrange("p (b u h t) -> p b u h t", b=2, u=2, h=H)
        n32 = xT[:, 2304:3072].rearrange("p (b u h t) -> p b u h t", b=2, u=2, h=H)
        vp = xT[:, 3072:3840].rearrange("p (u h t) -> p u h t", u=2, h=H)
        wsol = arena[:, 6144:6912].rearrange("p (u c) -> p u c", u=2)
        ysb = arena[:, 6912:7680].rearrange("p (u c) -> p u c", u=2)
        og = work[:, 7768:8536].rearrange("p (u c) -> p u c", u=2)
        osq = work[:, 8536:9304].rearrange("p (u c) -> p u c", u=2)
        ogT = work[:, 9304:10072].rearrange("p (u k n) -> p u k n", u=2, k=3)
        xr = work[:, 10072:10584].rearrange("p (u c) -> p u c", u=2)
        sgr = work[:, 10584:11352].rearrange("p (u c) -> p u c", u=2)
        ms = work[:, 11352:11364].rearrange("p (u c) -> p u c", u=2)
        rs = work[:, 11364:11376].rearrange("p (u c) -> p u c", u=2)
        bn = work[:, 11376:11388].rearrange("p (u c) -> p u c", u=2)
        mv = work[:, 11388:11392].rearrange("p (u c) -> p u c", u=2)
        sd = work[:, 11392:11394].rearrange("p (u c) -> p u c", u=2)
        rsd = work[:, 11394:11396].rearrange("p (u c) -> p u c", u=2)
        eps = work[:, 11396:11397]
        s_zero = counted("dve", "correction_banks_cleared")
        s_vp = counted("pool", "scaled_values_ready")
        s_sgr = counted("pool", "scaled_gate_ready")
        s_w0 = counted("pe", "block_solves_ready")
        s_w = counted("act", "block_solves_in_sbuf")
        s_y0 = counted("pe", "coupling_ready")
        s_y = counted("act", "coupling_in_sbuf")
        s_z = counted("pe", "correction_ready")
        s_w2 = counted("dve", "solution_ready")
        s_o = counted("pe", "attended_ready")
        s_og = counted("dve", "gated_ready")
        s_osq = counted("act", "gated_squares_ready")
        s_ms = counted("dve", "gated_square_sums_ready")
        s_rms = counted("act", "gated_rms_ready")
        s_rr = counted("dve", "gated_scale_ready")
        s_og2 = counted("pool", "normed_ready")
        s_ot = counted("pe", "normed_turned")
        s_ote = counted("act", "normed_turned_in_sbuf")
        s_xo = counted("pe", "delta_output_ready")
        s_xr = counted("dve", "residual_added")
        s_bn = counted("dve", "layernorm_stats_step")
        s_sd = counted("act", "layernorm_deviation_ready")
        s_rsd = counted("dve", "layernorm_scale_ready")
        s_x1 = counted("dve", "first_layernorm_done")
        s_rq = counted("dve", "query_square_mean_ready")
        kblk = arena[:, 0:4096].rearrange("p (u f h n) -> p u f h n", u=2, f=2, h=8)
        prob = arena[:, 4096:6144].rearrange("p (u f h k) -> p u f h k", u=2, f=2, h=8)
        probT = arena[:, 6144:8192].rearrange("p (u f c) -> p u f c", u=2, f=2)
        kx = work[:, 0:512].rearrange("p (u c) -> p u c", u=2)
        qr = work[:, 512:1024].rearrange("p (u c) -> p u c", u=2)
        kqT = work[:, 1024:2048].rearrange("p (u w f n) -> p u w f n", u=2, w=2, f=2)
        qt1 = work[:, 2048:2560].rearrange("p (u c) -> p u c", u=2)
        qt2 = work[:, 2560:3072].rearrange("p (u c) -> p u c", u=2)
        vdup = work[:, 3072:3328].rearrange("p (u s c) -> p u s c", u=2, s=2)
        vblk = work[:, 3328:3840].rearrange("p (u s g c) -> p u s g c", u=2, s=2, g=NKV)
        oT = work[:, 3840:4352].rearrange("p (u f n) -> p u f n", u=2, f=2)
        prob_u = prob.rearrange("p u f h k -> p u (f h) k")
        mxs = work[:, 4352:4384].rearrange("p (u h) -> p u h", u=2)
        sms = work[:, 4384:4416].rearrange("p (u h) -> p u h", u=2)
        sri = work[:, 4416:4448].rearrange("p (u h) -> p u h", u=2)
        bn2 = work[:, 4448:4460].rearrange("p (u c) -> p u c", u=2)
        mv2 = stats[:, 0:2 * NT].rearrange("p (n c) -> p n c", c=2)
        sd2 = stats[:, 2 * NT:3 * NT]
        rk = stats[:, 3 * NT:4 * NT]
        eps16 = work[:, 11397:11398]
        ksq = work[:, 7768:7768 + NT * CKV]
        kt1 = work[:, 8792:8792 + NT * CKV]
        kt2 = work[:, 9816:9816 + NT * CKV]
        halves = "p (h z c) -> p h z c"
        rope_q = [ropes[:, 0:D], ropes[:, D:2 * D]]
        rope_k = [ropes[:, 2 * D:2 * D + CKV], ropes[:, 2 * D + CKV:2 * D + 2 * CKV]]
        causb = negb[:, T:2 * T]
        ctx3 = ctxn[:].rearrange("p (n c) -> p n c", c=CKV)
        s_vin = [dma_sem(f"context_pair_in{u}") for u in range(2)]
        s_kd = counted("dve", "context_dve_step")
        s_ka = counted("act", "context_act_step")
        s_kp = counted("pool", "rotary_pool_step")
        s_kx = counted("act", "keys_spread")
        s_qr = counted("pool", "queries_rotated_step")
        s_kqt = counted("pe", "keys_queries_turned")
        s_kqe = counted("act", "keys_queries_turned_in_sbuf")
        s_kb = counted("pool", "softmax_key_blocks_ready")
        s_vb = counted("act", "value_blocks_ready")
        s_sc = counted("pe", "scores_ready")
        s_mx = counted("dve", "row_maxima_ready")
        s_sub = counted("dve", "shifted_scores_ready")
        s_exp = counted("act", "exponentials_ready")
        s_sum = counted("dve", "row_sums_step")
        s_pr = counted("dve", "probabilities_ready")
        s_pt = counted("pe", "probabilities_turned")
        s_pte = counted("act", "probabilities_turned_in_sbuf")
        s_pv = counted("pe", "softmax_outputs_ready")
        s_ove = counted("act", "softmax_outputs_in_sbuf")
        s_xp = counted("pe", "softmax_projected")
        s_xr2 = counted("dve", "second_residual_added")
        mv2s = work[:, 4460:4464].rearrange("p (u c) -> p u c", u=2)
        mv2_flat = stats[:, 0:2 * NT]
        s_mv2 = counted("dve", "second_layernorm_stats_kept")
        s_bn2 = counted("dve", "second_layernorm_stats_step")
        s_rqa = counted("act", "query_scale_act_step")
        s_rqd = counted("dve", "query_scale_ready")
        s_ln2a = counted("act", "second_layernorm_deviation_ready")
        s_ln2d = counted("dve", "second_layernorm_scale_ready")

        x2T3 = xT3
        wres = vsg
        wsh = work[:, 7768:7768 + SH * EW].rearrange("p (u c) -> p u c", u=SH)
        hbuf = arena[:, 0:2 * GT].rearrange("p (u c) -> p u c", u=2)
        ybf = arena[:, 1024:1024 + 2 * GT].rearrange("p (u c) -> p u c", u=2)
        logitT = arena[0:E, 0:NTOK]
        wab = sb("wab", KD * E)
        brow2 = work[:, 4608:4608 + NE * D // 2].bitcast(BF16)

        def route(k):
            return arena[:, 3072 + k * NT * E:3072 + (k + 1) * NT * E].rearrange("p (n e) -> p n e", e=E)
        elog, aff, lower, pick, pick2, spare, chosen, cum, cum2, slot = (route(k) for k in range(10))
        elog_flat = arena[:, 3072:3072 + NT * E]
        best = arena[:, 5632:5632 + 8 * NT].rearrange("p (k n) -> p k n", k=8)
        w_flat = arena[:, 5632 + 5 * NT:5632 + 7 * NT]
        byexp = arena[:, 5760:5760 + 8 * E].rearrange("p (k e) -> p k e", k=8)
        by_tile = arena[:, 6468:6468 + NSLOT * E].rearrange("p (j e) -> p j e", e=E)
        expert_f = arena[:, 7236:7236 + NSLOT]
        bn3 = arena[:, 7284:7332].rearrange("p (b t c) -> p b t c", b=2, t=4)
        mv3 = arena[:, 7332:7348].rearrange("p (b t c) -> p b t c", b=2, t=4)
        sd3 = arena[:, 7348:7356].rearrange("p (b t) -> p b t", b=2)
        ri3 = arena[:, 7356:7364].rearrange("p (b t) -> p b t", b=2)
        ob = arena[:, 0:2 * 4 * D].rearrange("p (b c) -> p b c", b=2)
        slots_i = sb("slots_i", 2 * NT, U32)
        idxs = sb("idxs", 2 * 8, U32)
        expert_i = sb("expert_i", NSLOT, U32)
        W4 = 4
        xg = work[:, 0:W4 * D].rearrange("p (v c) -> p v c", v=W4)
        xgT = work[:, 1024:1024 + W4 * D].rearrange("p (v k n) -> p v k n", v=W4, k=KD)
        geb = work[:, 2048:2048 + W4 * F].rearrange("p (v c) -> p v c", v=W4)
        yhb = work[:, 2560:2560 + W4 * F].rearrange("p (v c) -> p v c", v=W4)
        yTb = work[:, 3072:3072 + W4 * F].rearrange("p (v c) -> p v c", v=W4)
        yob = work[:, 3584:3584 + W4 * D].rearrange("p (v c) -> p v c", v=W4)
        xst = work[:, 9304:9304 + 2 * 4 * D].rearrange("p (b c) -> p b c", b=2)
        got = vsg[:, 0:2 * 8 * D].rearrange("p (b k c) -> p b k c", b=2, k=8)
        s_zero_in = dma_sem("slots_cleared")
        s_brow = dma_sem("biases_in_then_parts_out_then_rows_in")
        s_wr = dma_sem("routed_weights_in")
        s_scat = [dma_sem(f"rows_scattered{b}") for b in range(2)]
        s_xg = [dma_sem(f"slot_rows_in{v}") for v in range(W4)]
        s_yout = [dma_sem(f"slot_rows_out{v}") for v in range(W4)]
        s_got = [dma_sem(f"expert_rows_in{b}") for b in range(2)]
        s_bs = counted("dve", "bias_parts_ready")
        s_mask = counted("dve", "chosen_experts_ready")
        s_pre = counted("pe", "prefix_counts_ready")
        s_slots = counted("dve", "slots_ready")
        s_xst = counted("act", "rows_staged")
        s_ix = counted("pool", "slot_numbers_staged")
        s_xgt = counted("pe", "slot_rows_turned")
        s_xge = counted("act", "slot_rows_turned_in_sbuf")
        s_hh = counted("pe", "slot_hidden_ready")
        s_gg = counted("act", "slot_gate_ready")
        s_yh = counted("dve", "slot_product_ready")
        s_yt = counted("pe", "slot_product_turned")
        s_yte = counted("dve", "slot_product_turned_in_sbuf")
        s_yo = counted("pe", "slot_output_ready")
        s_yoe = counted("act", "slot_output_in_sbuf")
        s_f1 = counted("dve", "expert_rows_added")
        s_rw = dma_sem("router_weights_in")
        s_x2 = counted("dve", "second_layernorm_done")
        s_x2t = counted("pe", "tokens_turned")
        s_x2e = counted("act", "tokens_turned_in_sbuf")
        s_lg = counted("pe", "router_logits_by_expert_ready")
        s_lt = counted("act", "router_logits_by_expert_in_sbuf")
        s_lgt = counted("pe", "router_logits_turned")
        s_el = counted("act", "router_exponentials_ready")
        s_rt = counted("dve", "routing_step")
        s_h = counted("pe", "hidden_ready")
        s_ge = counted("act", "gate_branch_ready")
        s_yy = counted("dve", "hidden_product_ready")
        s_eot = counted("pe", "expert_output_tile_ready")
        s_ac = counted("dve", "expert_output_added")
        s_bn3 = counted("dve", "last_layernorm_stats_step")
        s_sd3 = counted("act", "last_layernorm_deviation_ready")
        s_ri3 = counted("dve", "last_layernorm_scale_ready")
        s_ob = counted("dve", "output_rows_ready")

        COUNTS_READ = 15
        PIN = 3

        block = ctx.enter_context(nc.Block())

        @block.sync
        def _(sp):
            for v in range(W4):
                sp.sem_inc(s_yout[v], 16)
            for u in range(2):
                sp.sem_inc(s_out[u], 16)
                sp.sem_inc(s_sc_out[u], 16)
            sp.dma_start(xT3[:, :, 0:GT], xt_d.rearrange("(k p) n -> p k n", k=KD)[:, :, 0:GT]).then_inc(s_xt[0], 16)
            sp.dma_start(wg3, wg_d.rearrange("(k p) c -> p k c", k=KD)).then_inc(s_wg, 16)
            sp.dma_start(wc3, wc_d.rearrange("(k p) c -> p k c", k=KD)).then_inc(s_cst, 16)
            sp.dma_start(colp[:], col_d).then_inc(s_cst, 16)
            sp.dma_start(consts[:], consts_d).then_inc(s_cst, 16)
            sp.dma_start(rowp[:], row_d.partition_broadcast(P)).then_inc(s_cst, 16)
            for g in range(1, NG):
                sp.dma_start(xT3[:, :, g * GT:(g + 1) * GT],
                             xt_d.rearrange("(k p) n -> p k n", k=KD)[:, :, g * GT:(g + 1) * GT]).then_inc(s_xt[g], 16)
            sp.dma_start(wo3, wo_d.rearrange("(k p) c -> p k c", k=3)).then_inc(s_wo, 16)
            sp.dma_start(wout3, wout_d.rearrange("(k p) c -> p k c", k=KD)).then_inc(s_wo, 16)
            sp.dma_start(x3, x_d.rearrange("(n p) d -> p n d", p=P)).then_inc(s_xn, 16)
            sp.dma_start(ctxn[:].rearrange("p (n c) -> p n c", c=CKV),
                         ctx_d.rearrange("(n p) c -> p n c", p=P)).then_inc(s_xn, 16)
            sp.dma_start(bsp[:, 0:BPC], bias_d).then_inc(s_brow, 16)
            sp.wait_ge(s_bs, at(1))
            sp.wait_ge(s_xn, 32)
            for j in range(0, NSLOT + 2, 2):
                sp.dma_start(slots_dr[j * P:(j + 2) * P].rearrange("(t p) d -> p t d", p=P), over(zero[:], 1, 2)
                             ).then_inc(s_zero_in, 16)
            sp.wait_ge(s_bs, at(6))
            sp.dma_start(bias_dr.rearrange("k (p c) -> p k c", p=P), bsb[:].rearrange("p (k c) -> p k c", k=3)).then_inc(s_brow, 16)
            sp.wait_ge(s_brow, 32)
            sp.dma_start(brow[0:3, :], bias_dr[:, 0:E * 2 * F]).then_inc(s_brow, 16)
            rows = scores_dr.rearrange("n (s r i) (q f c) -> r f q (n s) i c", s=2, r=2, q=2, f=2)

            def store_matrices(i):
                for u in range(2):
                    n = 2 * i + u
                    sp.wait_ge(s_rs, at(n + 1))
                    sp.dma_start(scores_dr[bass.ds(n, 1)].rearrange("n p c -> p (n c)"),
                                 rst[:, u].rearrange("p q f h t -> p (q f h t)")).then_inc(s_sc_out[u], 16)
                    sp.wait_ge(s_as, at(n + 1))
                    sp.dma_start(attend_dr[bass.ds(n, 1)].rearrange("n p c -> p (n c)"),
                                 ast[:, u].rearrange("p h t -> p (h t)")).then_inc(s_sc_out[u], 16)

            blocks = [(r, f) for r in range(2) for f in range(2)]

            def load_blocks(b0, b1, some):
                for u in range(2):
                    sp.wait_ge(s_sc_out[u], b1 // 2 * 16 + 16)
                for r, f in some:
                    p0 = 64 * r + 32 * f
                    sp.dma_start(rb_flat[p0 + b0:p0 + b1].rearrange("p (i c) -> p i c", i=BL), rows[r, f, r, b0:b1]
                                 ).then_inc(s_blk_in, 16)

            with sp.Fori(0, NT // 4) as i:
                store_matrices(i)
            for i in range(NT // 4, NT // 2):
                store_matrices(i)
                k = i - NT // 4
                load_blocks(0, B // 2, blocks[k:k + 1])
            load_blocks(B // 2, B, blocks)
            sp.wait_ge(s_invd, at(64))
            sp.wait_ge(s_invp, at(64))
            for k in range(2):
                b0 = k * B // 2
                for r in range(2):
                    for f in range(2):
                        p0 = 64 * r + 32 * f + b0
                        sp.dma_start(inverse_dr[b0:b0 + B // 2, r, :, f, :],
                                     nb_flat[p0:p0 + B // 2].rearrange("p (i c) -> p i c", i=BL)).then_inc(s_inv_out[k], 16)

            def load_pairs(k):
                for b in range(2):
                    i = 2 * k + b
                    sp.wait_ge(s_o, at(2 * (i - 1)))
                    sp.dma_start(at_s[:, b].rearrange("p u h t -> p u (h t)"),
                                 attend_dr[bass.ds(2 * i, 2)].rearrange("n p c -> p n c")).then_inc(s_pair_in[b], 16)
                    sp.dma_start(roff[:, b].rearrange("p u h t -> p u (h t)"),
                                 scores_dr[bass.ds(2 * i, 2), :, H * BL:].rearrange("n p c -> p n c")).then_inc(s_pair_in[b], 16)
                    sp.dma_start(n32[:, b].rearrange("p u h t -> p u (h t)"),
                                 inverse_dr[bass.ds(4 * i, 4)].rearrange("(n s) r i f c -> (s r i) n (f c)", s=2)
                                 ).then_inc(s_pair_in[b], 16)

            for half in range(2):
                sp.wait_ge(s_inv_out[half], 16 * 4)
                with sp.Fori(0, NT // 8) as k:
                    load_pairs(k + half * NT // 8)
            with sp.Fori(0, NT // 2) as i:
                for u in range(2):
                    n = 2 * i + u
                    sp.wait_ge(s_vb, at(n - 1))
                    sp.wait_ge(s_invp, at(64))
                    for z in range(2):
                        sp.dma_start(vdup[64 * z:64 * z + 64, u],
                                     ctx_d.rearrange("(n s k) c -> n k s c", s=2, k=T)[bass.ds(n, 1)]
                                     .rearrange("n k s c -> (n k) s c")).then_inc(s_vin[u], 16)
            sp.wait_ge(s_og, at(NT))
            sp.wait_ge(s_rsd, at(NT))
            sp.dma_start(wsh, wexp_d[E:NE].rearrange("e p c -> p e c")).then_inc(s_rw, 16)
            sp.dma_start(wab[:].rearrange("p (k e) -> p k e", k=KD),
                         wa_d.rearrange("(k p) e -> p k e", k=KD)).then_inc(s_rw, 16)
            sp.dma_start(brow2[0:3, :], bias_dr[:, E * 2 * F:]).then_inc(s_rw, 16)
            for e in range(0, E, 4):
                sp.dma_start(wres[:, e * EW:(e + 4) * EW].rearrange("p (e c) -> p e c", e=4),
                             wexp_d[e:e + 4].rearrange("e p c -> p e c")).then_inc(s_wr, 16)
            for b in range(2):
                sp.wait_ge(s_scat[b], 16 + 16 * NT)
            def load_rows(i):
                for v in range(W4):
                    sp.wait_ge(s_xgt, at(W4 * (i - 1) + v + 1))
                    sp.dma_start(xg[:, v, :], slots_dr[bass.ds((W4 * i + v) * P, P)]).then_inc(s_xg[v], 16)

            def store_rows(i):
                for v in range(W4):
                    j = W4 * i + v
                    sp.wait_ge(s_yoe, at(j + 1))
                    sp.dma_start(expert_dr[bass.ds(j * P, P)], yob[:, v, :]).then_inc(s_yout[v], 16)

            load_rows(0)
            load_rows(1)
            with sp.Fori(0, NSLOT // W4 - 2) as i:
                load_rows(i + 2)
                store_rows(i)
            store_rows(NSLOT // W4 - 2)
            store_rows(NSLOT // W4 - 1)
            with sp.Fori(0, NT // 8) as i:
                for b in range(2):
                    m = 2 * i + b
                    sp.wait_ge(s_ob, at(m + 1))
                    sp.dma_start(out_d[bass.ds(m * 4 * P, 4 * P)].rearrange("(t p) d -> p t d", p=P),
                                 ob[:, b, :].rearrange("p (t d) -> p t d", t=4)).then_inc(s_out[b], 16)
            for b in range(2):
                sp.wait_ge(s_out[b], 16 * (NT // 8) + 16)
            for v in range(W4):
                sp.wait_ge(s_yout[v], 16 * (NSLOT // W4) + 16)

        @block.tensor
        def _(pe):
            start_counts(pe, "pe")

            def project_gates(g):
                pe.wait_ge(s_xs, at(g + 1))
                alone(pe)
                for m in range(SPG):
                    pe.wait_ge(s_gev, at(SPG * g + m - 1))
                    alone(pe)
                    for k in range(KD):
                        mm = pe.matmul(ps[:, 4 + m % 2, 0:NGATE], xs[:, k, m * P:(m + 1) * P], wg3[:, k, :],
                                       start=(k == 0), stop=(k == KD - 1))
                    mm.then_inc(s_gmm, 1)

            def project_channels(g, tiles):
                for j in tiles:
                    pe.wait_ge(s_conv, at(bank_free(j, g)))
                    alone(pe)
                    for k in range(KD):
                        mm = pe.matmul(ps[0:ROWS[j], BANK[j], :], wc3[:, k, CH0[j]:CH0[j] + ROWS[j]],
                                       xT3[:, k, bass.ds(g * GT, GT)], start=(k == 0), stop=(k == KD - 1))
                    mm.then_inc(s_proj, 1)

            def sum_squares(g):
                pe.wait_ge(s_ssev, at(g))
                alone(pe)
                for j in range(4):
                    pe.wait_ge(s_sq, at(4 * g + j + 1))
                    alone(pe)
                    mm = pe.matmul(ps[32 * j:32 * j + 32, 7, :], consts[0:KR, C_HSEL:C_HSEL + 32], sqs[0:KR, j, :],
                                   start=True, stop=True)
                mm.then_inc(s_ss, 1)

            def turn_values(g, j):
                pe.wait_ge(s_silu, at(NCH * g + 5 + j))
                alone(pe)
                if j == 0:
                    pe.wait_ge(s_n2, at(g))
                    alone(pe)
                else:
                    pe.wait_ge(s_vev, at(3 * g + j))
                    alone(pe)
                for m in range(SPG):
                    mm = pe.transpose(ps[:, 6, m * P:(m + 1) * P], vs[:, j, m * P:(m + 1) * P], ident)
                mm.then_inc(s_vtr, 1)

            def turn_sums(g):
                pe.wait_ge(s_ssev, at(g + 1))
                pe.wait_ge(s_vev, at(3 * g + 3))
                alone(pe)
                for m in range(SPG):
                    mm = pe.transpose(ps[:, 6, m * P:(m + 1) * P], ssb[:, m * P:(m + 1) * P], ident)
                mm.then_inc(s_sst, 1)

            pe.wait_ge(s_wg, 16)
            project_gates(0)
            pe.wait_ge(s_xt[0], 16)
            pe.wait_ge(s_cst, 64)
            project_channels(0, range(NCH))
            for g in range(1, NG):
                pe.wait_ge(s_xt[g], 16)
            project_gates(1)

            def project_and_sum(g):
                project_channels(g + 1, range(4))
                sum_squares(g)
                for j in range(3):
                    project_channels(g + 1, [4 + j])
                    turn_values(g, j)
                turn_sums(g)

            with pe.Fori(0, NG - 2) as i:
                project_and_sum(i)
                project_gates(i + 2)
            project_and_sum(NG - 2)
            sum_squares(NG - 1)
            for j in range(3):
                turn_values(NG - 1, j)
            turn_sums(NG - 1)
            pe.wait_ge(s_n2, at(NG))
            pe.wait_ge(s_gev, at(NT))
            pe.wait_ge(s_conv, at(NCH * NG))
            pe.wait_ge(s_idb, at(3))
            alone(pe)
            with pe.Fori(0, NT // 2) as i:
                for u in range(2):
                    n = 2 * i + u
                    pe.wait_ge(s_gst, at(n + 1))
                    pe.wait_ge(s_e, at(n - 1))
                    alone(pe)
                    pe.matmul(ps[:, u, 0:H * T], consts[:, C_LTRI:C_LTRI + P],
                              gst[:, u].rearrange("p h t -> p (h t)"), start=True, stop=False)
                    pe.matmul(ps[:, u, 0:H * T], idb[:], over(negb[:, 0:T], 1, H),
                              start=False, stop=True).then_inc(s_dmm, 1)
                    pe.wait_ge(s_kst, at(n + 1))
                    pe.wait_ge(s_kblk, at(n + 1))
                    pe.wait_ge(s_qblk, at(n + 1))
                    pe.wait_ge(s_as, at(n - 1))
                    alone(pe)
                    for f in range(2):
                        for s in range(2):
                            mm = pe.matmul(ps[64 * s:64 * s + 64, 2 + 2 * u + f, 0:2 * HH * T],
                                           kst[0:KR, u, f, 64 * s:64 * s + 64],
                                           blk[0:KR, u, f, :, :, 64 * s:64 * s + 64].rearrange("p q h n -> p (q h) n"),
                                           start=True, stop=True)
                    mm.then_inc(s_kmm, 1)
            pe.wait_ge(s_as, at(NT))
            pe.wait_ge(s_pw, at(1))
            pe.wait_ge(s_zero, at(3))
            alone(pe)
            def solve_blocks(k, b):
                i = 2 * k + b
                for u in range(2):
                    n = 2 * i + u
                    pe.wait_ge(s_vp, at(n + 1))
                    pe.wait_ge(s_pair_in[b], 16 * PIN * (k + 1))
                    pe.wait_ge(s_xr, at(n - 3))
                    alone(pe)
                    for h in range(H):
                        for q in range(4):
                            r = slice(32 * q, 32 * q + 32)
                            mm = pe.matmul(ps[r, u, h * DV:(h + 1) * DV], n32[r, b, u, h, :], vp[r, u, h, :],
                                           start=True, stop=True)
                    mm.then_inc(s_w0, 1)

            def couple(k, b):
                i = 2 * k + b
                for u in range(2):
                    n = 2 * i + u
                    pe.wait_ge(s_w, at(n + 1))
                    pe.wait_ge(s_y, at(n - 1))
                    alone(pe)
                    for h in range(H):
                        for s in range(2):
                            mm = pe.matmul(ps[64 * s + 32:64 * s + 64, 2 + u, h * DV:(h + 1) * DV],
                                           roff[64 * s:64 * s + 32, b, u, h, :],
                                           wsol[64 * s:64 * s + 32, u, h * DV:(h + 1) * DV], start=True, stop=True)
                    mm.then_inc(s_y0, 1)

            def correct(k, b):
                i = 2 * k + b
                for u in range(2):
                    n = 2 * i + u
                    pe.wait_ge(s_y, at(n + 1))
                    pe.wait_ge(s_w2, at(n - 1))
                    alone(pe)
                    for h in range(H):
                        for s in range(2):
                            r = slice(64 * s + 32, 64 * s + 64)
                            mm = pe.matmul(ps[r, 4 + u, h * DV:(h + 1) * DV], n32[r, b, u, h, :],
                                           ysb[r, u, h * DV:(h + 1) * DV], start=True, stop=True)
                    mm.then_inc(s_z, 1)

            def attend(k, b):
                i = 2 * k + b
                for u in range(2):
                    n = 2 * i + u
                    pe.wait_ge(s_w2, at(n + 1))
                    pe.wait_ge(s_ote, at(n - 1))
                    alone(pe)
                    for h in range(H):
                        for s in range(2):
                            r = slice(64 * s, 64 * s + 64)
                            mm = pe.matmul(ps[r, 6 + u, h * DV:(h + 1) * DV], at_s[r, b, u, h, :],
                                           wsol[r, u, h * DV:(h + 1) * DV], start=True, stop=True)
                    mm.then_inc(s_o, 1)

            def turn_heads(i):
                for u in range(2):
                    n = 2 * i + u
                    pe.wait_ge(s_og2, at(n + 1))
                    alone(pe)
                    for k in range(3):
                        mm = pe.transpose(ps[:, 6 + u, k * P:(k + 1) * P], og[:, u, k * P:(k + 1) * P], ident)
                    mm.then_inc(s_ot, 1)

            def project(i):
                for u in range(2):
                    n = 2 * i + u
                    pe.wait_ge(s_ote, at(n + 1))
                    alone(pe)
                    for k in range(3):
                        mm = pe.matmul(ps[:, u, 0:D], ogT[:, u, k, :], wo3[:, k, :], start=(k == 0), stop=(k == 2))
                    mm.then_inc(s_xo, 1)

            def solve_and_project(i, k, b):
                solve_blocks(k, b)
                couple(k, b)
                correct(k, b)
                turn_heads(i)
                project(i)
                attend(k, b)

            solve_blocks(0, 0)
            couple(0, 0)
            correct(0, 0)
            attend(0, 0)
            with pe.Fori(0, NT // 4 - 1) as k:
                solve_and_project(2 * k, k, 1)
                solve_and_project(2 * k + 1, k + 1, 0)
            solve_and_project(NT // 2 - 2, NT // 4 - 1, 1)
            turn_heads(NT // 2 - 1)
            project(NT // 2 - 1)
            pe.wait_ge(s_xr, at(NT))
            pe.wait_ge(s_og, at(NT))
            alone(pe)

            def turn_keys_queries(i):
                for u in range(2):
                    n = 2 * i + u
                    pe.wait_ge(s_kx, at(n + 1))
                    pe.wait_ge(s_qr, at(3 * n + 3))
                    pe.wait_ge(s_xr2, at(n - 5))
                    alone(pe)
                    for w, src in enumerate((kx, qr)):
                        for f in range(2):
                            c = 2 * P * w + P * f
                            mm = pe.transpose(ps[:, u, c:c + P], src[:, u, f * P:(f + 1) * P], ident)
                    mm.then_inc(s_kqt, 1)

            def score(i):
                for u in range(2):
                    n = 2 * i + u
                    pe.wait_ge(s_kqe, at(n + 1))
                    pe.wait_ge(s_kb, at(n + 1))
                    alone(pe)
                    pe.wait_ge(s_sub, at(n - 1))
                    alone(pe)
                    for f in range(2):
                        bank = 2 + 2 * u + f
                        pe.matmul(ps[:, bank, :], idb[:], over(causb, 1, 8), start=True, stop=False)
                        for s in range(2):
                            q = slice(64 * s, 64 * s + 64)
                            mm = pe.matmul(ps[q, bank, :], kqT[:, u, 1, f, q], kblk[:, u, f, :, q],
                                           start=False, stop=True)
                        mm.then_inc(s_sc, 1)

            def turn_probabilities(i):
                for u in range(2):
                    n = 2 * i + u
                    for f in range(2):
                        pe.wait_ge(s_pr, at(n + 1))
                        pe.wait_ge(s_pte, at(2 * n + f - 1))
                        alone(pe)
                        for c in range(4):
                            mm = pe.transpose(ps[:, 6 + f, c * P:(c + 1) * P],
                                              prob[:, u, f, 2 * c:2 * c + 2, :].rearrange("p h k -> p (h k)"), ident)
                        mm.then_inc(s_pt, 1)

            def attend_softmax(i, last=False):
                for u in range(2):
                    n = 2 * i + u
                    pe.wait_ge(s_vb, at(n + 1))
                    if not last:
                        pe.wait_ge(s_kqe, at(n + 5))
                    alone(pe)
                    for f in range(2):
                        pe.wait_ge(s_pte, at(2 * n + f + 1))
                        alone(pe)
                        for s in range(2):
                            for c in range(4):
                                q = slice(c * P + 64 * s, c * P + 64 * s + 64)
                                mm = pe.matmul(ps[32 * c:32 * c + 32, u, f * P + 64 * s:f * P + 64 * s + 64],
                                               vblk[:, u, s, 2 * f + c // 2, :], probT[:, u, f, q], start=True, stop=True)
                    mm.then_inc(s_pv, 1)

            def project_softmax(i):
                for u in range(2):
                    n = 2 * i + u
                    pe.wait_ge(s_ove, at(n + 1))
                    alone(pe)
                    for k in range(KD):
                        mm = pe.matmul(ps[:, u, D:2 * D], oT[:, u, k, :], wout3[:, k, :], start=(k == 0), stop=(k == KD - 1))
                    mm.then_inc(s_xp, 1)

            turn_keys_queries(0)
            score(0)
            turn_keys_queries(1)
            with pe.Fori(0, NT // 2 - 2) as i:
                score(i + 1)
                turn_keys_queries(i + 2)
                turn_probabilities(i)
                attend_softmax(i)
                project_softmax(i)
            score(NT // 2 - 1)
            turn_probabilities(NT // 2 - 2)
            attend_softmax(NT // 2 - 2, last=True)
            project_softmax(NT // 2 - 2)
            turn_probabilities(NT // 2 - 1)
            attend_softmax(NT // 2 - 1, last=True)
            project_softmax(NT // 2 - 1)
            for g in range(NG + 2):
                if g < NG:
                    for t in range(SPG):
                        n = SPG * g + t
                        pe.wait_ge(s_x2, at(n + 1))
                        if g > 0:
                            pe.wait_ge(s_x2e, at(n - SPG + 1))
                        for k in range(KD):
                            mm = pe.transpose(ps[:, 2 + t, k * P:(k + 1) * P], xn[:, n * D + k * P:n * D + (k + 1) * P], ident)
                        mm.then_inc(s_x2t, 1)
                if g == 1:
                    pe.wait_ge(s_rw, 48)
                    pe.wait_ge(s_xr2, at(NT))
                if 1 <= g <= NG:
                    pe.wait_ge(s_x2e, at(SPG * g))
                    if g > 2:
                        pe.wait_ge(s_lt, at(g - 2))
                    for k in range(KD):
                        mm = pe.matmul(ps[0:E, g % 2, :], wab[:, k * E:(k + 1) * E], x2T3[:, k, (g - 1) * GT:g * GT],
                                       start=(k == 0), stop=(k == KD - 1))
                    mm.then_inc(s_lg, 1)
                if g >= 2:
                    pe.wait_ge(s_lt, at(g - 1))
                    for t in range(SPG):
                        n = SPG * (g - 2) + t
                        mm = pe.transpose(ps[:, 6, n * E:(n + 1) * E], logitT[:, n * P:(n + 1) * P], ident[0:E, 0:E])
                    mm.then_inc(s_lgt, 1)

            def shared_hidden(g):
                for e in range(SH):
                    if g > 0:
                        pe.wait_ge(s_yy, at(SH * (g - 1) + e + 1))
                    for w in range(2):
                        for c in range(KD):
                            o = w * KD * F + c * F
                            mm = pe.matmul(ps[:, 2 * w + e, :], wsh[:, e, o:o + F], x2T3[:, c, g * GT:(g + 1) * GT],
                                           start=(c == 0), stop=(c == KD - 1))
                    mm.then_inc(s_h, 1)

            def shared_outputs(g):
                pe.wait_ge(s_yy, at(SH * (g + 1)))
                for t in range(SPG):
                    if g > 0:
                        pe.wait_ge(s_ac, at(SPG * (g - 1) + t + 1))
                    o = ps[:, 4 + t, 0:D]
                    for e in range(SH):
                        pe.matmul(o, onesb[0:3, :], brow2[0:3, (E + e) * D:(E + e + 1) * D], start=(e == 0), stop=False)
                    for e in range(SH):
                        mm = pe.matmul(o, ybf[:, e, t * P:(t + 1) * P], wsh[:, e, 2 * KD * F:EW],
                                       start=False, stop=(e == SH - 1))
                    mm.then_inc(s_eot, 1)

            shared_hidden(0)
            pe.wait_ge(s_el, at(1))
            pe.wait_ge(s_mask, at(1))
            pe.matmul(ps[:, 6, 0:NT * E], consts[:, C_PRE:C_PRE + P], chosen.rearrange("p n e -> p (n e)"),
                      start=True, stop=True)
            pe.matmul(ps[:, 7, 0:NT * E], consts[:, C_ONE:C_ONE + P], chosen.rearrange("p n e -> p (n e)"),
                      start=True, stop=True).then_inc(s_pre, 1)
            shared_hidden(1)
            pe.wait_ge(s_rt, at(COUNTS_READ))
            for g in range(NG):
                shared_outputs(g)
                if g + 2 < NG:
                    shared_hidden(g + 2)
            pe.wait_ge(s_ac, at(NT))
            pe.wait_ge(s_yy, at(SH * NG))
            pe.wait_ge(s_wr, 64)
            pe.wait_ge(s_brow, 48)
            pe.wait_ge(s_slots, at(3))

            def turn_rows(i):
                for v in range(W4):
                    pe.wait_ge(s_xg[v], 16 * (i + 1))
                    if v == 0:
                        pe.wait_ge(s_yoe, at(W4 * (i - 1)))
                    alone(pe)
                    for k in range(KD):
                        mm = pe.transpose(ps[:, 2 * v, k * P:(k + 1) * P], xg[:, v, k * P:(k + 1) * P], ident)
                    mm.then_inc(s_xgt, 1)

            def hidden(i):
                which = []
                for v in range(W4):
                    j = W4 * i + v
                    e = pe.value_load(expert_i[0:1, bass.ds(j, 1)], min_val=0, max_val=(E - 1) * D)
                    which.append(e)
                    pe.wait_ge(s_xge, at(j + 1))
                    alone(pe)
                    h = ps[:, 2 * v + 1, 0:2 * F]
                    pe.matmul(h, onesb[0:3, :], brow[0:3, bass.ds(e, 2 * F)], start=True, stop=False)
                    for k in range(KD):
                        mm = pe.matmul(h, xgT[:, v, k, :],
                                       wres[:, bass.ds(e * (EW // D) + k * 2 * F, 2 * F)], start=False, stop=(k == KD - 1))
                    mm.then_inc(s_hh, 1)
                return which

            def turn_products(i):
                for v in range(W4):
                    j = W4 * i + v
                    pe.wait_ge(s_yh, at(j + 1))
                    alone(pe)
                    pe.transpose(ps[:, 2 * v + 1, 0:P], yhb[:, v, :], ident).then_inc(s_yt, 1)

            def outputs(i, which, last=False):
                for v in range(W4):
                    j = W4 * i + v
                    e = which[v]
                    pe.wait_ge(s_yte, at(j + 1))
                    if v == 0 and not last:
                        pe.wait_ge(s_xge, at(W4 * (i + 2)))
                    alone(pe)
                    o = ps[:, 2 * v, 0:D]
                    pe.matmul(o, onesb[0:3, :], brow2[0:3, bass.ds(e, D)], start=True, stop=False)
                    pe.matmul(o, yTb[:, v, :], wres[:, bass.ds(e * (EW // D) + 2 * KD * F, D)],
                              start=False, stop=True).then_inc(s_yo, 1)

            turn_rows(0)

            def slot_tiles(i):
                which = hidden(i)
                turn_rows(i + 1)
                turn_products(i)
                outputs(i, which)

            with pe.Fori(0, (NSLOT // W4 - 1) // 2) as k:
                slot_tiles(2 * k)
                slot_tiles(2 * k + 1)
            slot_tiles(NSLOT // W4 - 2)
            which = hidden(NSLOT // W4 - 1)
            turn_products(NSLOT // W4 - 1)
            outputs(NSLOT // W4 - 1, which, last=True)

        @block.scalar
        def _(act):
            start_counts(act, "act")
            act.wait_ge(s_cst, 64)

            def keep_gates(g):
                for m in range(SPG):
                    n = SPG * g + m
                    act.wait_ge(s_gmm, at(n + 1))
                    act.activation(sg[:, bass.ds(n * HV, HV)], ps[:, 4 + m % 2, 0:HV], ACT.Silu)
                    act.activation(ab[:, bass.ds(n * 2 * H, 2 * H)], ps[:, 4 + m % 2, HV:NGATE],
                                   ACT.Copy).then_inc(s_gev, 1)

            def first_tap(g, j):
                act.wait_ge(s_proj, at(NCH * g + j + 1))
                act.wait_ge(s_silu, at(bank_free(j, g)))
                act.activation(ybuf[0:ROWS[j], BANK[j], :], ps[0:ROWS[j], BANK[j], :], ACT.Copy,
                               scale=taps[0:ROWS[j], j, KSZ - 1:KSZ]).then_inc(s_tap0, 1)

            def silu(g, j):
                act.wait_ge(s_conv, at(NCH * g + j + 1))
                if j < 4:
                    dst = arena[0:KR, bass.ds(g * GT + j * NTOK, GT)]
                else:
                    dst = vs[:, j - 4, :]
                    act.wait_ge(s_vtr, at(3 * (g - 1) + j - 3))
                act.activation(dst, ybuf[0:ROWS[j], BANK[j], :], ACT.Silu).then_inc(s_silu, 1)

            def keep_squares(g):
                act.wait_ge(s_ss, at(g + 1))
                act.wait_ge(s_sst, at(g))
                act.activation(ssb, ps[:, 7, :], ACT.Copy).then_inc(s_ssev, 1)

            def keep_values(g, j):
                act.wait_ge(s_vtr, at(3 * g + j + 1))
                act.activation(
                    vt[:, bass.ds(SPG * HV * g, SPG * HV)].rearrange("p (m c) -> p m c", m=SPG)[:, :, j * P:(j + 1) * P],
                    ps[:, 6, :].rearrange("p (m c) -> p m c", m=SPG), ACT.Copy).then_inc(s_vev, 1)

            def first_channels(g):
                for j in range(4):
                    first_tap(g, j)

            def last_channels(g):
                for j in range(4, NCH):
                    silu(g, j - 4)
                    first_tap(g, j)
                for j in range(NCH - 4, NCH):
                    silu(g, j)

            keep_gates(0)
            first_channels(0)
            last_channels(0)
            keep_gates(1)
            act.wait_ge(s_zero, at(2))
            act.wait_ge(s_kd, at(2))
            act.activation(rk, rk, ACT.Sqrt, bias=eps, scale=1.0 / CKV).then_inc(s_ka, 1)

            def channels_and_values(g):
                first_channels(g + 1)
                keep_squares(g)
                for j in range(3):
                    silu(g + 1, j)
                    first_tap(g + 1, 4 + j)
                    keep_values(g, j)
                for j in range(NCH - 4, NCH):
                    silu(g + 1, j)

            with act.Fori(0, NG - 2) as i:
                channels_and_values(i)
                keep_gates(i + 2)
            channels_and_values(NG - 2)
            keep_squares(NG - 1)
            for j in range(3):
                keep_values(NG - 1, j)

            a_t, b_t = tab(T_A), tab(T_B)
            act.wait_ge(s_gd, at(2))
            act.activation(a_t, a_t, ACT.Exp, scale=-1.0).then_inc(s_gk, 1)
            act.activation(b_t, ab3[:, :, H:2 * H], ACT.Exp, scale=-1.0).then_inc(s_gk, 1)
            act.activation(rowp[:, R_ALOG:R_ALOG + H], rowp[:, R_ALOG:R_ALOG + H], ACT.Exp).then_inc(s_gk, 1)
            act.wait_ge(s_gk, at(1))
            act.activation(a_t, a_t, ACT.Ln, bias=1.0).then_inc(s_gk, 1)
            act.wait_ge(s_gd, at(5))
            act.activation(tab(T_NK).rearrange("p (n h) -> p n h", h=H), n23[:, :, H:2 * H],
                           ACT.Sqrt).then_inc(s_gk, 1)
            act.activation(tab(T_RQ).rearrange("p (n h) -> p n h", h=H), n23[:, :, 0:H],
                           ACT.Sqrt, scale=float(DK)).then_inc(s_gk, 1)
            with act.Fori(0, NT // 2) as i:
                for u in range(2):
                    n = 2 * i + u
                    act.wait_ge(s_kmm, at(n - 1))
                    for f in range(2):
                        ins = act.activation(kst[0:KR, u, f, :], arena[0:KR, bass.ds(n * P + (2 + f) * NTOK, P)], ACT.Copy)
                    ins.then_inc(s_kst, 1)
                    act.wait_ge(s_dmm, at(n + 1))
                    act.wait_ge(s_as, at(n - 1))
                    act.activation(est[:, u].rearrange("p h t -> p (h t)"), ps[:, u, 0:H * T], ACT.Exp).then_inc(s_e, 1)
            act.wait_ge(s_zero, at(3))
            def keep_solves(i):
                for u in range(2):
                    n = 2 * i + u
                    act.wait_ge(s_w0, at(n + 1))
                    act.wait_ge(s_o, at(n - 1))
                    act.activation(wsol[:, u, :], ps[:, u, 0:HV], ACT.Copy).then_inc(s_w, 1)

            def keep_coupling(i):
                for u in range(2):
                    n = 2 * i + u
                    act.wait_ge(s_y0, at(n + 1))
                    act.wait_ge(s_z, at(n - 1))
                    act.activation(ysb[:, u, :], ps[:, 2 + u, 0:HV], ACT.Copy).then_inc(s_y, 1)

            def square_heads(i):
                for u in range(2):
                    n = 2 * i + u
                    act.wait_ge(s_og, at(n + 1))
                    act.wait_ge(s_ms, at(n - 1))
                    act.activation(osq[:, u, :], og[:, u, :], ACT.Square).then_inc(s_osq, 1)

            def head_roots(i):
                for u in range(2):
                    n = 2 * i + u
                    act.wait_ge(s_ms, at(n + 1))
                    act.activation(ms[:, u, :], ms[:, u, :], ACT.Sqrt, bias=eps, scale=1.0 / DV).then_inc(s_rms, 1)

            def keep_heads(i):
                for u in range(2):
                    n = 2 * i + u
                    act.wait_ge(s_ot, at(n + 1))
                    act.wait_ge(s_xo, at(n - 1))
                    act.activation(ogT[:, u].rearrange("p k n -> p (k n)"), ps[:, 6 + u, 0:3 * P], ACT.Copy).then_inc(s_ote, 1)

            def deviations(i):
                for u in range(2):
                    n = 2 * i + u
                    act.wait_ge(s_bn, at(2 * n + 2))
                    act.activation(sd[:, u, :], mv[:, u, 1:2], ACT.Sqrt, bias=eps).then_inc(s_sd, 1)

            keep_solves(0)
            keep_coupling(0)
            square_heads(0)
            head_roots(0)
            with act.Fori(0, NT // 2 - 1) as i:
                keep_solves(i + 1)
                keep_coupling(i + 1)
                keep_heads(i)
                deviations(i)
                square_heads(i + 1)
                head_roots(i + 1)
            keep_heads(NT // 2 - 1)
            deviations(NT // 2 - 1)
            act.wait_ge(s_x1, at(NT))
            act.wait_ge(s_rq, at(NT))
            act.activation(rq_tab, rq_tab, ACT.Sqrt, bias=eps16, scale=float(HD)).then_inc(s_rqa, 1)
            def keep_keys_queries(i):
                for u in range(2):
                    n = 2 * i + u
                    act.wait_ge(s_kqt, at(n + 1))
                    act.wait_ge(s_kb, at(n - 1))
                    act.wait_ge(s_sc, at(2 * (n - 1)))
                    act.activation(kqT[:, u].rearrange("p w f n -> p (w f n)"), ps[:, u, :], ACT.Copy).then_inc(s_kqe, 1)

            def exponentials(i):
                for u in range(2):
                    n = 2 * i + u
                    act.wait_ge(s_sub, at(n + 1))
                    alone(act)
                    act.activation(prob_u[:, u], prob_u[:, u], ACT.Exp, scale=rq_tab[:, bass.ds(n, 1)]).then_inc(s_exp, 1)

            def keep_probabilities(i):
                for u in range(2):
                    n = 2 * i + u
                    for f in range(2):
                        act.wait_ge(s_pt, at(2 * n + f + 1))
                        act.wait_ge(s_pv, at(n - 1))
                        act.activation(probT[:, u, f, :], ps[:, 6 + f, :], ACT.Copy).then_inc(s_pte, 1)

            def keep_attended(i):
                for u in range(2):
                    n = 2 * i + u
                    act.wait_ge(s_pv, at(n + 1))
                    act.wait_ge(s_xp, at(n - 1))
                    act.activation(oT[:, u].rearrange("p f n -> p (f n)"), ps[:, u, 0:D], ACT.Copy).then_inc(s_ove, 1)

            def spread_keys(i):
                for u in range(2):
                    n = 2 * i + u
                    act.wait_ge(s_kqt, at(n - 1))
                    alone(act)
                    act.activation(kx[:, u, :].rearrange("p (g r c) -> p g r c", g=NKV, r=4),
                                   over(krope[:, bass.ds(n * CKV, CKV)].rearrange("p (g c) -> p g c", g=NKV), 2, 4),
                                   ACT.Copy).then_inc(s_kx, 1)

            def block_values(i):
                for u in range(2):
                    n = 2 * i + u
                    act.wait_ge(s_vin[u], 32 * (i + 1))
                    act.wait_ge(s_pv, at(n - 1))
                    for z in range(2):
                        for s in range(2):
                            ins = act.activation(vblk[:, u, s].rearrange("p g (z c) -> p g z c", z=2)[:, :, z],
                                                 vdup[:, u, s].rearrange("p (g c) -> p g c", g=NKV), ACT.Copy,
                                                 scale=consts[:, C_VM + z * HD:C_VM + z * HD + 1])
                    ins.then_inc(s_vb, 1)

            act.wait_ge(s_kp, at(16))
            act.wait_ge(s_rqd, at(1))
            spread_keys(0)
            keep_keys_queries(0)
            spread_keys(1)
            block_values(0)
            exponentials(0)
            keep_keys_queries(1)
            with act.Fori(0, NT // 2 - 2) as i:
                spread_keys(i + 2)
                keep_keys_queries(i + 2)
                keep_probabilities(i)
                keep_attended(i)
                block_values(i + 1)
                exponentials(i + 1)
            keep_probabilities(NT // 2 - 2)
            keep_attended(NT // 2 - 2)
            block_values(NT // 2 - 1)
            exponentials(NT // 2 - 1)
            act.wait_ge(s_mv2, at((NT - SPG) // 2))
            act.activation(sd2[:, 0:NT - SPG], mv2[:, 0:NT - SPG, 1], ACT.Sqrt, bias=eps).then_inc(s_ln2a, 1)
            keep_probabilities(NT // 2 - 1)
            keep_attended(NT // 2 - 1)
            act.wait_ge(s_mv2, at(NT // 2))
            act.activation(sd2[:, NT - SPG:NT], mv2[:, NT - SPG:NT, 1], ACT.Sqrt, bias=eps).then_inc(s_ln2a, 1)
            for g in range(NG + 1):
                if g < NG:
                    for t in range(SPG):
                        n = SPG * g + t
                        act.wait_ge(s_x2t, at(n + 1))
                        act.activation(x2T3[:, :, n * P:(n + 1) * P], ps[:, 2 + t, 0:D].rearrange("p (k n) -> p k n", k=KD),
                                       ACT.Copy).then_inc(s_x2e, 1)
                if g > 0:
                    act.wait_ge(s_lg, at(g))
                    act.activation(logitT[:, (g - 1) * GT:g * GT], ps[0:E, g % 2, :], ACT.Copy).then_inc(s_lt, 1)
            act.wait_ge(s_lgt, at(NG))
            act.activation(elog_flat, ps[:, 6, 0:NT * E], ACT.Exp, scale=-1.0).then_inc(s_el, 1)

            def stage_rows(m):
                if m >= 2:
                    act.wait_ge(s_scat[m % 2], 128 * (m // 2) + 16)
                act.activation(xst[:, m % 2, :], xn[:, m * 4 * D:(m + 1) * 4 * D], ACT.Copy).then_inc(s_xst, 1)

            act.wait_ge(s_x2, at(NT))
            stage_rows(0)
            stage_rows(1)
            for g in range(NG):
                for e in range(SH):
                    m = SH * g + e
                    act.wait_ge(s_h, at(m + 1))
                    if g > 0:
                        act.wait_ge(s_yy, at(m - 1))
                    act.activation(hbuf[:, e, :], ps[:, e, :], ACT.Gelu,
                                   bias=colp[:, E + e + W_GB:E + e + W_GB + 1]).then_inc(s_ge, 1)
                if 1 <= g < NG - 1:
                    stage_rows(g + 1)

            def keep_rows(i):
                for v in range(W4):
                    j = W4 * i + v
                    act.wait_ge(s_xgt, at(j + 1))
                    act.wait_ge(s_hh, at(j - W4 + 1))
                    act.activation(xgT[:, v].rearrange("p k n -> p (k n)"), ps[:, 2 * v, 0:D], ACT.Copy).then_inc(s_xge, 1)

            def gates(i):
                for v in range(W4):
                    j = W4 * i + v
                    act.wait_ge(s_hh, at(j + 1))
                    act.wait_ge(s_yh, at(j - W4 + 1))
                    act.activation(geb[:, v, :], ps[:, 2 * v + 1, 0:F], ACT.Gelu).then_inc(s_gg, 1)

            def keep_outputs(i):
                for v in range(W4):
                    j = W4 * i + v
                    act.wait_ge(s_yo, at(j + 1))
                    act.wait_ge(s_yout[v], 16 * i + 16)
                    act.activation(yob[:, v, :], ps[:, 2 * v, 0:D], ACT.Copy).then_inc(s_yoe, 1)

            keep_rows(0)
            with act.Fori(0, NSLOT // W4 - 1) as i:
                gates(i)
                keep_rows(i + 1)
                keep_outputs(i)
            gates(NSLOT // W4 - 1)
            keep_outputs(NSLOT // W4 - 1)
            with act.Fori(0, NT // 8) as i:
                for b in range(2):
                    m = 2 * i + b
                    act.wait_ge(s_bn3, at(8 * (m + 1)))
                    act.wait_ge(s_ri3, at(m - 1))
                    act.activation(sd3[:, b, :], mv3[:, b, :, 1], ACT.Sqrt, bias=eps).then_inc(s_sd3, 1)

        @block.vector
        def _(dve):
            start_counts(dve, "dve")
            dve.wait_ge(s_cst, 64)
            dve.memset(zero[:], 0.0).then_inc(s_bs, 1)
            dve.memset(onesb[:], 1.0).then_inc(s_idb, 1)
            dve.tensor_copy(idb[:], ident).then_inc(s_idb, 1)
            dve.tensor_copy(negb[:], consts[:, C_NEG:C_NEG + 2 * T]).then_inc(s_idb, 1)

            def convolve(g, tiles):
                for j in tiles:
                    m = NCH * g + j
                    r = ROWS[j]
                    y = ybuf[0:r, BANK[j], :].rearrange("p (s t) -> p s t", t=T)
                    z = ps[0:r, BANK[j], :].rearrange("p (s t) -> p s t", t=T)
                    dve.wait_ge(s_tap0, at(m + 1))
                    for d in range(1, KSZ):
                        if d > 1:
                            dve.wait_ge(s_tap, at(2 * m + d - 1))
                        dve.scalar_tensor_tensor(y[:, :, d:T], z[:, :, 0:T - d], taps[0:r, j, KSZ - 1 - d:KSZ - d],
                                                 y[:, :, d:T], ALU.mult, ALU.add
                                                 ).then_inc(s_tap if d < KSZ - 1 else s_conv, 1)

            def keep_sums(g):
                dve.wait_ge(s_sst, at(g + 1))
                for f in range(2):
                    ins = dve.tensor_copy(
                        n2[:, bass.ds(SPG * 2 * H * g, SPG * 2 * H)].rearrange(
                            "p (m q f h) -> p m q f h", m=SPG, q=2, f=2)[:, :, :, f, :],
                        ps[:, 6, :].rearrange("p (m q f c) -> p m q f c", m=SPG, q=2, f=2)[:, :, :, f, 0:HH])
                ins.then_inc(s_n2, 1)

            convolve(0, range(NCH))
            dve.wait_ge(s_xn, 32)
            dve.memset(eps, 1e-5).then_inc(s_zero, 1)
            dve.memset(eps16, HD * 1e-5).then_inc(s_zero, 1)
            dve.tensor_tensor(ksq, ctxn[:], ctxn[:], ALU.mult).then_inc(s_kd, 1)
            dve.wait_ge(s_kd, at(1))
            dve.tensor_reduce(rk, ksq.rearrange("p (n c) -> p n c", c=CKV), AXX, ALU.add).then_inc(s_kd, 1)
            dve.wait_ge(s_brow, 16)
            for k in range(3):
                if k > 0:
                    dve.wait_ge(s_bs, at(2 * k))
                    dve.tensor_tensor(bsp[:, k * BPC:(k + 1) * BPC], bsp[:, (k - 1) * BPC:k * BPC],
                                      bsb[:, (k - 1) * BPC:k * BPC], ALU.subtract).then_inc(s_bs, 1)
                    dve.wait_ge(s_bs, at(2 * k + 1))
                dve.tensor_copy(bsb[:, k * BPC:(k + 1) * BPC], bsp[:, k * BPC:(k + 1) * BPC]).then_inc(s_bs, 1)
            dve.wait_ge(s_ka, at(1))
            dve.reciprocal(rk, rk).then_inc(s_kd, 1)
            dve.wait_ge(s_kd, at(3))
            dve.tensor_tensor(ctx3, ctx3, over(rk, 2, CKV), ALU.mult).then_inc(s_kd, 1)
            with dve.Fori(0, NG - 1) as i:
                convolve(i + 1, range(NCH - 1))
                keep_sums(i)
                convolve(i + 1, [NCH - 1])
            keep_sums(NG - 1)
            a_t = tab(T_A).rearrange("p (n h) -> p n h", h=H)
            g_t = tab(T_G).rearrange("p (n h) -> p n h", h=H)
            c_t, b_t = tab(T_C), tab(T_B)
            dve.wait_ge(s_gev, at(NT))
            dve.tensor_tensor(g_t, ab3[:, :, 0:H], over(rowp[:, R_DT:R_DT + H], 1, NT), ALU.add).then_inc(s_gd, 1)
            dve.wait_ge(s_gd, at(1))
            dve.scalar_tensor_tensor(a_t, g_t, -1.0, g_t, ALU.mult, ALU.max).then_inc(s_gd, 1)
            dve.wait_ge(s_gd, at(2))
            dve.tensor_scalar(g_t, g_t, 0.0, None, ALU.max).then_inc(s_gd, 1)
            dve.wait_ge(s_n2, at(NG))
            dve.tensor_scalar(n2[:], n2[:], 1e-6, None, ALU.add).then_inc(s_gd, 1)
            dve.wait_ge(s_gd, at(4))
            dve.tensor_copy(c_t.rearrange("p (n h) -> p n h", h=H), n23[:, :, H:2 * H]).then_inc(s_gd, 1)
            dve.wait_ge(s_gk, at(4))
            dve.tensor_tensor(g_t, g_t, a_t, ALU.add).then_inc(s_gd, 1)
            dve.wait_ge(s_gd, at(6))
            dve.scalar_tensor_tensor(g_t, g_t, -1.0, over(rowp[:, R_ALOG:R_ALOG + H], 1, NT),
                                     ALU.mult, ALU.mult).then_inc(s_gd, 1)
            dve.scalar_tensor_tensor(c_t, b_t, 1.0, c_t, ALU.add, ALU.mult).then_inc(s_gd, 1)
            dve.wait_ge(s_gd, at(8))
            dve.reciprocal(c_t, c_t).then_inc(s_gd, 1)
            dve.wait_ge(s_gk, at(6))
            dve.reciprocal(tab(T_RQ), tab(T_RQ)).then_inc(s_gd, 1)
            dve.wait_ge(s_gd, at(9))

            def query_blocks(n, u):
                dve.wait_ge(s_kmm, at(n - 1))
                for f in range(2):
                    ins = dve.tensor_tensor(blk[0:KR, u, f, 1], over(arena[0:KR, bass.ds(n * P + f * NTOK, P)], 1, HH),
                                            over(consts[0:KR, C_HM:C_HM + HH], 2, P), ALU.mult)
                ins.then_inc(s_qblk, 1)

            def matrices(i, u):
                n = 2 * i + u
                dve.wait_ge(s_e, at(n + 1))
                dve.tensor_tensor(est[:, u], est[:, u], over(small[:, bass.ds(n * H + T_C * NT * H, H)], 2, T),
                                  ALU.mult).then_inc(s_ec, 1)
                dve.wait_ge(s_ec, at(n + 1))
                dve.wait_ge(s_kmm, at(n + 1))
                prod = ps[:, 2 + 2 * u:4 + 2 * u, 0:2 * HH * T].rearrange("p f (q c) -> p f q c", q=2)
                e2 = est[:, u].rearrange("p (f h) t -> p f (h t)", f=2)
                dve.wait_ge(s_sc_out[u], 32 * i + 16)
                for f in range(2):
                    ins = dve.tensor_tensor(rst[:, u, :, f].rearrange("p q h t -> p h q t"),
                                            prod[:, f, 0].rearrange("p (h q t) -> p h q t", h=HH, q=2),
                                            e2[:, f].rearrange("p (h q t) -> p h q t", h=HH, q=2), ALU.mult)
                ins.then_inc(s_rs, 1)
                dve.tensor_tensor(ast[:, u].rearrange("p (f h) t -> p f (h t)", f=2), prod[:, :, 1], e2,
                                  ALU.mult).then_inc(s_as, 1)

            query_blocks(0, 0)
            with dve.Fori(0, NT // 2 - 1) as i:
                for u in range(2):
                    query_blocks(2 * i + u + 1, 1 - u)
                    matrices(i, u)
            query_blocks(NT - 1, 1)
            matrices(NT // 2 - 1, 0)
            matrices(NT // 2 - 1, 1)
            dve.wait_ge(s_blk_in, 2 * 16 * 4)
            invert(dve, s_invd, 0, 2, tmp_d)
            dve.wait_ge(s_as, at(NT))
            dve.memset(ps[:, 4:6, :], 0.0).then_inc(s_zero, 1)
            dve.wait_ge(s_xn, 32)
            def finish_solution(i):
                for u in range(2):
                    n = 2 * i + u
                    dve.wait_ge(s_z, at(n + 1))
                    dve.tensor_tensor(wsol[:, u, :], wsol[:, u, :], ps[:, 4 + u, 0:HV], ALU.subtract).then_inc(s_w2, 1)

            def gate_values(i):
                for u in range(2):
                    n = 2 * i + u
                    dve.wait_ge(s_o, at(n + 1))
                    dve.wait_ge(s_sgr, at(n + 1))
                    dve.wait_ge(s_ot, at(n - 1))
                    dve.tensor_tensor(og[:, u, :], ps[:, 6 + u, 0:HV], sgr[:, u, :], ALU.mult).then_inc(s_og, 1)

            def head_squares(i):
                for u in range(2):
                    n = 2 * i + u
                    dve.wait_ge(s_osq, at(n + 1))
                    dve.wait_ge(s_rr, at(n - 1))
                    dve.tensor_reduce(ms[:, u, :], osq[:, u, :].rearrange("p (h t) -> p h t", h=H), AXX,
                                      ALU.add).then_inc(s_ms, 1)

            def head_scales(i):
                for u in range(2):
                    n = 2 * i + u
                    dve.wait_ge(s_rms, at(n + 1))
                    dve.wait_ge(s_og2, at(n - 1))
                    dve.reciprocal(rs[:, u, :], ms[:, u, :]).then_inc(s_rr, 1)

            def add_residual(i):
                for u in range(2):
                    n = 2 * i + u
                    dve.wait_ge(s_xo, at(n + 1))
                    dve.wait_ge(s_x1, at(n - 1))
                    dve.tensor_tensor(xr[:, u, :], ps[:, u, 0:D], xn[:, bass.ds(n * D, D)], ALU.add).then_inc(s_xr, 1)

            def row_moments(i):
                for u in range(2):
                    n = 2 * i + u
                    dve.wait_ge(s_xr, at(n + 1))
                    dve.wait_ge(s_sd, at(n - 1))
                    dve.bn_stats(bn[:, u, :], xr[:, u, :]).then_inc(s_bn, 1)
                    dve.wait_ge(s_bn, at(2 * n + 1))
                    alone(dve)
                    dve.bn_aggr(mv[:, u, :], bn[:, u, :]).then_inc(s_bn, 1)

            def norm_rows(i):
                for u in range(2):
                    n = 2 * i + u
                    dve.wait_ge(s_sd, at(n + 1))
                    dve.reciprocal(rsd[:, u, :], sd[:, u, :]).then_inc(s_rsd, 1)
                    dve.wait_ge(s_rsd, at(n + 1))
                    dve.tensor_scalar(xn[:, bass.ds(n * D, D)], xr[:, u, :], mv[:, u, 0:1], rsd[:, u, :],
                                      ALU.subtract, ALU.mult).then_inc(s_x1, 1)
                    dve.scalar_tensor_tensor(rq_tab[:, bass.ds(n, 1)], mv[:, u, 1:2], rsd[:, u, :], rsd[:, u, :],
                                             ALU.mult, ALU.mult).then_inc(s_rq, 1)

            finish_solution(0)
            gate_values(0)
            head_squares(0)
            head_scales(0)
            with dve.Fori(0, NT // 2 - 1) as i:
                finish_solution(i + 1)
                add_residual(i)
                row_moments(i)
                gate_values(i + 1)
                head_squares(i + 1)
                head_scales(i + 1)
                norm_rows(i)
            add_residual(NT // 2 - 1)
            row_moments(NT // 2 - 1)
            norm_rows(NT // 2 - 1)
            dve.wait_ge(s_rqa, at(1))
            dve.reciprocal(rq_tab, rq_tab).then_inc(s_rqd, 1)
            def shift_scores(i):
                for u in range(2):
                    n = 2 * i + u
                    sc = ps[:, 2 + 2 * u:4 + 2 * u, :].rearrange("p f (h k) -> p (f h) k", h=8)
                    dve.wait_ge(s_sc, at(2 * n + 2))
                    dve.tensor_reduce(mxs[:, u], sc, AXX, ALU.max).then_inc(s_mx, 1)
                    dve.wait_ge(s_mx, at(n + 1))
                    dve.wait_ge(s_pt, at(2 * n - 2))
                    dve.tensor_tensor(prob_u[:, u], sc, over(mxs[:, u], 2, T), ALU.subtract).then_inc(s_sub, 1)

            def normalise(i):
                for u in range(2):
                    n = 2 * i + u
                    dve.wait_ge(s_exp, at(n + 1))
                    dve.tensor_reduce(sms[:, u], prob_u[:, u], AXX, ALU.add).then_inc(s_sum, 1)
                    dve.wait_ge(s_sum, at(2 * n + 1))
                    dve.reciprocal(sri[:, u], sms[:, u]).then_inc(s_sum, 1)
                    dve.wait_ge(s_sum, at(2 * n + 2))
                    dve.tensor_tensor(prob_u[:, u], prob_u[:, u], over(sri[:, u], 2, T), ALU.mult).then_inc(s_pr, 1)

            def add_softmax(i):
                for u in range(2):
                    n = 2 * i + u
                    dve.wait_ge(s_xp, at(n + 1))
                    dve.wait_ge(s_qr, at(3 * n + 3))
                    row = xn[:, bass.ds(n * D, D)]
                    dve.tensor_tensor(row, ps[:, u, D:2 * D], row, ALU.add).then_inc(s_xr2, 1)
                for u in range(2):
                    n = 2 * i + u
                    dve.wait_ge(s_xr2, at(n + 1))
                    alone(dve)
                    dve.bn_stats(bn2[:, u, :], xn[:, bass.ds(n * D, D)]).then_inc(s_bn2, 1)
                for u in range(2):
                    dve.wait_ge(s_bn2, at(4 * i + u + 1))
                    alone(dve)
                    dve.bn_aggr(mv2s[:, u, :], bn2[:, u, :]).then_inc(s_bn2, 1)
                dve.wait_ge(s_bn2, at(4 * i + 4))
                alone(dve)
                dve.tensor_copy(mv2_flat[:, bass.ds(4 * i, 4)], mv2s[:, :, :].rearrange("p u c -> p (u c)")).then_inc(s_mv2, 1)

            shift_scores(0)
            with dve.Fori(0, NT // 2 - 1) as i:
                normalise(i)
                shift_scores(i + 1)
                add_softmax(i)
            normalise(NT // 2 - 1)
            for part, (n0, n1) in enumerate(((0, NT - SPG), (NT - SPG, NT))):
                if part == 1:
                    add_softmax(NT // 2 - 1)
                dve.wait_ge(s_ln2a, at(part + 1))
                dve.reciprocal(sd2[:, n0:n1], sd2[:, n0:n1]).then_inc(s_ln2d, 1)
                dve.wait_ge(s_ln2d, at(part + 1))
                for n in range(n0, n1):
                    row = xn[:, n * D:(n + 1) * D]
                    dve.tensor_scalar(row, row, mv2_flat[:, 2 * n:2 * n + 1], sd2[:, n:n + 1],
                                      ALU.subtract, ALU.mult).then_inc(s_x2, 1)
            steps = [0]

            def routed(ins):
                ins.then_inc(s_rt, 1)
                steps[0] += 1
                dve.wait_ge(s_rt, at(steps[0]))

            iota = over(consts[:, C_IOTA:C_IOTA + E], 1, NT)
            dve.wait_ge(s_el, at(1))
            routed(dve.tensor_scalar(aff, elog, 1.0, None, ALU.add))
            routed(dve.reciprocal(aff, aff))
            left = aff
            for k, sel in enumerate((pick, pick2)):
                routed(dve.tensor_reduce(best[:, k], left, AXX, ALU.max))
                routed(dve.tensor_tensor(lower, left, over(best[:, k], 2, E), ALU.is_lt))
                routed(dve.scalar_tensor_tensor(lower, lower, 64.0, iota, ALU.mult, ALU.add))
                routed(dve.tensor_reduce(best[:, 2], lower, AXX, ALU.min))
                routed(dve.tensor_tensor(sel, iota, over(best[:, 2], 2, E), ALU.is_equal))
                if k == 0:
                    routed(dve.scalar_tensor_tensor(spare, sel, -4.0, left, ALU.mult, ALU.add))
                    left = spare
            dve.tensor_tensor(chosen, pick, pick2, ALU.add).then_inc(s_mask, 1)

            def shared_products(g):
                for e in range(SH):
                    m = SH * g + e
                    dve.wait_ge(s_ge, at(m + 1))
                    if g > 0:
                        dve.wait_ge(s_eot, at(SPG * g))
                    dve.scalar_tensor_tensor(ybf[:, e, :], ps[:, 2 + e, :], colp[:, E + e + W_B1:E + e + W_B1 + 1],
                                             hbuf[:, e, :], ALU.add, ALU.mult).then_inc(s_yy, 1)

            def shared_sums(g):
                dve.wait_ge(s_xst, at(g + 1))
                for t in range(SPG):
                    n = SPG * g + t
                    dve.wait_ge(s_eot, at(n + 1))
                    row = xn[:, n * D:(n + 1) * D]
                    dve.scalar_tensor_tensor(row, row, 2.0, ps[:, 4 + t, 0:D], ALU.mult, ALU.add).then_inc(s_ac, 1)

            shared_products(0)
            dve.wait_ge(s_pre, at(1))
            routed(dve.tensor_copy(slot, ps[:, 6, 0:NT * E].rearrange("p (n e) -> p n e", e=E)))
            routed(dve.tensor_copy(cum, ps[:, 7, 0:NT * E].rearrange("p (n e) -> p n e", e=E)))
            routed(dve.tensor_tensor(slot, slot, cum, ALU.subtract))

            def running_sum(a, b, n):
                d = 1
                while d < n:
                    dve.tensor_copy(b[:, 0:d], a[:, 0:d])
                    routed(dve.tensor_tensor(b[:, d:n], a[:, d:n], a[:, 0:n - d], ALU.add))
                    a, b, d = b, a, 2 * d
                return a

            upto = running_sum(cum, cum2, NT)
            routed(dve.tensor_tensor(slot, slot, upto, ALU.add))
            routed(dve.tensor_tensor(spare, over(upto[:, NT - 1], 2, NT), over(consts[:, C_K128:C_K128 + NT], 1, E), ALU.is_gt))
            routed(dve.tensor_reduce(byexp[:, 0], spare, AXX, ALU.add))
            routed(dve.tensor_copy(byexp[:, 1], byexp[:, 0]))
            last = running_sum(byexp[:, 1], byexp[:, 2], E)
            routed(dve.tensor_tensor(byexp[:, 3], last, byexp[:, 0], ALU.subtract))
            routed(dve.tensor_scalar(byexp[:, 3], byexp[:, 3], float(P), None, ALU.mult))
            routed(dve.tensor_tensor(slot, slot, over(byexp[:, 3], 1, NT), ALU.add))
            for k, sel in enumerate((pick, pick2)):
                routed(dve.tensor_tensor(lower, sel, slot, ALU.mult))
                routed(dve.tensor_reduce(best[:, 3 + k], lower, AXX, ALU.add))
                dve.tensor_copy(slots_i[:].rearrange("p (n k) -> p n k", k=2)[:, :, k], best[:, 3 + k]).then_inc(s_slots, 1)
            routed(dve.tensor_tensor(by_tile, over(last, 1, NSLOT), over(consts[:, C_TILE:C_TILE + NSLOT], 2, E), ALU.is_le))
            routed(dve.tensor_reduce(expert_f, by_tile, AXX, ALU.add))
            routed(dve.tensor_scalar(expert_f, expert_f, float(E - 1), float(D), ALU.min, ALU.mult))
            dve.tensor_copy(expert_i[:], expert_f).then_inc(s_slots, 1)
            routed(dve.tensor_tensor(best[:, 3], best[:, 0], best[:, 1], ALU.add))
            routed(dve.reciprocal(best[:, 4], best[:, 3]))
            for k in range(2):
                routed(dve.tensor_tensor(best[:, 5 + k], best[:, k], best[:, 4], ALU.mult))
            dve.wait_ge(s_x2t, at(NT))
            for g in range(NG):
                shared_sums(g)
                if g + 1 < NG:
                    shared_products(g + 1)

            def products(i):
                for v in range(W4):
                    j = W4 * i + v
                    dve.wait_ge(s_gg, at(j + 1))
                    dve.wait_ge(s_yt, at(j - W4 + 1))
                    dve.tensor_tensor(yhb[:, v, :], ps[:, 2 * v + 1, F:2 * F], geb[:, v, :], ALU.mult).then_inc(s_yh, 1)

            def keep_products(i):
                for v in range(W4):
                    j = W4 * i + v
                    dve.wait_ge(s_yt, at(j + 1))
                    dve.wait_ge(s_yo, at(j - W4 + 1))
                    dve.tensor_copy(yTb[:, v, :], ps[:, 2 * v + 1, 0:P]).then_inc(s_yte, 1)

            with dve.Fori(0, NSLOT // W4) as i:
                products(i)
                keep_products(i)

            def weigh_rows(i, b):
                m = 2 * i + b
                dve.wait_ge(s_got[b], 128 * (i + 1))
                for t in range(4):
                    n = 4 * m + t
                    row = xn[:, bass.ds(n * D, D)]
                    for k in range(2):
                        if k > 0:
                            dve.wait_ge(s_f1, at(2 * n + 1))
                        dve.scalar_tensor_tensor(row, got[:, b, 2 * t + k, :], w_flat[:, bass.ds(n + k * NT, 1)], row,
                                                 ALU.mult, ALU.add).then_inc(s_f1, 1)
                for t in range(4):
                    n = 4 * m + t
                    dve.wait_ge(s_f1, at(2 * n + 2))
                    alone(dve)
                    dve.bn_stats(bn3[:, b, t], xn[:, bass.ds(n * D, D)]).then_inc(s_bn3, 1)
                for t in range(4):
                    dve.wait_ge(s_bn3, at(8 * m + t + 1))
                    dve.wait_ge(s_sd3, at(m - 1))
                    alone(dve)
                    dve.bn_aggr(mv3[:, b, t, :], bn3[:, b, t]).then_inc(s_bn3, 1)

            def norm_last(i, b):
                m = 2 * i + b
                dve.wait_ge(s_sd3, at(m + 1))
                dve.reciprocal(ri3[:, b, :], sd3[:, b, :]).then_inc(s_ri3, 1)
                dve.wait_ge(s_ri3, at(m + 1))
                dve.wait_ge(s_out[b], 16 * i + 16)
                for t in range(4):
                    n = 4 * m + t
                    ins = dve.tensor_scalar(ob[:, b, t * D:(t + 1) * D], xn[:, bass.ds(n * D, D)], mv3[:, b, t, 0:1],
                                            ri3[:, b, t:t + 1], ALU.subtract, ALU.mult)
                ins.then_inc(s_ob, 1)

            with dve.Fori(0, NT // 8) as i:
                weigh_rows(i, 0)
                norm_last(i, 0)
                weigh_rows(i, 1)
                norm_last(i, 1)

        @block.gpsimd
        def _(pool):
            start_counts(pool, "pool")

            def stage_group(g):
                pool.wait_ge(s_gmm, at(SPG * g))
                pool.tensor_copy(xs, xT3[:, :, bass.ds(g * GT, GT)]).then_inc(s_xs, 1)

            def square_channels(g):
                for j in range(4):
                    pool.wait_ge(s_silu, at(NCH * g + j + 1))
                    pool.wait_ge(s_ss, at(g))
                    src = arena[0:KR, bass.ds(g * GT + j * NTOK, GT)]
                    pool.tensor_tensor(sqs[0:KR, j, :], src, src, ALU.mult).then_inc(s_sq, 1)

            pool.wait_ge(s_xt[0], 16)
            stage_group(0)
            for g in range(1, NG):
                pool.wait_ge(s_xt[g], 16)
            stage_group(1)
            square_channels(0)
            pool.wait_ge(s_cst, 64)
            def turned(ins):
                ins.then_inc(s_kp, 1)

            for w0, nh, (cosw, sinw) in ((R_QN, NH, rope_q), (R_KN, NKV, rope_k)):
                w = rowp[:, w0:w0 + nh * HD]
                turned(pool.tensor_tensor(cosw.rearrange("p (h c) -> p h c", h=nh), w.rearrange("p (h c) -> p h c", h=nh),
                                          over(consts[:, C_COS:C_COS + HD], 1, nh), ALU.mult))
                for z in range(2):
                    turned(pool.tensor_tensor(sinw.rearrange(halves, h=nh, z=2)[:, :, z],
                                              w.rearrange(halves, h=nh, z=2)[:, :, 1 - z],
                                              over(consts[:, C_SIN + 8 * z:C_SIN + 8 * z + 8], 1, nh), ALU.mult))
            pool.wait_ge(s_kp, at(6))
            pool.wait_ge(s_kd, at(4))
            turned(pool.tensor_tensor(kt1.rearrange("p (n c) -> p n c", c=CKV), ctx3, over(rope_k[0], 1, NT), ALU.mult))
            for h in range(NKV):
                for z in range(2):
                    a, b = HD * h + 8 * z, HD * h + 8 * (1 - z)
                    turned(pool.tensor_tensor(kt2.rearrange("p (n c) -> p n c", c=CKV)[:, :, a:a + 8], ctx3[:, :, b:b + 8],
                                              over(rope_k[1][:, a:a + 8], 1, NT), ALU.mult))
            pool.wait_ge(s_kp, at(15))
            turned(pool.tensor_tensor(krope[:], kt1, kt2, ALU.add))
            with pool.Fori(0, NG - 2) as i:
                stage_group(i + 2)
                square_channels(i + 1)
            square_channels(NG - 1)
            pool.wait_ge(s_wo, 32)
            pool.tensor_scalar(wo[:], wo[:], colp[:, W_NORM:W_NORM + 1], None, ALU.mult).then_inc(s_pw, 1)
            pool.wait_ge(s_bs, at(1))
            for b in range(2):
                pool.dma_start(slots_dr[(NSLOT + 2 + b) * P:(NSLOT + 3 + b) * P], zero[:]).then_inc(s_scat[b], 16)
            pool.wait_ge(s_gd, at(9))
            pool.wait_ge(s_ss, at(NG))
            with pool.Fori(0, NT // 2) as i:
                for u in range(2):
                    n = 2 * i + u
                    pool.wait_ge(s_dmm, at(n - 1))
                    pool.tensor_tensor(gst[:, u], over(small[:, bass.ds(n * H + T_G * NT * H, H)], 2, T),
                                       over(tmask, 1, H), ALU.mult).then_inc(s_gst, 1)
                    pool.wait_ge(s_kmm, at(n - 1))
                    for f in range(2):
                        ins = pool.tensor_tensor(blk[0:KR, u, f, 0],
                                                 over(arena[0:KR, bass.ds(n * P + (2 + f) * NTOK, P)], 1, HH),
                                                 over(consts[0:KR, C_HM:C_HM + HH], 2, P), ALU.mult)
                    ins.then_inc(s_kblk, 1)
            pool.wait_ge(s_blk_in, 2 * 16 * 4)
            invert(pool, s_invp, 2, 1, tmp_p)
            def scale_values(i):
                for u in range(2):
                    n = 2 * i + u
                    pool.wait_ge(s_w0, at(n - 1))
                    pool.tensor_tensor(vp[:, u], vt[:, bass.ds(n * HV, HV)].rearrange("p (h t) -> p h t", h=H),
                                       over(small[:, bass.ds(n * H + T_NK * NT * H, H)], 2, DV), ALU.mult).then_inc(s_vp, 1)

            def scale_gate(i):
                for u in range(2):
                    n = 2 * i + u
                    pool.wait_ge(s_og, at(n - 1))
                    pool.tensor_tensor(sgr[:, u, :].rearrange("p (h t) -> p h t", h=H),
                                       sg[:, bass.ds(n * HV, HV)].rearrange("p (h t) -> p h t", h=H),
                                       over(small[:, bass.ds(n * H + T_RQ * NT * H, H)], 2, DV), ALU.mult).then_inc(s_sgr, 1)

            def norm_heads(i):
                for u in range(2):
                    n = 2 * i + u
                    pool.wait_ge(s_rr, at(n + 1))
                    o3 = og[:, u, :].rearrange("p (h t) -> p h t", h=H)
                    pool.wait_ge(s_osq, at(n + 1))
                    pool.tensor_tensor(o3, o3, over(rs[:, u, :], 2, DV), ALU.mult).then_inc(s_og2, 1)

            scale_values(0)
            scale_gate(0)
            with pool.Fori(0, NT // 2 - 1) as i:
                scale_values(i + 1)
                norm_heads(i)
                scale_gate(i + 1)
            norm_heads(NT // 2 - 1)
            pool.wait_ge(s_kp, at(16))

            def rotate_queries(i):
                for u in range(2):
                    n = 2 * i + u
                    pool.wait_ge(s_kqt, at(n - 1))
                    pool.wait_ge(s_x1, at(n + 1))
                    row = xn[:, bass.ds(n * D, D)]
                    pool.tensor_tensor(qt1[:, u, :], row, rope_q[0], ALU.mult)
                    for z in range(2):
                        ins = pool.tensor_tensor(qt2[:, u, :].rearrange(halves, h=NH, z=2)[:, :, z],
                                                 row.rearrange(halves, h=NH, z=2)[:, :, 1 - z],
                                                 rope_q[1].rearrange(halves, h=NH, z=2)[:, :, z], ALU.mult)
                        ins.then_inc(s_qr, 1)
                    pool.wait_ge(s_qr, at(3 * n + 2))
                    pool.tensor_tensor(qr[:, u, :], qt1[:, u, :], qt2[:, u, :], ALU.add).then_inc(s_qr, 1)

            def block_keys(i):
                for u in range(2):
                    n = 2 * i + u
                    pool.wait_ge(s_kqe, at(n + 1))
                    pool.wait_ge(s_sc, at(2 * (n - 1)))
                    for f in range(2):
                        ins = pool.tensor_tensor(kblk[:, u, f], over(kqT[:, u, 0, f, :], 1, 8),
                                                 over(consts[:, C_KM:C_KM + 8], 2, P), ALU.mult)
                    ins.then_inc(s_kb, 1)

            rotate_queries(0)
            block_keys(0)
            with pool.Fori(0, NT // 2 - 1) as i:
                rotate_queries(i + 1)
                block_keys(i + 1)
            pool.wait_ge(s_slots, at(2))
            pool.wait_ge(s_zero_in, 8 * (NSLOT + 2))
            with pool.Fori(0, NT // 8) as i:
                for b in range(2):
                    pool.wait_ge(s_scat[b], 128 * i + 16)
                    pool.tensor_copy(idxs[:, 8 * b:8 * b + 8], slots_i[:, bass.ds((2 * i + b) * 8, 8)]).then_inc(s_ix, 1)
                    pool.wait_ge(s_xst, at(2 * i + b + 1))
                    pool.wait_ge(s_ix, at(2 * i + b + 1))
                    alone(pool)
                    for c in range(8):
                        pool.indirect_dma_start(
                            out=slots_dr, out_offset=bass.IndirectOffsetOnAxis(ap=idxs[:, 8 * b + c:8 * b + c + 1], axis=0),
                            in_=xst[:, b, c // 2 * D:(c // 2 + 1) * D], in_offset=None).then_inc(s_scat[b], 16)
            for v in range(W4):
                pool.wait_ge(s_yout[v], 16 * (NSLOT // W4) + 16)
            pool.wait_ge(s_yo, at(NSLOT))
            with pool.Fori(0, NT // 8) as i:
                for b in range(2):
                    m = NT // 4 + 2 * i + b
                    pool.wait_ge(s_f1, at(8 * (2 * i + b - 2) + 8))
                    pool.tensor_copy(idxs[:, 8 * b:8 * b + 8], slots_i[:, bass.ds((2 * i + b) * 8, 8)]).then_inc(s_ix, 1)
                    pool.wait_ge(s_ix, at(m + 1))
                    alone(pool)
                    for c in range(8):
                        pool.indirect_dma_start(
                            out=got[:, b, c, :], out_offset=None, in_=expert_dr,
                            in_offset=bass.IndirectOffsetOnAxis(ap=idxs[:, 8 * b + c:8 * b + c + 1], axis=0)
                        ).then_inc(s_got[b], 16)


def kernel(**inputs):
    import numpy as _np
    import concourse.bacc as _bacc
    from concourse.bass_utils import run_bass_kernel_spmd as _run

    a = {k: _np.asarray(v) for k, v in inputs.items()}
    x = _np.ascontiguousarray(a["x"]).reshape(NTOK, D)
    wq, wk, wv = a["L0_attn_Wq"], a["L0_attn_Wk"], a["L0_attn_Wv"]
    cat = _np.concatenate
    conv = cat([a["L0_attn_conv_q_w"], a["L0_attn_conv_k_w"], a["L0_attn_conv_v_w"]])[:, 0, :]
    col = _np.zeros((P, NCOL), _np.float32)
    for j in range(NCH):
        col[0:ROWS[j], W_TAP + j * KSZ:W_TAP + (j + 1) * KSZ] = conv[CH0[j]:CH0[j] + ROWS[j]]
    col[:, W_NORM] = _np.tile(a["L0_attn_norm_w"], 2)
    col[:, W_GB:W_GB + NE] = cat([a["L0_ffn_rgb"], a["L0_ffn_sgb"]]).T
    col[:, W_B1:W_B1 + NE] = cat([a["L0_ffn_rb1"], a["L0_ffn_sb1"]]).T
    row = cat([a["L0_attn_A_log"], a["L0_attn_dt_bias"], a["L0_xattn_q_norm_w"], a["L0_xattn_k_norm_w"]])
    g = cat([a["L0_ffn_rg"], a["L0_ffn_sg"]])
    w1 = cat([a["L0_ffn_rw1"], a["L0_ffn_sw1"]])
    w2 = cat([a["L0_ffn_rw2"], a["L0_ffn_sw2"]])
    lay = lambda w: w.reshape(-1, KD, P, F).transpose(0, 2, 1, 3).reshape(-1, P, KD * F)
    pair = lambda u, w: cat([u.reshape(-1, KD, P, F), w.reshape(-1, KD, P, F)], axis=3).transpose(0, 2, 1, 3).reshape(-1, P, 2 * KD * F)
    arrays = {
        "xt": x.T, "x": x, "ctx": a["ctx_512"].reshape(NTOK, CKV), "consts": constants(),
        "row": row.reshape(NROW), "col": col,
        "wc": cat([wq, wk, wv]).T, "wg": cat([a["L0_attn_Wg"], a["L0_attn_Wa"], a["L0_attn_Wb"]]).T,
        "wo": a["L0_attn_Wo"].T, "wout": a["L0_xattn_w_out"].T, "wa": a["L0_ffn_wa"],
        "wexp": cat([cat([pair(g[0:E], w1[0:E]), w2[0:E]], axis=2), cat([lay(g[E:NE]), lay(w1[E:NE]), w2[E:NE]], axis=2)]),
        "bias": cat([cat([a["L0_ffn_rgb"], a["L0_ffn_rb1"]], axis=1).reshape(-1), a["L0_ffn_rb2"].reshape(-1),
                     a["L0_ffn_sb2"].reshape(-1)]).reshape(P, (E * 2 * F + NE * D) // P),
    }
    nc = _bacc.Bacc("TRN2", target_bir_lowering=False, num_devices=1)
    args = []
    for name in arrays:
        arrays[name] = _np.ascontiguousarray(arrays[name], dtype=_np.float32)
        args.append(nc.dram_tensor(name + "_dram", arrays[name].shape, F32, kind="ExternalInput").ap())
    out = nc.dram_tensor("out_dram", (NTOK, D), F32, kind="ExternalOutput").ap()
    build(nc, *args, out)
    r = _run(nc, [{k + "_dram": v for k, v in arrays.items()}], core_ids=[0])
    return r.results[0]["out_dram"].reshape(B, T, D)
```
